# Optimizing a Trainium2 kernel written in Bass

```python
import numpy as np
import jax
import jax.numpy as jnp

def _softmax(x, axis=-1):
    return jax.nn.softmax(x, axis=axis)

def _gelu(x):
    return jax.nn.gelu(x, approximate=True)

def _silu(x):
    return jax.nn.silu(x)

def _sigmoid(x):
    return jax.nn.sigmoid(x)

def _layernorm(x, axis=-1, eps=1e-05):
    m = jnp.mean(x, axis=axis, keepdims=True)
    v = jnp.var(x, axis=axis, keepdims=True)
    return (x - m) / jnp.sqrt(v + eps)

def _scatter_add(tgt, idx, src, axis=0):
    return tgt.at[idx].add(src)

def _segment_sum(src, seg, n):
    return jax.ops.segment_sum(src, seg, n)
kernel_name = 'mk_decoder_preln_d2_seqx_r4_52ee72'

def setup_inputs(seed: int=0):
    np.random.seed(seed)
    _w = jnp.asarray

    def _rec_inputs():
        import jax
        import jax.numpy as jnp
        _rk = jax.random.key(seed)
        x = -0.0003929 + 0.9999 * jax.random.normal(jax.random.fold_in(_rk, 1), (2, 512, 512), jnp.float32)
        _lenS = 512 - jax.random.randint(jax.random.fold_in(_rk, 7), (2,), 0, max(1, 512 // 4) + 1, jnp.int32)
        _lenS2 = 1024 - jax.random.randint(jax.random.fold_in(_rk, 8), (2,), 0, max(1, 1024 // 4) + 1, jnp.int32)
        _ctx_2048P = jax.random.normal(jax.random.fold_in(_rk, 11), (2, 16, 512), jnp.float32)
        _ctx_2048c = jax.random.dirichlet(jax.random.fold_in(_rk, 511), 0.3 * jnp.ones((16,), jnp.float32), (2, 1024))
        _ctx_2048t = jnp.einsum('bsk,bkd->bsd', _ctx_2048c, _ctx_2048P)
        _ctx_2048t = _ctx_2048t * jax.lax.rsqrt(jnp.mean(jnp.square(_ctx_2048t)) + 1e-12) * 0.953939
        ctx_2048 = -0.000514642 + 1.00011 * (_ctx_2048t + 0.3 * jax.random.normal(jax.random.fold_in(_rk, 611), (2, 1024, 512), jnp.float32))
        return (x, ctx_2048)
    x, ctx_2048 = _rec_inputs()

    def _L0_attn_setup():
        import math
        import jax, jax.numpy as jnp
        import numpy as np
        D_MODEL = 512
        NUM_HEADS = 16
        D_HEAD = D_MODEL // NUM_HEADS
        THETA = 10000.0

        def _rope_tables(seq_len, d_head):
            idx = jnp.arange(0, d_head, 2, dtype=jnp.float32)
            inv_freq = THETA ** (-idx / d_head)
            angles = jnp.arange(seq_len, dtype=jnp.float32)[:, None] * inv_freq[None, :]
            return (jnp.cos(angles), jnp.sin(angles))

        def _apply_rope(x, cos, sin):
            B, H, S, d = x.shape
            xp = x.reshape(B, H, S, d // 2, 2)
            xe, xo = (xp[..., 0], xp[..., 1])
            rot = jnp.stack([xe * cos - xo * sin, xe * sin + xo * cos], axis=-1)
            return rot.reshape(B, H, S, d)
        key = jax.random.key(seed)
        k_x, k_q, k_k, k_v, k_o = jax.random.split(key, 5)
        std = math.sqrt(2.0 / (D_MODEL + D_MODEL))
        x = jax.random.normal(k_x, (4, 512, D_MODEL), dtype=jnp.float32)
        Wq = jax.random.normal(k_q, (D_MODEL, D_MODEL), dtype=jnp.float32) * std
        Wk = jax.random.normal(k_k, (D_MODEL, D_MODEL), dtype=jnp.float32) * std
        Wv = jax.random.normal(k_v, (D_MODEL, D_MODEL), dtype=jnp.float32) * std
        Wo = jax.random.normal(k_o, (D_MODEL, D_MODEL), dtype=jnp.float32) * std
        return {'x': x, 'Wq': Wq, 'Wk': Wk, 'Wv': Wv, 'Wo': Wo}
    _L0_attn_all = _L0_attn_setup()
    _L0_attn_in = {k: v for k, v in _L0_attn_all.items() if k in ('Wq', 'Wk', 'Wv', 'Wo')}
    del _L0_attn_all

    def _L0_xattn_setup():
        import jax, jax.numpy as jnp
        import numpy as np
        NUM_HEADS = 16

        def _qdq(x):
            s = jnp.maximum(jnp.max(jnp.abs(x), axis=-1, keepdims=True) / 127.0, 1e-08)
            return jnp.clip(jnp.round(x / s), -127.0, 127.0) * s
        key = jax.random.key(seed)
        ks = jax.random.split(key, 8)
        B, N, M, D = (2, 1024, 128, 512)
        w_std = 0.02
        return {'x': jax.random.normal(ks[0], (B, N, D), jnp.float32), 'cond': jax.random.normal(ks[1], (B, M, D), jnp.float32), 'wq': jax.random.normal(ks[2], (D, D), jnp.float32) * w_std, 'bq': jax.random.normal(ks[3], (D,), jnp.float32) * w_std, 'wkv': jax.random.normal(ks[4], (2 * D, D), jnp.float32) * w_std, 'bkv': jax.random.normal(ks[5], (2 * D,), jnp.float32) * w_std, 'wp': jax.random.normal(ks[6], (D, D), jnp.float32) * w_std, 'bp': jax.random.normal(ks[7], (D,), jnp.float32) * w_std}
    _L0_xattn_all = _L0_xattn_setup()
    _L0_xattn_in = {k: v for k, v in _L0_xattn_all.items() if k in ('wq', 'bq', 'wkv', 'bkv', 'wp', 'bp')}
    del _L0_xattn_all

    def _L0_ffn_setup():
        import jax, jax.numpy as jnp
        import numpy as np
        from functools import partial
        SEQ, BATCH, HIDDEN = (512, 4, 512)
        FFN = 352
        N_EXPERTS = 8
        TOP_K = 2
        EPS = 1e-20
        key = jax.random.key(seed)
        k0, k1, k2, k3 = jax.random.split(key, 4)
        x = jax.random.normal(k0, (SEQ, BATCH, HIDDEN), dtype=jnp.float32)
        wg = jax.random.normal(k1, (N_EXPERTS, HIDDEN), dtype=jnp.float32) * 0.02
        w1 = jax.random.normal(k2, (N_EXPERTS, HIDDEN, 2 * FFN), dtype=jnp.float32) * 0.02
        w2 = jax.random.normal(k3, (N_EXPERTS, FFN, HIDDEN), dtype=jnp.float32) * 0.02
        return {'x': x, 'wg': wg, 'w1': w1, 'w2': w2}
    _L0_ffn_all = _L0_ffn_setup()
    _L0_ffn_in = {k: v for k, v in _L0_ffn_all.items() if k in ('wg', 'w1', 'w2')}
    del _L0_ffn_all

    def _L1_attn_setup():
        import jax, jax.numpy as jnp
        import numpy as np
        import math
        D_MODEL = 512
        NUM_HEAD = 16
        HEAD_DIM = D_MODEL // NUM_HEAD

        def _trunc_normal(key, shape, std):
            return jax.random.truncated_normal(key, -3.0, 3.0, shape, dtype=jnp.float32) * std
        key = jax.random.key(seed)
        kx, kp, ko = jax.random.split(key, 3)
        b, s = (4, 512)
        x = jax.random.normal(kx, (b, s, D_MODEL), dtype=jnp.float32)
        sigma_p = math.sqrt(2.0 / (D_MODEL + 3 * D_MODEL))
        w_project = _trunc_normal(kp, (3 * D_MODEL, D_MODEL), sigma_p)
        sigma_o = math.sqrt(2.0 / (D_MODEL + D_MODEL))
        w_out = _trunc_normal(ko, (D_MODEL, D_MODEL), sigma_o)
        return {'x': x, 'w_project': w_project, 'w_out': w_out}
    _L1_attn_all = _L1_attn_setup()
    _L1_attn_in = {k: v for k, v in _L1_attn_all.items() if k in ('w_project', 'w_out')}
    del _L1_attn_all

    def _L1_xattn_setup():
        import jax, jax.numpy as jnp
        import numpy as np
        DIM = 512
        H = 16
        D = 128
        INNER = H * D
        N_IMG = 257
        EPS = 1e-06

        def rms_norm(x, scale, eps=EPS):
            ms = jnp.mean(jnp.square(x), axis=-1, keepdims=True)
            return x * jax.lax.rsqrt(ms + eps) * scale

        def sdpa(q, k, v):
            scale = 1.0 / jnp.sqrt(jnp.asarray(D, q.dtype))
            scores = jnp.einsum('bshd,blhd->bhsl', q, k) * scale
            attn = jax.nn.softmax(scores, axis=-1)
            return jnp.einsum('bhsl,blhd->bshd', attn, v)
        key = jax.random.key(seed)
        ks = jax.random.split(key, 16)
        std = 1.0 / np.sqrt(DIM)
        inp = {'x': jax.random.normal(ks[0], (2, 1024, DIM), jnp.float32), 'context': jax.random.normal(ks[1], (2, 769, DIM), jnp.float32), 'q_w': jax.random.normal(ks[2], (DIM, INNER), jnp.float32) * std, 'q_b': jnp.zeros((INNER,), jnp.float32), 'k_w': jax.random.normal(ks[3], (DIM, INNER), jnp.float32) * std, 'k_b': jnp.zeros((INNER,), jnp.float32), 'v_w': jax.random.normal(ks[4], (DIM, INNER), jnp.float32) * std, 'v_b': jnp.zeros((INNER,), jnp.float32), 'ki_w': jax.random.normal(ks[5], (DIM, INNER), jnp.float32) * std, 'ki_b': jnp.zeros((INNER,), jnp.float32), 'vi_w': jax.random.normal(ks[6], (DIM, INNER), jnp.float32) * std, 'vi_b': jnp.zeros((INNER,), jnp.float32), 'o_w': jax.random.normal(ks[7], (INNER, DIM), jnp.float32) * std, 'o_b': jnp.zeros((DIM,), jnp.float32), 'nq_s': jnp.ones((INNER,), jnp.float32), 'nkt_s': jnp.ones((INNER,), jnp.float32), 'nki_s': jnp.ones((INNER,), jnp.float32)}
        return inp
    _L1_xattn_all = _L1_xattn_setup()
    _L1_xattn_in = {k: v for k, v in _L1_xattn_all.items() if k in ('q_w', 'q_b', 'k_w', 'k_b', 'v_w', 'v_b', 'ki_w', 'ki_b', 'vi_w', 'vi_b', 'o_w', 'o_b', 'nq_s', 'nkt_s', 'nki_s')}
    del _L1_xattn_all

    def _L1_ffn_setup():
        import jax, jax.numpy as jnp
        import numpy as np
        D_MODEL = 512
        D_HIDDEN = 352
        NUM_SHARED = 2
        NUM_ROUTED = 32
        TOP_K = 6

        def _expert_apply(xf, w1, b1, w2, b2):
            return jnp.maximum(xf @ w1 + b1, 0.0) @ w2 + b2
        key = jax.random.key(seed)
        ks = jax.random.split(key, 11)
        d, h = (D_MODEL, D_HIDDEN)
        s1 = 1.0 / np.sqrt(d)
        s2 = 1.0 / np.sqrt(h)
        x = jax.random.normal(ks[0], (2, 512, d), dtype=jnp.float32)
        sw1 = jax.random.uniform(ks[1], (NUM_SHARED, d, h), jnp.float32, -s1, s1)
        sb1 = jax.random.uniform(ks[2], (NUM_SHARED, h), jnp.float32, -s1, s1)
        sw2 = jax.random.uniform(ks[3], (NUM_SHARED, h, d), jnp.float32, -s2, s2)
        sb2 = jax.random.uniform(ks[4], (NUM_SHARED, d), jnp.float32, -s2, s2)
        rw1 = jax.random.uniform(ks[5], (NUM_ROUTED, d, h), jnp.float32, -s1, s1)
        rb1 = jax.random.uniform(ks[6], (NUM_ROUTED, h), jnp.float32, -s1, s1)
        rw2 = jax.random.uniform(ks[7], (NUM_ROUTED, h, d), jnp.float32, -s2, s2)
        rb2 = jax.random.uniform(ks[8], (NUM_ROUTED, d), jnp.float32, -s2, s2)
        router_w = jax.random.uniform(ks[9], (d, NUM_ROUTED), jnp.float32, -s1, s1)
        router_b = jax.random.uniform(ks[10], (NUM_ROUTED,), jnp.float32, -s1, s1)
        return {'x': x, 'sw1': sw1, 'sb1': sb1, 'sw2': sw2, 'sb2': sb2, 'rw1': rw1, 'rb1': rb1, 'rw2': rw2, 'rb2': rb2, 'router_w': router_w, 'router_b': router_b}
    _L1_ffn_all = _L1_ffn_setup()
    _L1_ffn_in = {k: v for k, v in _L1_ffn_all.items() if k in ('sw1', 'sb1', 'sw2', 'sb2', 'rw1', 'rb1', 'rw2', 'rb2', 'router_w', 'router_b')}
    del _L1_ffn_all
    return {'x': x, 'ctx_2048': ctx_2048, 'L0_attn_Wq': _L0_attn_in['Wq'], 'L0_attn_Wk': _L0_attn_in['Wk'], 'L0_attn_Wv': _L0_attn_in['Wv'], 'L0_attn_Wo': _L0_attn_in['Wo'], 'L0_xattn_wq': _L0_xattn_in['wq'], 'L0_xattn_bq': _L0_xattn_in['bq'], 'L0_xattn_wkv': _L0_xattn_in['wkv'], 'L0_xattn_bkv': _L0_xattn_in['bkv'], 'L0_xattn_wp': _L0_xattn_in['wp'], 'L0_xattn_bp': _L0_xattn_in['bp'], 'L0_ffn_wg': _L0_ffn_in['wg'], 'L0_ffn_w1': _L0_ffn_in['w1'], 'L0_ffn_w2': _L0_ffn_in['w2'], 'L1_attn_w_project': _L1_attn_in['w_project'], 'L1_attn_w_out': _L1_attn_in['w_out'], 'L1_xattn_q_w': _L1_xattn_in['q_w'], 'L1_xattn_q_b': _L1_xattn_in['q_b'], 'L1_xattn_k_w': _L1_xattn_in['k_w'], 'L1_xattn_k_b': _L1_xattn_in['k_b'], 'L1_xattn_v_w': _L1_xattn_in['v_w'], 'L1_xattn_v_b': _L1_xattn_in['v_b'], 'L1_xattn_ki_w': _L1_xattn_in['ki_w'], 'L1_xattn_ki_b': _L1_xattn_in['ki_b'], 'L1_xattn_vi_w': _L1_xattn_in['vi_w'], 'L1_xattn_vi_b': _L1_xattn_in['vi_b'], 'L1_xattn_o_w': _L1_xattn_in['o_w'], 'L1_xattn_o_b': _L1_xattn_in['o_b'], 'L1_xattn_nq_s': _L1_xattn_in['nq_s'], 'L1_xattn_nkt_s': _L1_xattn_in['nkt_s'], 'L1_xattn_nki_s': _L1_xattn_in['nki_s'], 'L1_ffn_sw1': _L1_ffn_in['sw1'], 'L1_ffn_sb1': _L1_ffn_in['sb1'], 'L1_ffn_sw2': _L1_ffn_in['sw2'], 'L1_ffn_sb2': _L1_ffn_in['sb2'], 'L1_ffn_rw1': _L1_ffn_in['rw1'], 'L1_ffn_rb1': _L1_ffn_in['rb1'], 'L1_ffn_rw2': _L1_ffn_in['rw2'], 'L1_ffn_rb2': _L1_ffn_in['rb2'], 'L1_ffn_router_w': _L1_ffn_in['router_w'], 'L1_ffn_router_b': _L1_ffn_in['router_b']}

def reference(x, ctx_2048, L0_attn_Wq, L0_attn_Wk, L0_attn_Wv, L0_attn_Wo, L0_xattn_wq, L0_xattn_bq, L0_xattn_wkv, L0_xattn_bkv, L0_xattn_wp, L0_xattn_bp, L0_ffn_wg, L0_ffn_w1, L0_ffn_w2, L1_attn_w_project, L1_attn_w_out, L1_xattn_q_w, L1_xattn_q_b, L1_xattn_k_w, L1_xattn_k_b, L1_xattn_v_w, L1_xattn_v_b, L1_xattn_ki_w, L1_xattn_ki_b, L1_xattn_vi_w, L1_xattn_vi_b, L1_xattn_o_w, L1_xattn_o_b, L1_xattn_nq_s, L1_xattn_nkt_s, L1_xattn_nki_s, L1_ffn_sw1, L1_ffn_sb1, L1_ffn_sw2, L1_ffn_sb2, L1_ffn_rw1, L1_ffn_rb1, L1_ffn_rw2, L1_ffn_rb2, L1_ffn_router_w, L1_ffn_router_b):
    import jax
    import jax.numpy as jnp

    def _L0_attn_ref(x, Wq, Wk, Wv, Wo):
        import math
        import jax, jax.numpy as jnp
        import numpy as np
        D_MODEL = 512
        NUM_HEADS = 16
        D_HEAD = D_MODEL // NUM_HEADS
        THETA = 10000.0

        def _rope_tables(seq_len, d_head):
            idx = jnp.arange(0, d_head, 2, dtype=jnp.float32)
            inv_freq = THETA ** (-idx / d_head)
            angles = jnp.arange(seq_len, dtype=jnp.float32)[:, None] * inv_freq[None, :]
            return (jnp.cos(angles), jnp.sin(angles))

        def _apply_rope(x, cos, sin):
            B, H, S, d = x.shape
            xp = x.reshape(B, H, S, d // 2, 2)
            xe, xo = (xp[..., 0], xp[..., 1])
            rot = jnp.stack([xe * cos - xo * sin, xe * sin + xo * cos], axis=-1)
            return rot.reshape(B, H, S, d)
        B, S, D = x.shape
        H, dh = (NUM_HEADS, D_HEAD)

        def proj(W):
            y = jnp.einsum('bsi,oi->bso', x, W)
            return y.reshape(B, S, H, dh).transpose(0, 2, 1, 3)
        q, k, v = (proj(Wq), proj(Wk), proj(Wv))
        cos, sin = _rope_tables(S, dh)
        q = _apply_rope(q, cos, sin)
        k = _apply_rope(k, cos, sin)
        scores = jnp.einsum('bhqd,bhkd->bhqk', q.astype(jnp.float32), k.astype(jnp.float32)) / math.sqrt(dh)
        causal = jnp.tril(jnp.ones((S, S), dtype=bool))
        scores = jnp.where(causal, scores, jnp.finfo(jnp.float32).min)
        probs = jax.nn.softmax(scores, axis=-1).astype(v.dtype)
        attn = jnp.einsum('bhqk,bhkd->bhqd', probs, v)
        attn = attn.transpose(0, 2, 1, 3).reshape(B, S, D)
        return jnp.einsum('bsi,oi->bso', attn, Wo)

    def _L0_xattn_ref(x, cond, wq, bq, wkv, bkv, wp, bp):
        import jax, jax.numpy as jnp
        import numpy as np
        NUM_HEADS = 16

        def _qdq(x):
            s = jnp.maximum(jnp.max(jnp.abs(x), axis=-1, keepdims=True) / 127.0, 1e-08)
            return jnp.clip(jnp.round(x / s), -127.0, 127.0) * s
        B, N, C = x.shape
        M = cond.shape[1]
        H = NUM_HEADS
        Dh = C // H
        q = _qdq(x) @ _qdq(wq).T + bq
        kv = cond @ wkv.T + bkv
        k, v = jnp.split(kv, 2, axis=-1)
        q = q.reshape(B, N, H, Dh)
        k = k.reshape(B, M, H, Dh)
        v = v.reshape(B, M, H, Dh)
        scale = 1.0 / np.sqrt(Dh)
        attn = jax.nn.softmax(jnp.einsum('bnhd,bmhd->bhnm', q, k) * scale, axis=-1)
        o = jnp.einsum('bhnm,bmhd->bnhd', attn, v).reshape(B, N, C)
        out = _qdq(o) @ _qdq(wp).T + bp
        return out

    def _L0_ffn_ref(x, wg, w1, w2):
        import jax, jax.numpy as jnp
        import numpy as np
        from functools import partial
        SEQ, BATCH, HIDDEN = (512, 4, 512)
        FFN = 352
        N_EXPERTS = 8
        TOP_K = 2
        EPS = 1e-20
        S, B, H = x.shape
        T = B * S
        xt = jnp.transpose(x, (1, 0, 2)).reshape(T, H)
        logits = xt @ wg.T
        scores = jax.nn.softmax(logits, axis=-1)
        topk_w, topk_i = jax.lax.top_k(scores, TOP_K)
        topk_w = topk_w / (jnp.sum(topk_w, axis=-1, keepdims=True) + EPS)
        C = jnp.zeros((T, N_EXPERTS), dtype=xt.dtype)
        C = C.at[jnp.arange(T)[:, None], topk_i].add(topk_w)

        def step(acc, inputs):
            w1e, w2e, ce = inputs
            h = xt @ w1e
            a, b = jnp.split(h, 2, axis=-1)
            y = jax.nn.silu(a) * b @ w2e
            return (acc + ce[:, None] * y, None)
        out0 = jnp.zeros((T, H), dtype=xt.dtype)
        out, _ = jax.lax.scan(step, out0, (w1, w2, C.T))
        return jnp.transpose(out.reshape(B, S, H), (1, 0, 2))

    def _L1_attn_ref(x, w_project, w_out):
        import jax, jax.numpy as jnp
        import numpy as np
        import math
        D_MODEL = 512
        NUM_HEAD = 16
        HEAD_DIM = D_MODEL // NUM_HEAD

        def _trunc_normal(key, shape, std):
            return jax.random.truncated_normal(key, -3.0, 3.0, shape, dtype=jnp.float32) * std
        b, s, d = x.shape
        qkv = jnp.einsum('bsd,od->bso', x, w_project)
        qkv = qkv.reshape(b, s, 3, NUM_HEAD, HEAD_DIM)
        qkv = jnp.transpose(qkv, (2, 0, 3, 1, 4))
        q, k, v = (qkv[0], qkv[1], qkv[2])
        att = jnp.einsum('bhqd,bhkd->bhqk', q, k) / math.sqrt(HEAD_DIM)
        causal = jnp.triu(jnp.ones((s, s), dtype=bool), k=1)
        att = jnp.where(causal[None, None, :, :], jnp.float32(-1000000000.0), att)
        att = jax.nn.softmax(att, axis=-1)
        out = jnp.einsum('bhqk,bhkd->bhqd', att, v)
        out = jnp.transpose(out, (0, 2, 1, 3)).reshape(b, s, d)
        return jnp.einsum('bsd,od->bso', out, w_out)

    def _L1_xattn_ref(x, context, q_w, q_b, k_w, k_b, v_w, v_b, ki_w, ki_b, vi_w, vi_b, o_w, o_b, nq_s, nkt_s, nki_s):
        import jax, jax.numpy as jnp
        import numpy as np
        DIM = 512
        H = 16
        D = 128
        INNER = H * D
        N_IMG = 257
        EPS = 1e-06

        def rms_norm(x, scale, eps=EPS):
            ms = jnp.mean(jnp.square(x), axis=-1, keepdims=True)
            return x * jax.lax.rsqrt(ms + eps) * scale

        def sdpa(q, k, v):
            scale = 1.0 / jnp.sqrt(jnp.asarray(D, q.dtype))
            scores = jnp.einsum('bshd,blhd->bhsl', q, k) * scale
            attn = jax.nn.softmax(scores, axis=-1)
            return jnp.einsum('bhsl,blhd->bshd', attn, v)
        B, S, _ = x.shape
        img_ctx = context[:, :N_IMG]
        txt_ctx = context[:, N_IMG:]
        q = rms_norm(x @ q_w + q_b, nq_s).reshape(B, S, H, D)
        k_txt = rms_norm(txt_ctx @ k_w + k_b, nkt_s).reshape(B, -1, H, D)
        v_txt = (txt_ctx @ v_w + v_b).reshape(B, -1, H, D)
        out_txt = sdpa(q, k_txt, v_txt)
        k_img = rms_norm(img_ctx @ ki_w + ki_b, nki_s).reshape(B, -1, H, D)
        v_img = (img_ctx @ vi_w + vi_b).reshape(B, -1, H, D)
        out_img = sdpa(q, k_img, v_img)
        out = (out_txt + out_img).reshape(B, S, INNER)
        return out @ o_w + o_b

    def _L1_ffn_ref(x, sw1, sb1, sw2, sb2, rw1, rb1, rw2, rb2, router_w, router_b):
        import jax, jax.numpy as jnp
        import numpy as np
        D_MODEL = 512
        D_HIDDEN = 352
        NUM_SHARED = 2
        NUM_ROUTED = 32
        TOP_K = 6

        def _expert_apply(xf, w1, b1, w2, b2):
            return jnp.maximum(xf @ w1 + b1, 0.0) @ w2 + b2
        B, S, d = x.shape
        flat = x.reshape(-1, d)
        T = flat.shape[0]

        def sh_body(acc, p):
            w1, b1, w2, b2 = p
            return (acc + _expert_apply(flat, w1, b1, w2, b2), None)
        shared_out, _ = jax.lax.scan(sh_body, jnp.zeros_like(flat), (sw1, sb1, sw2, sb2))
        shared_out = shared_out / NUM_SHARED
        logits = flat @ router_w + router_b
        probs = jax.nn.softmax(logits, axis=-1)
        topk_p, topk_i = jax.lax.top_k(probs, TOP_K)
        topk_p = topk_p / jnp.sum(topk_p, axis=-1, keepdims=True)
        gates = jnp.zeros((T, NUM_ROUTED), dtype=flat.dtype)
        gates = gates.at[jnp.arange(T)[:, None], topk_i].add(topk_p)

        def r_body(acc, p):
            w1, b1, w2, b2, g = p
            return (acc + g[:, None] * _expert_apply(flat, w1, b1, w2, b2), None)
        routed_out, _ = jax.lax.scan(r_body, jnp.zeros_like(flat), (rw1, rb1, rw2, rb2, gates.T))
        return (shared_out + routed_out).reshape(B, S, d)
    x = x + _L0_attn_ref(_layernorm(x, axis=-1), L0_attn_Wq, L0_attn_Wk, L0_attn_Wv, L0_attn_Wo)
    x = x + _L0_xattn_ref(_layernorm(x, axis=-1), ctx_2048, L0_xattn_wq, L0_xattn_bq, L0_xattn_wkv, L0_xattn_bkv, L0_xattn_wp, L0_xattn_bp)
    x = x + _L0_ffn_ref(_layernorm(x, axis=-1), L0_ffn_wg, L0_ffn_w1, L0_ffn_w2)
    x = x + _L1_attn_ref(_layernorm(x, axis=-1), L1_attn_w_project, L1_attn_w_out)
    x = x + _L1_xattn_ref(_layernorm(x, axis=-1), ctx_2048, L1_xattn_q_w, L1_xattn_q_b, L1_xattn_k_w, L1_xattn_k_b, L1_xattn_v_w, L1_xattn_v_b, L1_xattn_ki_w, L1_xattn_ki_b, L1_xattn_vi_w, L1_xattn_vi_b, L1_xattn_o_w, L1_xattn_o_b, L1_xattn_nq_s, L1_xattn_nkt_s, L1_xattn_nki_s)
    x = x + _L1_ffn_ref(_layernorm(x, axis=-1), L1_ffn_sw1, L1_ffn_sb1, L1_ffn_sw2, L1_ffn_sb2, L1_ffn_rw1, L1_ffn_rb1, L1_ffn_rw2, L1_ffn_rb2, L1_ffn_router_w, L1_ffn_router_b)
    return x

_drawn_inputs = setup_inputs


def setup_inputs(seed=0):
    import zlib

    import numpy as np

    out = dict(_drawn_inputs(seed))
    spreads = {'L1_xattn_q_b': (0.0, 0.339),
     'L1_xattn_k_b': (0.0, 0.8),
     'L1_xattn_v_b': (0.0, 0.1),
     'L1_xattn_ki_b': (0.0, 0.8),
     'L1_xattn_vi_b': (0.0, 0.1),
     'L1_xattn_o_b': (0.0, 0.1),
     'L1_xattn_nq_s': (1.0, 0.2),
     'L1_xattn_nkt_s': (1.0, 0.2),
     'L1_xattn_nki_s': (1.0, 0.2)}
    factors = {'L0_xattn_wq': 8.0,
     'L0_xattn_bq': 21.606,
     'L0_xattn_bkv': 7.139,
     'L0_xattn_bp': 3.707,
     'L0_ffn_wg': 3.454,
     'L0_ffn_w1': 2.956,
     'L0_ffn_w2': 2.978,
     'L1_ffn_sb1': 8.0,
     'L1_ffn_sb2': 5.102,
     'L1_ffn_rb1': 27.865,
     'L1_ffn_rb2': 8.0,
     'L1_ffn_router_b': 6.315}
    for name, (base, spread) in spreads.items():
        noise = np.random.default_rng([zlib.crc32(name.encode()), seed]).standard_normal(out[name].shape)
        drawn = base * np.exp(spread * noise) if base else spread * noise
        out[name] = jnp.asarray(drawn.astype(out[name].dtype))
    for name, factor in factors.items():
        out[name] = (out[name] * factor).astype(out[name].dtype)
    return out
```

```python
from contextlib import ExitStack

import numpy as np

import concourse.bass as bass
from concourse import mybir

P = 128
B, S, D = 2, 512, 512
T = B * S
NT = T // P
KC = D // P
H = 16
DH = D // H
HPC = P // DH
CTX = 1024
NE0, NE1, NSH = 8, 32, 2
TOP0, TOP1 = 2, 6
F = 352
FCH = [(0, 128), (128, 128), (256, 96)]
DX = 128
INNER = H * DX
NIMG = 257
LN_EPS = 1e-5
RMS_EPS = 1e-6
TOPK_EPS = 1e-20
MASKED = -1.0e30
ROUND = 12582912.0

ALU = mybir.AluOpType
ACT = mybir.ActivationFunctionType
F32 = mybir.dt.float32
BF16 = mybir.dt.bfloat16
U32 = mybir.dt.uint32
X_AXIS = mybir.AxisListType.X


class Stage:

    def __init__(self, nc, name):
        self.nc, self.name, self.stack, self.sems = nc, name, ExitStack(), []

    def sbuf(self, name, shape, dt=F32):
        return self.stack.enter_context(self.nc.sbuf_tensor(f"{self.name}_{name}", shape, dt))

    def sem(self, name):
        s = self.nc.alloc_semaphore(f"{self.name}_{name}")
        self.sems.append(s)
        return s

    def __enter__(self):
        return self

    def __exit__(self, *exc):
        if exc[0] is None:
            self.nc.clear_and_free_semaphores(self.sems)
            self.nc.all_engine_barrier()
        return self.stack.__exit__(*exc)


class Shared:
    pass


def load_constants(nc, g, x, ident, ones):
    with Stage(nc, "init") as st:
        loaded = st.sem("loaded")
        cast = st.sem("cast")
        with nc.Block() as block:
            @block.sync
            def _(sp):
                sp.dma_start(g.x[:, :, :], x.rearrange("(t p) d -> p t d", p=P)).then_inc(loaded, 16)
                sp.dma_start(g.ident[:, :], ident).then_inc(loaded, 16)
                sp.dma_start(g.ones[:, :], ones).then_inc(loaded, 16)

            @block.vector
            def _(dve):
                dve.wait_ge(loaded, 48)
                nc.vector.tensor_copy(g.ident16[:, :], g.ident[:, :]).then_inc(cast, 1)
                nc.vector.memset(g.ln_eps[:, :], LN_EPS).then_inc(cast, 1)
                nc.vector.memset(g.rms_eps[:, :], RMS_EPS).then_inc(cast, 1)
                dve.wait_ge(cast, 3)


def layer_norm(nc, g, name, turn=True):
    with Stage(nc, name) as st:
        stats = st.sbuf("stats", [P, NT, 6])
        mv = st.sbuf("mv", [P, NT, 2])
        std = st.sbuf("std", [P, NT])
        rstd = st.sbuf("rstd", [P, NT])
        xn = st.sbuf("xn", [P, NT, D]) if turn else g.xt[:, :, :].rearrange("p k (a d) -> p (k a) d", d=D)
        stats_done, mean_done, std_done = st.sem("stats_done"), st.sem("mean_done"), st.sem("std_done")
        rstd_done, normed, turned, copied = st.sem("rstd_done"), st.sem("normed"), st.sem("turned"), st.sem("copied")
        with nc.Block() as block:
            @block.vector
            def _(dve):
                for t in range(NT):
                    nc.vector.bn_stats(stats[:, t, :], g.x[:, t, :]).then_inc(stats_done, 1)
                for t in range(NT):
                    dve.wait_ge(stats_done, t + 1)
                    nc.vector.bn_aggr(mv[:, t, :], stats[:, t, :]).then_inc(mean_done, 1)
                dve.wait_ge(std_done, 1)
                nc.vector.reciprocal(rstd[:, :], std[:, :]).then_inc(rstd_done, 1)
                dve.wait_ge(rstd_done, 1)
                for t in range(NT):
                    nc.vector.tensor_scalar(xn[:, t, :], g.x[:, t, :], mv[:, t, 0:1], rstd[:, t:t + 1],
                                            ALU.subtract, ALU.mult).then_inc(normed, 1)

            @block.scalar
            def _(act):
                act.wait_ge(mean_done, NT)
                nc.scalar.activation(std[:, :], mv[:, :, 1], ACT.Sqrt, bias=g.ln_eps[:, 0:1]).then_inc(std_done, 1)
                for t in range(NT if turn else 0):
                    act.wait_ge(turned, t + 1)
                    nc.scalar.activation(g.xt[:, :, t * P:(t + 1) * P],
                                         g.ps[:, t % 4, :].rearrange("p (k c) -> p k c", k=KC),
                                         ACT.Copy).then_inc(copied, 1)

            @block.tensor
            def _(pe):
                for t in range(NT if turn else 0):
                    pe.wait_ge(normed, t + 1)
                    if t >= 4:
                        pe.wait_ge(copied, t - 3)
                    for k in range(KC):
                        mm = nc.tensor.transpose(g.ps[:, t % 4, k * P:(k + 1) * P], xn[:, t, k * P:(k + 1) * P],
                                                 g.ident[:, :])
                    mm.then_inc(turned, 1)


def self_attention(nc, g, name, wqkv, wo, rope, mask):
    with Stage(nc, name) as st:
        qt = st.sbuf("qt", [P, B * KC, S])
        kt = st.sbuf("kt", [P, B * KC, S])
        v = st.sbuf("v", [P, B * KC, S // P, P])
        ot = st.sbuf("ot", [P, B * KC, S])
        wos = st.sbuf("wo", [P, KC, D])
        masks = st.sbuf("mask", [P, P])
        wo_loaded = st.sem("wo_loaded")
        with Stage(nc, name + "_proj") as pr:
            project_self(nc, g, pr, wqkv, rope, qt, kt, v, wos, wo, wo_loaded, masks, mask)
        with Stage(nc, name + "_core") as co:
            attention_core(nc, g, co, qt, kt, v, ot, S // P, masks)
        with Stage(nc, name + "_out") as ou:
            made, added = ou.sem("made"), ou.sem("added")
            with nc.Block() as block:
                @block.tensor
                def _(pe):
                    pe.wait_ge(wo_loaded, 16)
                    for t in range(NT):
                        b, s = divmod(t * P, S)
                        if t >= 4:
                            pe.wait_ge(added, t - 3)
                        for k in range(KC):
                            mm = nc.tensor.matmul(g.ps[:, t % 4, :], ot[:, b * KC + k, s:s + P], wos[:, k, :],
                                                  start=(k == 0), stop=(k == KC - 1))
                        mm.then_inc(made, 1)

                @block.vector
                def _(dve):
                    for t in range(NT):
                        dve.wait_ge(made, t + 1)
                        nc.vector.tensor_tensor(g.x[:, t, :], g.x[:, t, :], g.ps[:, t % 4, :],
                                                ALU.add).then_inc(added, 1)


def project_self(nc, g, st, wqkv, rope, qt, kt, v, wos, wo, wo_loaded, masks, mask):
    w = st.sbuf("w", [P, KC, 3 * D])
    w_loaded, made, copied = st.sem("w_loaded"), st.sem("made"), st.sem("copied")
    v_made, v_copied = st.sem("v_made"), st.sem("v_copied")
    units = [(c, b, dst, part) for part, dst in enumerate((qt, kt)) for c in range(KC) for b in range(B)]
    RAW = 3
    if rope:
        cos, sin, swap = st.sbuf("cos", [P, S]), st.sbuf("sin", [P, S]), st.sbuf("swap", [P, P])
        raw, rc, rs = st.sbuf("raw", [P, RAW, S]), st.sbuf("rc", [P, 2, S]), st.sbuf("rs", [P, 2, S])
        swapped, cos_done, sin_done, rotated = (st.sem("swapped"), st.sem("cos_done"), st.sem("sin_done"),
                                                st.sem("rotated"))
    r_loaded = st.sem("r_loaded")
    with nc.Block() as block:
        @block.sync
        def _(sp):
            for part in range(3):
                sp.dma_start(w[:, :, part * D:(part + 1) * D],
                             wqkv[:, part * D:(part + 1) * D].rearrange("(k p) n -> p k n", p=P)).then_inc(w_loaded, 16)
                if rope and part == 0:
                    sp.dma_start(cos[:, :], rope[0]).then_inc(r_loaded, 16)
                    sp.dma_start(sin[:, :], rope[1]).then_inc(r_loaded, 16)
                    sp.dma_start(swap[:, :], rope[2]).then_inc(r_loaded, 16)
            sp.dma_start(wos[:, :, :], wo.rearrange("(k p) n -> p k n", p=P)).then_inc(wo_loaded, 16)
            sp.dma_start(masks[:, :], mask).then_inc(wo_loaded, 16)
            sp.wait_ge(wo_loaded, 32)

        @block.tensor
        def _(pe):
            def swap_pairs(j):
                pe.wait_ge(copied, j + 1)
                if j == 0:
                    pe.wait_ge(r_loaded, 48)
                if j >= 2:
                    pe.wait_ge(sin_done, j - 1)
                nc.tensor.matmul(g.ps[:, 4 + j % 2, :], swap[:, :], raw[:, j % RAW, :], start=True,
                                 stop=True).then_inc(swapped, 1)

            for j, (c, b, dst, part) in enumerate(units):
                if j % 8 == 0:
                    pe.wait_ge(w_loaded, 48)
                if j >= 4:
                    pe.wait_ge(copied, j - 3)
                for k in range(KC):
                    mm = nc.tensor.matmul(g.ps[:, j % 4, :], w[:, k, part * D + c * P:part * D + (c + 1) * P],
                                          g.xt[:, k, b * S:(b + 1) * S], start=(k == 0), stop=(k == KC - 1))
                mm.then_inc(made, 1)
                if rope and j >= 1:
                    swap_pairs(j - 1)
            if rope:
                swap_pairs(len(units) - 1)
            for t in range(NT):
                if t >= 2:
                    pe.wait_ge(v_copied, t - 1)
                for k in range(KC):
                    mm = nc.tensor.matmul(g.ps[:, 6 + t % 2, :], g.xt[:, k, t * P:(t + 1) * P], w[:, k, 2 * D:3 * D],
                                          start=(k == 0), stop=(k == KC - 1))
                mm.then_inc(v_made, 1)

        @block.scalar
        def _(act):
            for j, (c, b, dst, part) in enumerate(units):
                act.wait_ge(made, j + 1)
                if rope and j >= RAW:
                    act.wait_ge(cos_done, j - RAW + 1)
                    act.wait_ge(swapped, j - RAW + 1)
                out = raw[:, j % RAW, :] if rope else dst[:, b * KC + c, :]
                nc.scalar.activation(out, g.ps[:, j % 4, :], ACT.Copy,
                                     scale=DH ** -0.5 if part == 0 else 1.0).then_inc(copied, 1)
            for t in range(NT):
                b, kb = divmod(t, S // P)
                act.wait_ge(v_made, t + 1)
                nc.scalar.activation(v[:, b * KC:(b + 1) * KC, kb, :],
                                     g.ps[:, 6 + t % 2, :].rearrange("p (c d) -> p c d", c=KC),
                                     ACT.Copy).then_inc(v_copied, 1)

        if rope:
            @block.gpsimd
            def _(pool):
                pool.wait_ge(r_loaded, 48)
                for j in range(len(units)):
                    pool.wait_ge(copied, j + 1)
                    if j >= 2:
                        pool.wait_ge(rotated, j - 1)
                    nc.gpsimd.tensor_tensor(rc[:, j % 2, :], raw[:, j % RAW, :], cos[:, :],
                                            ALU.mult).then_inc(cos_done, 1)

            @block.vector
            def _(dve):
                dve.wait_ge(r_loaded, 48)
                for j, (c, b, dst, part) in enumerate(units):
                    dve.wait_ge(swapped, j + 1)
                    nc.vector.tensor_tensor(rs[:, j % 2, :], g.ps[:, 4 + j % 2, :], sin[:, :],
                                            ALU.mult).then_inc(sin_done, 1)
                    dve.wait_ge(sin_done, j + 1)
                    dve.wait_ge(cos_done, j + 1)
                    nc.vector.tensor_tensor(dst[:, b * KC + c, :], rc[:, j % 2, :], rs[:, j % 2, :],
                                            ALU.add).then_inc(rotated, 1)


def attention_core(nc, g, st, qt, kt, v, ot, nkt, masks=None):
    causal = masks is not None
    NI, U, QB = B * KC, HPC * (S // P), S // P
    NK = nkt * P
    SB = 4 if causal else 2
    sbank = (lambda k: k % SB) if causal else (lambda k: 2 * (k % SB))
    SKEW = 3 if causal else 2
    PR = 4
    HALVES = 1 if causal else 2
    qm = st.sbuf("qm", [P, HPC, S])
    vm = st.sbuf("vm", [P, nkt, P])
    prob = st.sbuf("prob", [P, PR, NK])
    pt = st.sbuf("pt", [P, 2, nkt, S])
    nmax, rsum, rinv = st.sbuf("nmax", [P, PR]), st.sbuf("rsum", [P, PR]), st.sbuf("rinv", [P, PR])
    scores = st.sem("scores")
    max_done = st.sem("max_done")
    exp_done = st.sem("exp_done")
    rinv_done = st.sem("rinv_done")
    prob_done = st.sem("prob_done")
    turned = [st.sem(f"turned{n}") for n in range(HALVES)]
    pt_done = [st.sem(f"pt_done{n}") for n in range(HALVES)]
    pv_done = st.sem("pv_done")
    ot_done = st.sem("ot_done")
    zeroed = st.sem("zeroed")
    qm_done = st.sem("qm_done")
    vm_done = st.sem("vm_done")
    width = (lambda qb: (qb + 1) * P) if causal else (lambda qb: NK)

    def s_ps(k, n):
        return g.ps[:, sbank(k):sbank(k) + (1 if causal else 2), :].rearrange("p a n -> p (a n)")[:, 0:n]

    def t_bank(k, half):
        return 4 + k % 2 if causal else 4 + half

    with nc.Block() as block:
        @block.tensor
        def _(pe):
            def step(i, k, first=False, tail=False):
                u = U * i + k
                h, qb = divmod(k, QB)
                if not tail:
                    if qb == 0:
                        pe.wait_ge(qm_done, HPC * i + h + 1)
                    if not (first and k < SB):
                        pe.wait_ge(exp_done, u - SB + 1)
                    n = width(qb)
                    for a in range(0, n, 512):
                        e = min(n, a + 512)
                        mm = nc.tensor.matmul(s_ps(k, n)[:, a:e], qm[:, h, qb * P:(qb + 1) * P], kt[:, i, a:e],
                                              start=True, stop=not causal)
                    if causal:
                        mm = nc.tensor.matmul(s_ps(k, n)[:, qb * P:n], g.ident[:, :], masks[:, :], start=False,
                                              stop=True)
                    mm.then_inc(scores, 1)
                kk = k - SKEW
                if first and kk < 0:
                    return
                w = u - SKEW
                if not tail or kk < U:
                    wq = kk % QB
                    pe.wait_ge(prob_done, w + 1)
                    for half in range(HALVES):
                        if causal:
                            if not (first and kk < 2):
                                pe.wait_ge(pt_done[0], w - 1)
                            tiles = range(wq + 1)
                        else:
                            if not (first and kk < 1):
                                pe.wait_ge(pt_done[half], w)
                            tiles = range(4 * half, 4 * half + 4)
                        for n, j in enumerate(tiles):
                            mm = nc.tensor.transpose(g.ps[:, t_bank(kk, half), n * P:(n + 1) * P],
                                                     prob[:, kk % PR, j * P:(j + 1) * P], g.ident[:, :])
                        mm.then_inc(turned[half], 1)
                if kk % QB == 0 and not (first and kk == 0):
                    hh = (kk // QB - 1) % HPC
                    heads = HPC * i + kk // QB
                    for half in range(HALVES):
                        pe.wait_ge(pt_done[half], w)
                    pe.wait_ge(vm_done, heads)
                    if hh == 0 and not first:
                        pe.wait_ge(ot_done, i)
                    for j in range(nkt):
                        a = j * P if causal else 0
                        mm = nc.tensor.matmul(g.ps[hh * DH:(hh + 1) * DH, 6, a:S], vm[:, j, hh * DH:(hh + 1) * DH],
                                              pt[:, hh % 2, j, a:S], start=(j == 0), stop=(j == nkt - 1))
                    mm.then_inc(pv_done, 1)

            for k in range(U):
                step(0, k, first=True)
            with pe.Fori(1, NI) as i:
                for k in range(U):
                    step(i, k)
            for k in range(U, U + SKEW + 1):
                step(NI - 1, k, tail=True)

        @block.vector
        def _(dve):
            def step(i, k, first=False, tail=False):
                u = U * i + k
                if not tail:
                    dve.wait_ge(scores, u + 1)
                    nc.vector.tensor_reduce(nmax[:, k % PR:k % PR + 1], s_ps(k, width(k % QB)), X_AXIS, ALU.max,
                                            negate=True).then_inc(max_done, 1)
                if not (first and k < 1) and k <= U:
                    dve.wait_ge(exp_done, u)
                    s = (k - 1) % PR
                    nc.vector.reciprocal(rinv[:, s:s + 1], rsum[:, s:s + 1]).then_inc(rinv_done, 1)
                kk = k - SKEW
                if (first and kk < 0) or kk >= U:
                    return
                w = u - SKEW
                hh, wq = divmod(kk % U, QB)
                dve.wait_ge(turned[0], w + 1)
                if wq == 0 and not (first and hh < 2):
                    dve.wait_ge(pv_done, HPC * i + kk // QB - 1)
                n = wq + 1 if causal else 4
                nc.vector.tensor_copy(pt[:, hh % 2, 0:n, wq * P:(wq + 1) * P],
                                      g.ps[:, t_bank(kk, 0), 0:n * P].rearrange("p (j q) -> p j q", j=n)
                                      ).then_inc(pt_done[0], 1)

            for k in range(U):
                step(0, k, first=True)
            with dve.Fori(1, NI) as i:
                for k in range(U):
                    step(i, k)
            for k in range(U, U + SKEW):
                step(NI - 1, k, tail=True)

        @block.scalar
        def _(act):
            def store(iters):
                act.wait_ge(pv_done, HPC * iters)
                nc.scalar.activation(ot[:, iters - 1, :], g.ps[:, 6, :], ACT.Copy).then_inc(ot_done, 1)

            def step(i, k, first=False, tail=False):
                u = U * i + k
                if not tail:
                    act.wait_ge(max_done, u + 1)
                    if not (first and k < PR):
                        for half in range(HALVES):
                            act.wait_ge(turned[half], u - PR + 1)
                    s = k % PR
                    n = width(k % QB)
                    nc.scalar.activation(prob[:, s, 0:n], s_ps(k, n), ACT.Exp, bias=nmax[:, s:s + 1],
                                         accum_out=rsum[:, s:s + 1]).then_inc(exp_done, 1)
                kk = k - SKEW
                if not causal and not (first and kk < 0) and kk < U:
                    w = u - SKEW
                    hh, wq = divmod(kk % U, QB)
                    act.wait_ge(turned[1], w + 1)
                    if wq == 0 and not (first and hh < 2):
                        act.wait_ge(pv_done, HPC * i + kk // QB - 1)
                    nc.scalar.activation(pt[:, hh % 2, 4:8, wq * P:(wq + 1) * P],
                                         g.ps[:, t_bank(kk, 1), :].rearrange("p (j q) -> p j q", j=4),
                                         ACT.Copy).then_inc(pt_done[1], 1)
                if k == SKEW + 2 and not first and not tail:
                    store(i)

            for k in range(U):
                step(0, k, first=True)
            with act.Fori(1, NI) as i:
                for k in range(U):
                    step(i, k)
            for k in range(U, U + SKEW):
                step(NI - 1, k, tail=True)
            store(NI)

        @block.gpsimd
        def _(pool):
            def put_q(i, h):
                nc.gpsimd.tensor_copy(qm[h * DH:(h + 1) * DH, h, :], qt[h * DH:(h + 1) * DH, i, :]).then_inc(qm_done, 1)
                pool.wait_ge(qm_done, HPC * i + h + 1)

            def put_v(i, h):
                nc.gpsimd.tensor_copy(vm[:, :, h * DH:(h + 1) * DH], v[:, i, :, h * DH:(h + 1) * DH]).then_inc(vm_done, 1)

            def step(i, k, first=False, last=False):
                u = U * i + k
                h, qb = divmod(k, QB)
                n = width(qb)
                pool.wait_ge(rinv_done, u + 1)
                nc.gpsimd.tensor_tensor(prob[:, k % PR, 0:n], prob[:, k % PR, 0:n],
                                        rinv[:, k % PR:k % PR + 1].to_broadcast([P, n]), ALU.mult).then_inc(prob_done, 1)
                if qb == QB - 1:
                    if not last:
                        pool.wait_ge(scores, u + 1)
                        pool.wait_ge(prob_done, u + 1)
                        put_q(i + 1, h)
                    if h == 0 and not first:
                        pool.wait_ge(pv_done, HPC * i)
                        put_v(i, HPC - 1)
                    if h > 0 and not last:
                        pool.wait_ge(pv_done, HPC * i + h)
                        put_v(i + 1, h - 1)

            nc.gpsimd.memset(qm[:, :, :], 0.0).then_inc(zeroed, 1)
            pool.wait_ge(zeroed, 1)
            for h in range(HPC):
                put_q(0, h)
            for h in range(HPC):
                put_v(0, h)
            for k in range(U):
                step(0, k, first=True)
            with pool.Fori(1, NI - 1) as i:
                for k in range(U):
                    step(i, k)
            for k in range(U):
                step(NI - 1, k, last=True)


def cross_attention0(nc, g, name, ctxt, wq, bq_cols, wkvt, bk_cols, bkv, wp, bp):
    xn = g.xt[:, :, :].rearrange("p k (a d) -> p (k a) d", d=D)
    NKT = CTX // P
    with Stage(nc, name) as st:
        qt = st.sbuf("qt", [P, B * KC, S])
        kt = st.sbuf("kt", [P, B * KC, CTX])
        v = st.sbuf("v", [P, B * KC, NKT, P])
        wpt = st.sbuf("wpt", [P, KC, D], BF16)
        wp_scale = st.sbuf("wp_scale", [P, KC])
        with Stage(nc, name + "_proj") as pr:
            project_cross0(nc, g, pr, xn, ctxt, wq, bq_cols, wkvt, bk_cols, bkv, wp, qt, kt, v, wpt, wp_scale)
        ot = st.sbuf("ot", [P, B * KC, S])
        with Stage(nc, name + "_core") as co:
            attention_core(nc, g, co, qt, kt, v, ot, NKT)
        with Stage(nc, name + "_out") as ou:
            output_cross0(nc, g, ou, ot, wpt, wp_scale, bp)


def project_cross0(nc, g, st, xn, ctxt, wq, bq_cols, wkvt, bk_cols, bkv, wp, qt, kt, v, wpt, wp_scale):
    NKT = CTX // P
    NCH = B * CTX // 512
    RING = 2
    w_rows = [st.sbuf("wq_rows", [P, KC, D]), st.sbuf("wp_rows", [P, KC, D])]
    w_int = [st.sbuf("wq_int", [P, KC, D], BF16), st.sbuf("wp_int", [P, KC, D], BF16)]
    wqt = st.sbuf("wqt", [P, KC, D], BF16)
    wts = [wqt, wpt]
    wq_scale = st.sbuf("wq_scale", [P, KC])
    wkv = st.sbuf("wkv", [P, KC, 2 * D])
    ctx = st.sbuf("ctx", [P, RING, KC, 512])
    x_int = st.sbuf("x_int", [P, NT, D], BF16)
    xqt = st.sbuf("xqt", [P, KC, T], BF16)
    rounded = st.sbuf("rounded", [P, 2, D])
    top = st.sbuf("top", [P, NT + 2 * KC])
    scale = st.sbuf("scale", [P, NT + 2 * KC])
    inv = st.sbuf("inv", [P, NT + 2 * KC])
    diag = st.sbuf("diag", [P, 2, P])
    xs_row = st.sbuf("xs_row", [P, T])
    bqs, bks = st.sbuf("bqs", [P, KC]), st.sbuf("bks", [P, KC])
    bqss = st.sbuf("bqss", [P, KC])
    bv = st.sbuf("bv", [P, D])
    qs = rounded
    w_loaded = [st.sem("wq_loaded"), st.sem("wp_loaded")]
    wkv_loaded, b_loaded = st.sem("wkv_loaded"), st.sem("b_loaded")
    ctx_loaded = [st.sem(f"ctx_loaded{n}") for n in range(RING)]
    tops, scaled, inverted, shifted, clipped = (st.sem("tops"), st.sem("scaled"), st.sem("inverted"),
                                                st.sem("shifted"), st.sem("clipped"))
    ints = st.sem("ints")
    turned, turned_done = st.sem("turned"), st.sem("turned_done")
    diag_done, row_made, row_done = st.sem("diag_done"), st.sem("row_made"), st.sem("row_done")
    q_made, q_scaled, q_done, bias_done = st.sem("q_made"), st.sem("q_scaled"), st.sem("q_done"), st.sem("bias_done")
    k_made, k_done, v_made, v_done = st.sem("k_made"), st.sem("k_done"), st.sem("v_made"), st.sem("v_done")
    jobs = [(w_rows[0][:, c, :], w_int[0][:, c, :], c) for c in range(KC)]
    jobs += [(xn[:, t, :], x_int[:, t, :], KC + t) for t in range(NT)]
    jobs += [(w_rows[1][:, c, :], w_int[1][:, c, :], KC + NT + c) for c in range(KC)]
    NJ = len(jobs)
    with nc.Block() as block:
        @block.sync
        def _(sp):
            sp.dma_start(wkv[:, :, 0:D], wkvt[:, 0:D].rearrange("(k p) n -> p k n", p=P)).then_inc(wkv_loaded, 16)
            for n in range(NCH):
                if n >= RING:
                    sp.wait_ge(k_made, KC * (n - RING + 1))
                    sp.wait_ge(v_made, 4 * (n - RING + 1))
                sp.dma_start(ctx[:, n % RING, :, :],
                             ctxt[:, n * 512:(n + 1) * 512].rearrange("(k p) n -> p k n", p=P)
                             ).then_inc(ctx_loaded[n % RING], 16)
                if n == 0:
                    sp.dma_start(bks[:, :], bk_cols).then_inc(b_loaded, 16)
                    sp.dma_start(bqs[:, :], bq_cols).then_inc(b_loaded, 16)
                    sp.dma_start(bv[:, :], bkv[D:2 * D].partition_broadcast(P)).then_inc(b_loaded, 16)
                    sp.dma_start(wkv[:, :, D:2 * D],
                                 wkvt[:, D:2 * D].rearrange("(k p) n -> p k n", p=P)).then_inc(wkv_loaded, 16)
                    for n, src in enumerate((wq, wp)):
                        sp.dma_start(w_rows[n][:, :, :], src.rearrange("(c p) n -> p c n", p=P)).then_inc(w_loaded[n], 16)

        @block.vector
        def _(dve):
            def round_rows(first, n, group):
                for j in range(first, first + n):
                    nc.vector.tensor_reduce(top[:, j:j + 1], jobs[j][0], X_AXIS, ALU.max,
                                            apply_absolute_value=True).then_inc(tops, 1)
                dve.wait_ge(tops, first + n)
                nc.vector.tensor_scalar(scale[:, first:first + n], top[:, first:first + n], 1.0 / 127.0, 1e-8,
                                        ALU.mult, ALU.max).then_inc(scaled, 1)
                dve.wait_ge(scaled, group + 1)
                nc.vector.reciprocal(inv[:, first:first + n], scale[:, first:first + n]).then_inc(inverted, 1)
                dve.wait_ge(inverted, group + 1)
                for j in range(first, first + n):
                    if j >= 2:
                        dve.wait_ge(ints, j - 1)
                    nc.vector.tensor_scalar(rounded[:, j % 2, :], jobs[j][0], inv[:, j:j + 1], ROUND, ALU.mult,
                                            ALU.add).then_inc(shifted, 1)
                    dve.wait_ge(shifted, j + 1)
                    nc.vector.tensor_scalar(rounded[:, j % 2, :], rounded[:, j % 2, :], ROUND - 127.0, ROUND + 127.0,
                                            ALU.max, ALU.min).then_inc(clipped, 1)

            def values(n):
                for t in range(4):
                    m = 4 * n + t
                    b, kb = divmod(m, NKT)
                    dve.wait_ge(v_made, m + 1)
                    nc.vector.tensor_tensor(v[:, b * KC:(b + 1) * KC, kb, :],
                                            g.ps[:, 4 + m % 2, :].rearrange("p (c d) -> p c d", c=KC),
                                            bv[:, :].rearrange("p (c d) -> p c d", c=KC), ALU.add).then_inc(v_done, 1)

            dve.wait_ge(b_loaded, 48)
            nc.vector.tensor_scalar(bqss[:, :], bqs[:, :], DH ** -0.5, None, ALU.mult).then_inc(bias_done, 1)
            values(0)
            dve.wait_ge(w_loaded[0], 16)
            round_rows(0, KC, 0)
            values(1)
            round_rows(KC, NT, 1)
            values(2)
            dve.wait_ge(w_loaded[1], 16)
            round_rows(KC + NT, KC, 2)
            nc.vector.tensor_copy(wp_scale[:, :], scale[:, KC + NT:NJ]).then_inc(bias_done, 1)
            nc.vector.tensor_copy(wq_scale[:, :], scale[:, 0:KC]).then_inc(bias_done, 1)
            values(3)
            for t in range(NT):
                if t >= 2:
                    dve.wait_ge(row_made, t - 1)
                nc.vector.tensor_scalar(diag[:, t % 2, :], g.ident[:, :], scale[:, KC + t:KC + t + 1], None,
                                        ALU.mult).then_inc(diag_done, 1)
            dve.wait_ge(bias_done, 3)
            dve.wait_ge(row_done, 2)
            for j in range(2 * KC):
                c, b = divmod(j, B)
                dve.wait_ge(q_made, j + 1)
                if j >= 2:
                    dve.wait_ge(q_done, j - 1)
                nc.vector.scalar_tensor_tensor(qs[:, j % 2, :], g.ps[:, j % 4, :], wq_scale[:, c:c + 1],
                                               xs_row[:, b * S:(b + 1) * S], ALU.mult, ALU.mult).then_inc(q_scaled, 1)

        @block.scalar
        def _(act):
            def keys(n):
                b, half = divmod(n, CTX // 512)
                for c in range(KC):
                    m = KC * n + c
                    act.wait_ge(k_made, m + 1)
                    nc.scalar.activation(kt[:, b * KC + c, half * 512:(half + 1) * 512], g.ps[:, m % 4, :], ACT.Identity,
                                         bias=bks[:, c:c + 1]).then_inc(k_done, 1)

            def whole(first, n):
                for j in range(first, first + n):
                    act.wait_ge(clipped, j + 1)
                    nc.scalar.activation(jobs[j][1], rounded[:, j % 2, :], ACT.Copy, bias=-ROUND).then_inc(ints, 1)

            def turn(n, dst):
                act.wait_ge(turned, n + 1)
                nc.scalar.activation(dst, g.ps[:, 6 + n % 2, 0:256].bitcast(BF16).rearrange("p (k c) -> p k c", k=KC),
                                     ACT.Copy).then_inc(turned_done, 1)

            act.wait_ge(b_loaded, 48)
            keys(0)
            whole(0, KC)
            keys(1)
            whole(KC, NT)
            keys(2)
            whole(KC + NT, KC)
            keys(3)
            for n, c in enumerate(range(KC)):
                turn(n, wqt[:, :, c * P:(c + 1) * P])
            for t in range(NT):
                turn(KC + t, xqt[:, :, t * P:(t + 1) * P])
            for c in range(KC):
                turn(KC + NT + c, wpt[:, :, c * P:(c + 1) * P])
            for n in range(2):
                act.wait_ge(row_made, 4 * (n + 1))
                nc.scalar.activation(xs_row[:, n * 512:(n + 1) * 512], g.ps[:, 4 + n, :], ACT.Copy).then_inc(row_done, 1)
            act.wait_ge(bias_done, 1)
            for j in range(2 * KC):
                c, b = divmod(j, B)
                act.wait_ge(q_scaled, j + 1)
                nc.scalar.activation(qt[:, b * KC + c, :], qs[:, j % 2, :], ACT.Identity, bias=bqss[:, c:c + 1],
                                     scale=DH ** -0.5).then_inc(q_done, 1)

        @block.tensor
        def _(pe):
            for n in range(NCH):
                pe.wait_ge(ctx_loaded[n % RING], 16 * (n // RING + 1))
                pe.wait_ge(wkv_loaded, 32)
                for c in range(KC):
                    m = KC * n + c
                    if m >= 4:
                        pe.wait_ge(k_done, m - 3)
                    for k in range(KC):
                        mm = nc.tensor.matmul(g.ps[:, m % 4, :], wkv[:, k, c * P:(c + 1) * P], ctx[:, n % RING, k, :],
                                              start=(k == 0), stop=(k == KC - 1))
                    mm.then_inc(k_made, 1)
                for t in range(4):
                    m = 4 * n + t
                    if m >= 2:
                        pe.wait_ge(v_done, m - 1)
                    for k in range(KC):
                        mm = nc.tensor.matmul(g.ps[:, 4 + m % 2, :], ctx[:, n % RING, k, t * P:(t + 1) * P],
                                              wkv[:, k, D:2 * D], start=(k == 0), stop=(k == KC - 1))
                    mm.then_inc(v_made, 1)
            for n, (_, whole, _) in enumerate(jobs):
                pe.wait_ge(ints, n + 1)
                if n >= 2:
                    pe.wait_ge(turned_done, n - 1)
                for k in range(KC):
                    mm = nc.tensor.transpose(g.ps[:, 6 + n % 2, 0:256].bitcast(BF16)[:, k * P:(k + 1) * P],
                                             whole[:, k * P:(k + 1) * P], g.ident16[:, :])
                mm.then_inc(turned, 1)
            for t in range(NT):
                pe.wait_ge(diag_done, t + 1)
                if t == 0:
                    pe.wait_ge(v_done, B * NKT)
                nc.tensor.matmul(g.ps[:, 4 + t // 4, t % 4 * P:(t % 4 + 1) * P], g.ones[:, :], diag[:, t % 2, :],
                                 start=True, stop=True).then_inc(row_made, 1)
            pe.wait_ge(turned_done, NJ)
            pe.wait_ge(k_done, KC * NCH)
            for j in range(2 * KC):
                c, b = divmod(j, B)
                if j >= 4:
                    pe.wait_ge(q_scaled, j - 3)
                for k in range(KC):
                    mm = nc.tensor.matmul(g.ps[:, j % 4, :], wqt[:, k, c * P:(c + 1) * P],
                                          xqt[:, k, b * S:(b + 1) * S], start=(k == 0), stop=(k == KC - 1))
                mm.then_inc(q_made, 1)


def output_cross0(nc, g, st, ot, wpt, wp_scale, bp):
    o_int = st.sbuf("o_int", [P, NT, D], BF16)
    oqt = st.sbuf("oqt", [P, NT, KC, P], BF16)
    rounded = st.sbuf("rounded", [P, NT, D])
    top, scale, inv = st.sbuf("top", [P, NT]), st.sbuf("scale", [P, NT]), st.sbuf("inv", [P, NT])
    diag = st.sbuf("diag", [P, KC, P])
    ws_row, bps = st.sbuf("ws_row", [P, D]), st.sbuf("bps", [P, D])
    y = st.sbuf("y", [P, 2, D])
    b_loaded, diag_done, row_made, row_done = st.sem("b_loaded"), st.sem("diag_done"), st.sem("row_made"), st.sem("row_done")
    rows, tops, scaled, inverted = st.sem("rows"), st.sem("tops"), st.sem("scaled"), st.sem("inverted")
    shifted, clipped, ints = st.sem("shifted"), st.sem("clipped"), st.sem("ints")
    turned, turned_done, made, y_done, added = (st.sem("turned"), st.sem("turned_done"), st.sem("made"),
                                                st.sem("y_done"), st.sem("added"))
    biased = st.sem("biased")
    with nc.Block() as block:
        @block.sync
        def _(sp):
            sp.dma_start(bps[:, :], bp.partition_broadcast(P)).then_inc(b_loaded, 16)

        @block.gpsimd
        def _(pool):
            pool.wait_ge(b_loaded, 16)
            for t in range(NT):
                nc.gpsimd.tensor_tensor(g.x[:, t, :], g.x[:, t, :], bps[:, :], ALU.add).then_inc(biased, 1)

        def project(pe, t):
            pe.wait_ge(turned_done, t + 1)
            if t >= 2:
                pe.wait_ge(y_done, t - 1)
            for k in range(KC):
                mm = nc.tensor.matmul(g.ps[:, 2 + t % 2, :], oqt[:, t, k, :], wpt[:, k, :], start=(k == 0),
                                      stop=(k == KC - 1))
            mm.then_inc(made, 1)

        @block.tensor
        def _(pe):
            for c in range(KC):
                pe.wait_ge(diag_done, c + 1)
                mm = nc.tensor.matmul(g.ps[:, 7, c * P:(c + 1) * P], g.ones[:, :], diag[:, c, :], start=True, stop=True)
            mm.then_inc(row_made, 1)
            pe.wait_ge(row_done, 1)
            for t in range(NT):
                b, s = divmod(t * P, S)
                for k in range(KC):
                    mm = nc.tensor.transpose(g.ps[:, t, k * P:(k + 1) * P], ot[:, b * KC + k, s:s + P], g.ident[:, :])
                mm.then_inc(rows, 1)
            for t in range(NT):
                pe.wait_ge(ints, t + 1)
                if t == 0:
                    pe.wait_ge(clipped, 4)
                if t >= 2:
                    pe.wait_ge(turned_done, t - 1)
                for k in range(KC):
                    mm = nc.tensor.transpose(g.ps[:, t % 2, 0:256].bitcast(BF16)[:, k * P:(k + 1) * P],
                                             o_int[:, t, k * P:(k + 1) * P], g.ident16[:, :])
                mm.then_inc(turned, 1)
                if t >= 1:
                    project(pe, t - 1)
            project(pe, NT - 1)

        @block.vector
        def _(dve):
            for c in range(KC):
                nc.vector.tensor_scalar(diag[:, c, :], g.ident[:, :], wp_scale[:, c:c + 1], None,
                                        ALU.mult).then_inc(diag_done, 1)
            for t in range(NT):
                dve.wait_ge(rows, t + 1)
                nc.vector.tensor_reduce(top[:, t:t + 1], g.ps[:, t, :], X_AXIS, ALU.max,
                                        apply_absolute_value=True).then_inc(tops, 1)
            dve.wait_ge(tops, NT)
            nc.vector.tensor_scalar(scale[:, :], top[:, :], 1.0 / 127.0, 1e-8, ALU.mult, ALU.max).then_inc(scaled, 1)
            dve.wait_ge(scaled, 1)
            nc.vector.reciprocal(inv[:, :], scale[:, :]).then_inc(inverted, 1)
            dve.wait_ge(inverted, 1)
            for t in range(NT):
                nc.vector.tensor_scalar(rounded[:, t, :], g.ps[:, t, :], inv[:, t:t + 1], ROUND, ALU.mult,
                                        ALU.add).then_inc(shifted, 1)
                dve.wait_ge(shifted, t + 1)
                nc.vector.tensor_scalar(rounded[:, t, :], rounded[:, t, :], ROUND - 127.0, ROUND + 127.0, ALU.max,
                                        ALU.min).then_inc(clipped, 1)
            for t in range(NT):
                dve.wait_ge(made, t + 1)
                if t == 0:
                    dve.wait_ge(row_done, 1)
                nc.vector.scalar_tensor_tensor(y[:, t % 2, :], g.ps[:, 2 + t % 2, :], scale[:, t:t + 1], ws_row[:, :],
                                               ALU.mult, ALU.mult).then_inc(y_done, 1)
                dve.wait_ge(y_done, t + 1)
                dve.wait_ge(biased, t + 1)
                nc.vector.tensor_tensor(g.x[:, t, :], g.x[:, t, :], y[:, t % 2, :], ALU.add).then_inc(added, 1)

        def put(act, t):
            act.wait_ge(turned, t + 1)
            nc.scalar.activation(oqt[:, t, :, :],
                                 g.ps[:, t % 2, 0:256].bitcast(BF16).rearrange("p (k c) -> p k c", k=KC),
                                 ACT.Copy).then_inc(turned_done, 1)

        @block.scalar
        def _(act):
            act.wait_ge(row_made, 1)
            nc.scalar.activation(ws_row[:, :], g.ps[:, 7, :], ACT.Copy).then_inc(row_done, 1)
            for t in range(NT):
                act.wait_ge(clipped, t + 1)
                nc.scalar.activation(o_int[:, t, :], rounded[:, t, :], ACT.Copy, bias=-ROUND).then_inc(ints, 1)
                if t >= 1:
                    put(act, t - 1)
            put(act, NT - 1)



def router(nc, g, st, name, wr, bias, experts, top_k, gates, iota_e, picks=None):
    w = st.sbuf("w", [P, KC, experts])
    bs = st.sbuf("bs", [P, experts])
    logit = st.sbuf("logit", [P, NT, experts])
    top = st.sbuf("top", [P, NT])
    total, inv = st.sbuf("total", [P, NT]), st.sbuf("inv", [P, NT])
    best = st.sbuf("best", [P, NT, 8])
    at, atf = st.sbuf("at", [P, NT, 8], U32), st.sbuf("atf", [P, NT, 8])
    ksum, kinv = st.sbuf("ksum", [P, NT]), st.sbuf("kinv", [P, NT])
    one = st.sbuf("one", [P, 2, NT, experts])
    iota = st.sbuf("iota", [P, experts])
    loaded, made, exped, step = st.sem("loaded"), st.sem("made"), st.sem("exped"), st.sem("step")
    shape = [P, NT, experts]

    def over(a):
        return a.rearrange("p (t o) -> p t o", o=1).to_broadcast(shape)

    with nc.Block() as block:
        @block.sync
        def _(sp):
            sp.dma_start(w[:, :, :], wr.rearrange("(k p) e -> p k e", p=P)).then_inc(loaded, 16)
            sp.dma_start(iota[:, :], iota_e[0:experts].partition_broadcast(P)).then_inc(loaded, 16)
            if bias is not None:
                sp.dma_start(bs[:, :], bias.partition_broadcast(P)).then_inc(loaded, 16)

        @block.tensor
        def _(pe):
            pe.wait_ge(loaded, 32 if bias is None else 48)
            for t in range(NT):
                for k in range(KC):
                    mm = nc.tensor.matmul(g.ps[:, 0, t * experts:(t + 1) * experts], g.xt[:, k, t * P:(t + 1) * P],
                                          w[:, k, :], start=(k == 0), stop=(k == KC - 1))
            mm.then_inc(made, 1)

        @block.scalar
        def _(act):
            act.wait_ge(step, 3)
            nc.scalar.activation(logit[:, :, :], logit[:, :, :], ACT.Exp).then_inc(exped, 1)

        @block.vector
        def _(dve):
            done = [0]

            def then(ins):
                ins.then_inc(step, 1)
                done[0] += 1
                dve.wait_ge(step, done[0])

            raw = g.ps[:, 0, 0:NT * experts].rearrange("p (t e) -> p t e", t=NT)
            dve.wait_ge(made, 1)
            if bias is None:
                then(nc.vector.tensor_copy(logit[:, :, :], raw))
            else:
                dve.wait_ge(loaded, 48)
                then(nc.vector.tensor_tensor(logit[:, :, :], raw,
                                             bs[:, :].rearrange("p (o e) -> p o e", o=1).to_broadcast(shape), ALU.add))
            then(nc.vector.tensor_reduce(top[:, :], logit[:, :, :], X_AXIS, ALU.max))
            then(nc.vector.tensor_tensor(logit[:, :, :], logit[:, :, :], over(top[:, :]), ALU.subtract))
            dve.wait_ge(exped, 1)
            then(nc.vector.tensor_reduce(total[:, :], logit[:, :, :], X_AXIS, ALU.add))
            then(nc.vector.reciprocal(inv[:, :], total[:, :]))
            then(nc.vector.tensor_tensor(logit[:, :, :], logit[:, :, :], over(inv[:, :]), ALU.mult))
            for t in range(NT):
                then(nc.vector.max(best[:, t, :], logit[:, t, :]))
                then(nc.vector.max_index(at[:, t, :], best[:, t, :], logit[:, t, :]))
            then(nc.vector.tensor_copy(atf[:, :, :], at[:, :, :]))
            then(nc.vector.tensor_reduce(ksum[:, :], best[:, :, 0:top_k], X_AXIS, ALU.add))
            then(nc.vector.tensor_scalar(ksum[:, :], ksum[:, :], TOPK_EPS, None, ALU.add))
            then(nc.vector.reciprocal(kinv[:, :], ksum[:, :]))
            then(nc.vector.tensor_tensor(best[:, :, :], best[:, :, :],
                                         kinv[:, :].rearrange("p (t o) -> p t o", o=1).to_broadcast([P, NT, 8]), ALU.mult))
            for k in range(top_k):
                then(nc.vector.tensor_tensor(one[:, 0], iota[:, :].rearrange("p (o e) -> p o e", o=1).to_broadcast(shape),
                                             atf[:, :, k:k + 1].to_broadcast(shape), ALU.is_equal))
                then(nc.vector.tensor_tensor(gates if k == 0 else one[:, 1], one[:, 0],
                                             best[:, :, k:k + 1].to_broadcast(shape), ALU.mult))
                if k:
                    then(nc.vector.tensor_tensor(gates, gates, one[:, 1], ALU.add))


def experts_all_tokens(nc, g, st, w1, w2, experts, gates, gated, b1_rows=None, b2_rows=None):
    NF = len(FCH)
    HU = 2 * NF
    W1 = 2 * F if gated else F
    w1s = [st.sbuf(f"w1_{n}", [P, KC, W1]) for n in range(2)]
    w2s = [st.sbuf(f"w2_{n}", [P, NF, D]) for n in range(2)]
    ht = [st.sbuf(f"ht{n}", [P, NF, T]) for n in range(2)]
    silu = st.sbuf("silu", [P, 2, 512]) if gated else None
    w1_loaded = [st.sem(f"w1_loaded{n}") for n in range(2)]
    w2_loaded = [st.sem(f"w2_loaded{n}") for n in range(2)]
    h_made = st.sem("h_made")
    h_done = st.sem("h_done")
    silu_done = st.sem("silu_done")
    y_made = st.sem("y_made")
    y_added = st.sem("y_added")
    b_loaded, b_turned, b_done, bias_made, bias_added = (st.sem("b_loaded"), st.sem("b_turned"), st.sem("b_done"),
                                                         st.sem("bias_made"), st.sem("bias_added"))
    if not gated:
        b1 = st.sbuf("b1", [P, 2, NF])
        b1_put = st.sem("b1_put")
        b1r, b1t = st.sbuf("b1r", [experts, F]), st.sbuf("b1t", [P, NF, experts])
        b2r = st.sbuf("b2r", [experts, D])
        gt = st.sbuf("gt", [experts, T])
    bank = lambda u, half: (2 * (u % 2) + half) if gated else u % 4
    with nc.Block() as block:
        @block.sync
        def _(sp):
            def load(e, slot, first=False):
                if not first:
                    sp.wait_ge(h_made, HU * (e - 1))
                sp.dma_start(w1s[slot][:, :, :], w1[e].rearrange("(k p) f -> p k f", p=P)).then_inc(w1_loaded[slot], 16)
                if not first:
                    sp.wait_ge(y_made, NT * (e - 1))
                sp.dma_start(w2s[slot][:, 0:2, :], w2[e, 0:256, :].rearrange("(c p) n -> p c n", p=P)
                             ).then_inc(w2_loaded[slot], 16)
                sp.dma_start(w2s[slot][0:FCH[2][1], 2, :], w2[e, 256:F, :]).then_inc(w2_loaded[slot], 16)

            load(0, 0, first=True)
            if not gated:
                sp.dma_start(b1r[:, :], b1_rows).then_inc(b_loaded, 16)
                sp.dma_start(b2r[:, :], b2_rows).then_inc(b_loaded, 16)
            load(1, 1, first=True)
            if experts > 2:
                with sp.Fori(1, experts // 2) as i:
                    load(2 * i, 0)
                    load(2 * i + 1, 1)

        @block.tensor
        def _(pe):
            def expert(i, slot, first=False):
                e = 2 * i + slot
                pe.wait_ge(w1_loaded[slot], 16 * i + 16)
                for u in range(HU):
                    half, f = divmod(u, NF)
                    f0, fn = FCH[f]
                    free = 2 if gated else 4
                    if not (first and slot == 0 and u < free):
                        pe.wait_ge(h_done, HU * e + u - free + 1)
                    for part in range(2 if gated else 1):
                        for k in range(KC):
                            mm = nc.tensor.matmul(g.ps[0:fn, bank(u, part), :],
                                                  w1s[slot][:, k, part * F + f0:part * F + f0 + fn],
                                                  g.xt[:, k, half * 512:(half + 1) * 512], start=(k == 0),
                                                  stop=(k == KC - 1))
                    mm.then_inc(h_made, 1)
                pe.wait_ge(w2_loaded[slot], 32 * i + 32)
                for t in range(NT):
                    if t % 4 == 0:
                        pe.wait_ge(h_done, HU * e + NF * (t // 4 + 1))
                    if not (first and slot == 0 and t < 4):
                        pe.wait_ge(y_added, NT * e + t - 3)
                    for f, (f0, fn) in enumerate(FCH):
                        mm = nc.tensor.matmul(g.ps[:, 4 + t % 4, :], ht[slot][0:fn, f, t * P:(t + 1) * P],
                                              w2s[slot][0:fn, f, :], start=(f == 0), stop=(f == NF - 1))
                    mm.then_inc(y_made, 1)

            if not gated:
                pe.wait_ge(b_loaded, 32)
                for f, (f0, fn) in enumerate(FCH):
                    mm = nc.tensor.transpose(g.ps[0:fn, 0, f * experts:(f + 1) * experts], b1r[:, f0:f0 + fn],
                                             g.ident[0:experts, 0:experts])
                for t in range(NT):
                    mm = nc.tensor.transpose(g.ps[0:experts, 1 + t // 4, t % 4 * P:(t % 4 + 1) * P], gates[:, t, :],
                                             g.ident[:, :])
                mm.then_inc(b_turned, 1)
                pe.wait_ge(b_done, 3)
                for t in range(NT):
                    if t >= 4:
                        pe.wait_ge(bias_added, t - 3)
                    nc.tensor.matmul(g.ps[:, 4 + t % 4, :], gt[:, t * P:(t + 1) * P], b2r[:, :], start=True,
                                     stop=True).then_inc(bias_made, 1)
                pe.wait_ge(bias_added, NT)
            expert(0, 0, first=True)
            expert(0, 1, first=True)
            if experts > 2:
                with pe.Fori(1, experts // 2) as i:
                    expert(i, 0)
                    expert(i, 1)

        @block.scalar
        def _(act):
            if not gated:
                act.wait_ge(b_turned, 1)
                for f, (f0, fn) in enumerate(FCH):
                    if f != 1:
                        a, n = (0, 2) if f == 0 else (2, 1)
                        nc.scalar.activation(b1t[0:fn, a:a + n, :],
                                             g.ps[0:fn, 0, a * experts:(a + n) * experts].rearrange(
                                                 "p (f e) -> p f e", f=n), ACT.Copy).then_inc(b_done, 1)
                nc.scalar.activation(gt[:, :], g.ps[0:experts, 1:3, :].rearrange("p a n -> p (a n)"),
                                     ACT.Copy).then_inc(b_done, 1)

            def expert(i, slot, first=False):
                e = 2 * i + slot
                if not gated:
                    for rows, lo, hi in ((P, 0, NF - 1), (FCH[-1][1], NF - 1, NF)):
                        nc.scalar.activation(b1[0:rows, slot, lo:hi],
                                             b1t[0:rows, lo:hi, bass.ds(e, 1)].rearrange("p f o -> p (f o)"),
                                             ACT.Copy).then_inc(b1_put, 1)
                    act.wait_ge(b1_put, 2 * e + 2)
                for u in range(HU):
                    half, f = divmod(u, NF)
                    f0, fn = FCH[f]
                    act.wait_ge(h_made, HU * e + u + 1)
                    if gated:
                        if not (first and slot == 0 and u < 2):
                            act.wait_ge(h_done, HU * e + u - 1)
                        nc.scalar.activation(silu[0:fn, u % 2, :], g.ps[0:fn, bank(u, 0), :], ACT.Silu).then_inc(silu_done, 1)
                    else:
                        if u == 0 and not first:
                            act.wait_ge(y_made, NT * (e - 1))
                        nc.scalar.activation(ht[slot][0:fn, f, half * 512:(half + 1) * 512], g.ps[0:fn, bank(u, 0), :],
                                             ACT.Relu, bias=b1[0:fn, slot, f:f + 1]).then_inc(h_done, 1)

            if not gated:
                act.wait_ge(b_done, 3)
            expert(0, 0, first=True)
            expert(0, 1, first=True)
            if experts > 2:
                with act.Fori(1, experts // 2) as i:
                    expert(i, 0)
                    expert(i, 1)

        @block.vector
        def _(dve):
            def expert(i, slot, first=False):
                e = 2 * i + slot
                if gated:
                    for u in range(HU):
                        half, f = divmod(u, NF)
                        f0, fn = FCH[f]
                        dve.wait_ge(silu_done, HU * e + u + 1)
                        if u == 0 and not first:
                            dve.wait_ge(y_made, NT * (e - 1))
                        nc.vector.tensor_tensor(ht[slot][0:fn, f, half * 512:(half + 1) * 512], g.ps[0:fn, bank(u, 1), :],
                                                silu[0:fn, u % 2, :], ALU.mult).then_inc(h_done, 1)
                for t in range(NT):
                    dve.wait_ge(y_made, NT * e + t + 1)
                    if not (first and slot == 0):
                        dve.wait_ge(y_added, NT * e + t - NT + 1)
                    nc.vector.scalar_tensor_tensor(g.x[:, t, :], g.ps[:, 4 + t % 4, :], gates[:, t, bass.ds(e, 1)],
                                                   g.x[:, t, :], ALU.mult, ALU.add).then_inc(y_added, 1)

            if not gated:
                for t in range(NT):
                    dve.wait_ge(bias_made, t + 1)
                    nc.vector.tensor_tensor(g.x[:, t, :], g.x[:, t, :], g.ps[:, 4 + t % 4, :],
                                            ALU.add).then_inc(bias_added, 1)
                dve.wait_ge(bias_added, NT)
            expert(0, 0, first=True)
            expert(0, 1, first=True)
            if experts > 2:
                with dve.Fori(1, experts // 2) as i:
                    expert(i, 0)
                    expert(i, 1)


def moe0(nc, g, name, wgt, w1, w2, iota_e):
    with Stage(nc, name) as st:
        gates = st.sbuf("gates", [P, NT, NE0])
        with Stage(nc, name + "_route") as ro:
            router(nc, g, ro, name, wgt, None, NE0, TOP0, gates[:, :, :], iota_e)
        with Stage(nc, name + "_experts") as ex:
            experts_all_tokens(nc, g, ex, w1, w2, NE0, gates, gated=True)


def moe1(nc, g, name, sw1, sb1, sw2, sb2, rw1, rb1, rw2, rb2, wr, br, iota_e):
    with Stage(nc, name) as st:
        gates = st.sbuf("gates", [P, NT, NE1])
        even = st.sbuf("even", [P, NT, NSH])
        with Stage(nc, name + "_route") as ro:
            router(nc, g, ro, name, wr, br, NE1, TOP1, gates[:, :, :], iota_e)
        with Stage(nc, name + "_even") as ev:
            set_ = ev.sem("set")
            with nc.Block() as block:
                @block.vector
                def _(dve):
                    nc.vector.memset(even[:, :, :], 1.0 / NSH).then_inc(set_, 1)
                    dve.wait_ge(set_, 1)
        with Stage(nc, name + "_shared") as sh:
            experts_all_tokens(nc, g, sh, sw1, sw2, NSH, even, False, sb1, sb2)
        with Stage(nc, name + "_routed") as ex:
            experts_all_tokens(nc, g, ex, rw1, rw2, NE1, gates, False, rb1, rb2)


def cross_attention1(nc, g, name, a):
    NKT = CTX // P
    k_dram = nc.dram_tensor("k_raw", (B * H, P, CTX), F32, kind="Internal").ap()
    q_dram = nc.dram_tensor("q_raw", (B * H, P, S), F32, kind="Internal").ap()
    v_dram = nc.dram_tensor("v_rows", (B * H, NKT, P, DX), F32, kind="Internal").ap()
    with Stage(nc, name) as st:
        rk = st.sbuf("rk", [P, B * CTX])
        rq = st.sbuf("rq", [P, T])
        k_scale = st.sbuf("k_scale", [P, 2, B * H])
        with Stage(nc, name + "_made") as md:
            ctx = md.sbuf("ctx", [P, KC, B * CTX])
            ctx_loaded = md.sem("ctx_loaded")
            with Stage(nc, name + "_kq") as kq:
                project_kq1(nc, g, kq, a, ctx, ctx_loaded, k_dram, q_dram, rk, rq, k_scale)
            with Stage(nc, name + "_v") as vs:
                project_v1(nc, g, vs, a, ctx, v_dram)
        ot = st.sbuf("ot", [P, B * H, S])
        wo = st.sbuf("wo", [P, H, D])
        bo = st.sbuf("bo", [P, D])
        o_loaded = st.sem("o_loaded")
        with Stage(nc, name + "_core") as co:
            attention_core1(nc, g, co, a, k_dram, q_dram, v_dram, rk, rq, k_scale, ot, wo, bo, o_loaded)
        with Stage(nc, name + "_out") as ou:
            made, added, biased = ou.sem("made"), ou.sem("added"), ou.sem("biased")
            with nc.Block() as block:
                @block.gpsimd
                def _(pool):
                    pool.wait_ge(o_loaded, 32)
                    for t in range(NT):
                        nc.gpsimd.tensor_tensor(g.x[:, t, :], g.x[:, t, :], bo[:, :], ALU.add).then_inc(biased, 1)

                @block.tensor
                def _(pe):
                    pe.wait_ge(o_loaded, 32)
                    for t in range(NT):
                        b, s = divmod(t * P, S)
                        if t >= 4:
                            pe.wait_ge(added, t - 3)
                        for h in range(H):
                            mm = nc.tensor.matmul(g.ps[:, t % 4, :], ot[:, b * H + h, s:s + P], wo[:, h, :],
                                                  start=(h == 0), stop=(h == H - 1))
                        mm.then_inc(made, 1)

                @block.vector
                def _(dve):
                    for t in range(NT):
                        dve.wait_ge(made, t + 1)
                        dve.wait_ge(biased, t + 1)
                        nc.vector.tensor_tensor(g.x[:, t, :], g.x[:, t, :], g.ps[:, t % 4, :],
                                                ALU.add).then_inc(added, 1)


def project_kq1(nc, g, st, a, ctx, ctx_loaded, k_dram, q_dram, rk, rq, k_scale):
    UH = 6
    NS = B * CTX + T
    ki_w, k_w, q_w = a["L1_xattn_ki_w"], a["L1_xattn_k_w"], a["L1_xattn_q_w"]
    w = [st.sbuf(f"w{n}", [P, 3, KC, DX]) for n in range(2)]
    cols = st.sbuf("cols", [P, 3, H])
    bias = st.sbuf("bias", [P, 2, 3])
    bias_put = st.sem("bias_put")
    norm_cols = st.sbuf("norm_cols", [P, 3, H])
    raw = st.sbuf("raw", [P, UH, 512])
    sq = st.sbuf("sq", [P, 2, 512])
    sums = st.sbuf("sums", [P, NS])
    rms = st.sbuf("rms", [P, 2, 512])
    eps_q = st.sbuf("eps_q", [P, 1])
    w_loaded = [st.sem(f"w_loaded{n}") for n in range(2)]
    b_loaded, made, done = st.sem("b_loaded"), st.sem("made"), st.sem("done")
    squared, summed, zeroed = st.sem("squared"), st.sem("summed"), st.sem("zeroed")
    stored = [st.sem(f"stored{n}") for n in range(UH)]
    total, rooted, inverted, scaled = st.sem("total"), st.sem("rooted"), st.sem("inverted"), st.sem("scaled")
    with nc.Block() as block:
        @block.sync
        def _(sp):
            def load(h, slot, first=False):
                if not first:
                    sp.wait_ge(made, UH * (h - 1))
                for n, src in enumerate((ki_w, k_w, q_w)):
                    sp.dma_start(w[slot][:, n, :, :],
                                 src[:, bass.ds(h * DX, DX)].rearrange("(k p) n -> p k n", p=P)).then_inc(w_loaded[slot], 16)

            def store(h):
                for u in range(UH):
                    sp.wait_ge(done, UH * h + u + 1)
                    if u < 4:
                        b, half = divmod(u, 2)
                        dst = k_dram[h + b * H, :, half * 512:(half + 1) * 512]
                    else:
                        dst = q_dram[h + (u - 4) * H, :, :]
                    sp.dma_start(dst, raw[:, u, :]).then_inc(stored[u], 16)

            load(0, 0, first=True)
            for c in range(B * 2):
                sp.dma_start(ctx[:, :, c * 512:(c + 1) * 512],
                             a["ctxt"][:, c * 512:(c + 1) * 512].rearrange("(k p) n -> p k n", p=P)).then_inc(ctx_loaded, 16)
                if c == 0:
                    for n, b in enumerate(("ki_b", "k_b", "q_b")):
                        sp.dma_start(cols[:, n, :], a[b + "_cols"]).then_inc(b_loaded, 16)
                    for n, b in enumerate(("nq_s", "nki_s", "nkt_s")):
                        sp.dma_start(norm_cols[:, n, :], a[b + "_cols"]).then_inc(b_loaded, 16)
            load(1, 1, first=True)
            store(0)
            load(2, 0)
            store(1)
            load(3, 1)
            with sp.Fori(1, H // 2 - 1) as i:
                store(2 * i)
                load(2 * i + 2, 0)
                store(2 * i + 1)
                load(2 * i + 3, 1)
            store(H - 2)
            store(H - 1)
            for u in range(UH):
                sp.wait_ge(stored[u], 16 * H)

        @block.tensor
        def _(pe):
            def head(i, slot, first=False):
                h = 2 * i + slot
                pe.wait_ge(w_loaded[slot], 48 * i + 48)
                for u in range(UH):
                    if not (first and slot == 0):
                        pe.wait_ge(done, UH * h + u - UH + 1)
                    if u == 0:
                        parts = [(0, 0, NIMG), (1, NIMG, 512)]
                    elif u == 2:
                        parts = [(0, CTX, CTX + NIMG), (1, CTX + NIMG, CTX + 512)]
                    else:
                        parts = [(1, u * 512, (u + 1) * 512)]
                    for k in range(KC if u >= 4 else 0):
                        mm = nc.tensor.matmul(g.ps[:, u, :], w[slot][:, 2, k, :], g.xt[:, k, (u - 4) * S:(u - 3) * S],
                                              start=(k == 0), stop=(k == KC - 1))
                    for n, lo, hi in parts if u < 4 else ():
                        for k in range(KC):
                            mm = nc.tensor.matmul(g.ps[:, u, lo - u * 512:hi - u * 512], w[slot][:, n, k, :],
                                                  ctx[:, k, lo:hi], start=(k == 0), stop=(k == KC - 1))
                    mm.then_inc(made, 1)

            pe.wait_ge(ctx_loaded, 64)
            head(0, 0, first=True)
            head(0, 1, first=True)
            with pe.Fori(1, H // 2) as i:
                head(i, 0)
                head(i, 1)
            pe.wait_ge(summed, UH * H)
            for c in range(NS // 512):
                nc.tensor.matmul(g.ps[:, c, :], g.ones[:, :], sums[:, c * 512:(c + 1) * 512], start=True,
                                 stop=True).then_inc(total, 1)

        @block.scalar
        def _(act):
            def head(i, slot, first=False):
                h = 2 * i + slot
                nc.scalar.activation(bias[:, slot, :], cols[:, :, bass.ds(h, 1)].rearrange("p n o -> p (n o)"),
                                     ACT.Copy).then_inc(bias_put, 1)
                act.wait_ge(bias_put, h + 1)
                for u in range(UH):
                    act.wait_ge(made, UH * h + u + 1)
                    if not (first and slot == 0):
                        act.wait_ge(stored[u], 16 * h)
                        act.wait_ge(squared, UH * h + u - UH + 1)
                    parts = [(0, 0, NIMG), (1, NIMG, 512)] if u in (0, 2) else [(1 if u < 4 else 2, 0, 512)]
                    for n, lo, hi in parts:
                        ins = nc.scalar.activation(raw[:, u, lo:hi], g.ps[:, u, lo:hi], ACT.Identity,
                                                   bias=bias[:, slot, n:n + 1])
                    ins.then_inc(done, 1)

            act.wait_ge(b_loaded, 96)
            head(0, 0, first=True)
            head(0, 1, first=True)
            with act.Fori(1, H // 2) as i:
                head(i, 0)
                head(i, 1)
            act.wait_ge(zeroed, 2)
            for c in range(NS // 512):
                act.wait_ge(total, c + 1)
                if c >= 2:
                    act.wait_ge(inverted, c - 1)
                keys = c < B * 2
                nc.scalar.activation(rms[:, c % 2, :], g.ps[:, c, :], ACT.Sqrt,
                                     scale=1.0 / INNER if keys else float(DX) / INNER,
                                     bias=g.rms_eps[:, 0:1] if keys else eps_q[:, 0:1]).then_inc(rooted, 1)

        @block.vector
        def _(dve):
            def head(i, slot, first=False):
                h = 2 * i + slot
                for u in range(UH):
                    dve.wait_ge(done, UH * h + u + 1)
                    if not (first and slot == 0 and u < 2):
                        dve.wait_ge(summed, UH * h + u - 1)
                    nc.vector.tensor_tensor(sq[:, u % 2, :], raw[:, u, :], raw[:, u, :], ALU.mult).then_inc(squared, 1)

            nc.vector.memset(eps_q[:, :], RMS_EPS * DX).then_inc(zeroed, 1)
            dve.wait_ge(b_loaded, 96)
            for n in range(2):
                for b in range(B):
                    nc.vector.tensor_tensor(k_scale[:, n, b * H:(b + 1) * H], norm_cols[:, 0, :], norm_cols[:, 1 + n, :],
                                            ALU.mult).then_inc(scaled, 1)
            head(0, 0, first=True)
            head(0, 1, first=True)
            with dve.Fori(1, H // 2) as i:
                head(i, 0)
                head(i, 1)
            for c in range(NS // 512):
                dve.wait_ge(rooted, c + 1)
                dst = rk[:, c * 512:(c + 1) * 512] if c < B * 2 else rq[:, (c - B * 2) * 512:(c - B * 2 + 1) * 512]
                nc.vector.reciprocal(dst, rms[:, c % 2, :]).then_inc(inverted, 1)

        @block.gpsimd
        def _(pool):
            def head(i, slot, first=False):
                h = 2 * i + slot
                for u in range(UH):
                    pool.wait_ge(squared, UH * h + u + 1)
                    if not (first and slot == 0):
                        pool.wait_ge(summed, UH * h + u - UH + 1)
                    nc.gpsimd.tensor_tensor(sums[:, u * 512:(u + 1) * 512], sums[:, u * 512:(u + 1) * 512],
                                            sq[:, u % 2, :], ALU.add).then_inc(summed, 1)

            nc.gpsimd.memset(sums[:, :], 0.0).then_inc(zeroed, 1)
            pool.wait_ge(zeroed, 2)
            head(0, 0, first=True)
            head(0, 1, first=True)
            with pool.Fori(1, H // 2) as i:
                head(i, 0)
                head(i, 1)


def project_v1(nc, g, st, a, ctx, v_dram):
    NKT = CTX // P
    HG = 512 // DX
    NG = H // HG
    EDGE, REST = divmod(NIMG, P)
    assert REST == 1
    RING = 4
    w = [st.sbuf(f"w{n}", [P, 2, KC, 512]) for n in range(2)]
    bias = st.sbuf("bias", [P, 2, INNER])
    rows = st.sbuf("rows", [P, RING, 512])
    w_loaded = [st.sem(f"w_loaded{n}") for n in range(2)]
    b_loaded, made, done, edged = st.sem("b_loaded"), st.sem("made"), st.sem("done"), st.sem("edged")
    stored = [st.sem(f"stored{n}") for n in range(RING)]
    UT = B * NKT
    with nc.Block() as block:
        @block.sync
        def _(sp):
            def load(n, slot, first=False):
                if not first:
                    sp.wait_ge(made, UT * (n - 1))
                for m, src in enumerate((a["L1_xattn_vi_w"], a["L1_xattn_v_w"])):
                    sp.dma_start(w[slot][:, m, :, :],
                                 src[:, bass.ds(n * 512, 512)].rearrange("(k p) n -> p k n", p=P)).then_inc(w_loaded[slot], 16)

            def store(n):
                for t in range(UT):
                    b, kb = divmod(t, NKT)
                    sp.wait_ge(done, UT * n + t + 1)
                    sp.dma_start(v_dram[bass.ds(n * HG + b * H, HG), kb, :, :].rearrange("h p d -> p h d"),
                                 rows[:, t % RING, :].rearrange("p (h d) -> p h d", h=HG)).then_inc(stored[t % RING], 16)

            load(0, 0, first=True)
            sp.dma_start(bias[:, 0, :], a["L1_xattn_vi_b"].partition_broadcast(P)).then_inc(b_loaded, 16)
            sp.dma_start(bias[:, 1, :], a["L1_xattn_v_b"].partition_broadcast(P)).then_inc(b_loaded, 16)
            load(1, 1, first=True)
            with sp.Fori(0, NG // 2 - 1) as i:
                store(2 * i)
                load(2 * i + 2, 0)
                store(2 * i + 1)
                load(2 * i + 3, 1)
            store(NG - 2)
            store(NG - 1)
            for r in range(RING):
                sp.wait_ge(stored[r], 16 * NG * UT // RING)

        @block.tensor
        def _(pe):
            def group(i, slot, first=False):
                n = 2 * i + slot
                pe.wait_ge(w_loaded[slot], 32 * i + 32)
                for t in range(UT):
                    b, kb = divmod(t, NKT)
                    if not (first and slot == 0 and t < 4):
                        pe.wait_ge(done, UT * n + t - 3)
                    kind = 0 if kb < EDGE else 1
                    for k in range(KC):
                        mm = nc.tensor.matmul(g.ps[:, t % 4, :], ctx[:, k, t * P:(t + 1) * P], w[slot][:, kind, k, :],
                                              start=(k == 0), stop=(k == KC - 1))
                    if kb == EDGE:
                        for k in range(KC):
                            mm = nc.tensor.matmul(g.ps[0:1, 4 + b, :], ctx[:, k, t * P:t * P + 1], w[slot][:, 0, k, :],
                                                  start=(k == 0), stop=(k == KC - 1))
                    mm.then_inc(made, 1)

            group(0, 0, first=True)
            group(0, 1, first=True)
            with pe.Fori(1, NG // 2) as i:
                group(i, 0)
                group(i, 1)

        @block.vector
        def _(dve):
            def group(i, slot, first=False):
                n = 2 * i + slot
                for t in range(UT):
                    b, kb = divmod(t, NKT)
                    dve.wait_ge(made, UT * n + t + 1)
                    r = t % RING
                    if not (first and slot == 0 and t < RING):
                        dve.wait_ge(stored[r], (UT // RING * n + t // RING) * 16)
                    kind = 0 if kb < EDGE else 1
                    ins = nc.vector.tensor_tensor(rows[:, r, :], g.ps[:, t % 4, :], bias[:, kind, bass.ds(n * 512, 512)],
                                                  ALU.add)
                    if kb == EDGE:
                        ins.then_inc(edged, 1)
                        dve.wait_ge(edged, B * n + b + 1)
                        ins = nc.vector.tensor_tensor(rows[0:1, r, :], g.ps[0:1, 4 + b, :],
                                                      bias[0:1, 0, bass.ds(n * 512, 512)], ALU.add)
                    ins.then_inc(done, 1)

            dve.wait_ge(b_loaded, 32)
            group(0, 0, first=True)
            group(0, 1, first=True)
            with dve.Fori(1, NG // 2) as i:
                group(i, 0)
                group(i, 1)


def attention_core1(nc, g, st, a, k_dram, q_dram, v_dram, rk, rq, k_scale, ot, wo, bo, o_loaded):
    NKT, QB = CTX // P, S // P
    HP, U = 2, 2 * QB
    NI = B * H // HP
    NB = NI // B
    SB, SKEW, PR = 2, 2, 4
    SPANS = [(0, NIMG), (NIMG, CTX)]
    k = st.sbuf("k", [P, HP, CTX])
    q = st.sbuf("q", [P, HP, S])
    v = st.sbuf("v", [P, HP, NKT, DX])
    prob = g.xt
    pt = st.sbuf("pt", [P, HP, NKT, S])
    nmax, rsum, rinv = st.sbuf("nmax", [P, PR, 2]), st.sbuf("rsum", [P, PR, 2]), st.sbuf("rinv", [P, PR, 2])
    kq_loaded = [st.sem(f"kq_loaded{n}") for n in range(HP)]
    v_loaded = [st.sem(f"v_loaded{n}") for n in range(HP)]
    k_done, q_done = st.sem("k_done"), st.sem("q_done")
    scores = st.sem("scores")
    max_done = st.sem("max_done")
    exp_done = st.sem("exp_done")
    rinv_done = st.sem("rinv_done")
    prob_done = st.sem("prob_done")
    turned = [st.sem(f"turned{n}") for n in range(2)]
    pt_done = [st.sem(f"pt_done{n}") for n in range(2)]
    pv_done = st.sem("pv_done")
    ot_done = st.sem("ot_done")

    def s_ps(n):
        return g.ps[:, 2 * (n % SB):2 * (n % SB) + 2, :].rearrange("p a n -> p (a n)")

    def over_pairs(eng, step):
        for n in range(U):
            step(0, n, 0, 0, first=True)
        with eng.Fori(1, NB - 1) as i:
            for n in range(U):
                step(i, n, 0, 0)
        for n in range(U):
            step(NB - 1, n, 0, 1)
        with eng.Fori(NB, NI - 1) as i:
            for n in range(U):
                step(i, n, 1, 1)
        for n in range(U):
            step(NI - 1, n, 1, None)

    with nc.Block() as block:
        @block.sync
        def _(sp):
            def load(i, s, first=False):
                j = HP * i + s
                if not first:
                    sp.wait_ge(scores, QB * (j - 1))
                sp.dma_start(k[:, s, :], k_dram[j, :, :]).then_inc(kq_loaded[s], 16)
                sp.dma_start(q[:, s, :], q_dram[j, :, :]).then_inc(kq_loaded[s], 16)
                if not first:
                    sp.wait_ge(pv_done, j - 1)
                sp.dma_start(v[:, s, :, :], v_dram[j, :, :, :].rearrange("t p d -> p t d")).then_inc(v_loaded[s], 16)

            load(0, 0, first=True)
            load(0, 1, first=True)
            sp.dma_start(wo[:, :, :], a["L1_xattn_o_w"].rearrange("(h p) n -> p h n", p=P)).then_inc(o_loaded, 16)
            sp.dma_start(bo[:, :], a["L1_xattn_o_b"].partition_broadcast(P)).then_inc(o_loaded, 16)
            with sp.Fori(1, NI) as i:
                load(i, 0)
                load(i, 1)
            sp.wait_ge(o_loaded, 32)

        @block.tensor
        def _(pe):
            def step(i, n, b=0, nb=0, first=False, tail=False):
                u = U * i + n
                s, qb = divmod(n % U, QB)
                if not tail:
                    if qb == 0:
                        pe.wait_ge(k_done, HP * i + s + 1)
                        pe.wait_ge(q_done, HP * i + s + 1)
                    if not (first and n < SB):
                        pe.wait_ge(exp_done, u - SB + 1)
                    for c in range(0, CTX, 512):
                        mm = nc.tensor.matmul(s_ps(n)[:, c:c + 512], q[:, s, qb * P:(qb + 1) * P], k[:, s, c:c + 512],
                                              start=True, stop=True)
                    mm.then_inc(scores, 1)
                nn = n - SKEW
                if first and nn < 0:
                    return
                w = u - SKEW
                if nn < U:
                    pe.wait_ge(prob_done, w + 1)
                    for half in range(2):
                        if not (first and nn < 1):
                            pe.wait_ge(pt_done[half], w)
                        for m in range(4):
                            c = (4 * half + m) * P
                            mm = nc.tensor.transpose(g.ps[:, 4 + half, m * P:(m + 1) * P], prob[:, nn % PR, c:c + P],
                                                     g.ident[:, :])
                        mm.then_inc(turned[half], 1)
                if nn % QB == 0 and not (first and nn == 0):
                    hs = (nn // QB - 1) % HP
                    heads = HP * i + nn // QB
                    for half in range(2):
                        pe.wait_ge(pt_done[half], w)
                    pe.wait_ge(v_loaded[hs], 16 * (i + (nn // QB + 1) // HP))
                    if not (first and nn // QB - 1 < HP):
                        pe.wait_ge(ot_done, heads - HP)
                    for m in range(NKT):
                        mm = nc.tensor.matmul(g.ps[:, 6 + hs, :], v[:, hs, m, :], pt[:, hs, m, :], start=(m == 0),
                                              stop=(m == NKT - 1))
                    mm.then_inc(pv_done, 1)

            over_pairs(pe, step)
            for n in range(U, U + SKEW + 1):
                step(NI - 1, n, tail=True)

        @block.vector
        def _(dve):
            def put_k(j, s, b, loads):
                dve.wait_ge(kq_loaded[s], 32 * loads)
                for m, (lo, hi) in enumerate(SPANS):
                    ins = nc.vector.scalar_tensor_tensor(k[:, s, lo:hi], k[:, s, lo:hi], k_scale[:, m, bass.ds(j, 1)],
                                                         rk[:, b * CTX + lo:b * CTX + hi], ALU.mult, ALU.mult)
                ins.then_inc(k_done, 1)

            def step(i, n, b=0, nb=0, first=False, tail=False):
                u = U * i + n
                s, qb = divmod(n % U, QB)
                if not tail:
                    dve.wait_ge(scores, u + 1)
                    for m, (lo, hi) in enumerate(SPANS):
                        ins = nc.vector.tensor_reduce(nmax[:, n % PR, m:m + 1], s_ps(n)[:, lo:hi], X_AXIS, ALU.max,
                                                      negate=True)
                    ins.then_inc(max_done, 1)
                if not (first and n < 1) and n <= U:
                    dve.wait_ge(exp_done, u)
                    nc.vector.reciprocal(rinv[:, (n - 1) % PR, :], rsum[:, (n - 1) % PR, :]).then_inc(rinv_done, 1)
                nn = n - SKEW
                if not (first and nn < 0) and nn < U:
                    w = u - SKEW
                    hs, wq = divmod(nn % U, QB)
                    dve.wait_ge(turned[0], w + 1)
                    if wq == 0 and not (first and nn // QB < HP):
                        dve.wait_ge(pv_done, HP * i + nn // QB - 1)
                    nc.vector.tensor_copy(pt[:, hs, 0:4, wq * P:(wq + 1) * P],
                                          g.ps[:, 4, :].rearrange("p (m q) -> p m q", m=4)).then_inc(pt_done[0], 1)
                if not tail and qb == 2:
                    if s == 0 and not first:
                        put_k(HP * i + 1, 1, b, i + 1)
                    if s == 1 and nb is not None:
                        put_k(HP * i + 2, 0, nb, i + 2)

            put_k(0, 0, 0, 1)
            put_k(1, 1, 0, 1)
            over_pairs(dve, step)
            for n in range(U, U + SKEW):
                step(NI - 1, n, tail=True)

        @block.scalar
        def _(act):
            def store(j, s):
                act.wait_ge(pv_done, j + 1)
                nc.scalar.activation(ot[:, j, :], g.ps[:, 6 + s, :], ACT.Copy).then_inc(ot_done, 1)

            def step(i, n, b=0, nb=0, first=False, tail=False):
                u = U * i + n
                if not tail:
                    act.wait_ge(max_done, u + 1)
                    if not (first and n < PR):
                        for half in range(2):
                            act.wait_ge(turned[half], u - PR + 1)
                    for m, (lo, hi) in enumerate(SPANS):
                        ins = nc.scalar.activation(prob[:, n % PR, lo:hi], s_ps(n)[:, lo:hi], ACT.Exp,
                                                   bias=nmax[:, n % PR, m:m + 1], accum_out=rsum[:, n % PR, m:m + 1])
                    ins.then_inc(exp_done, 1)
                nn = n - SKEW
                if not (first and nn < 0) and nn < U:
                    w = u - SKEW
                    hs, wq = divmod(nn % U, QB)
                    act.wait_ge(turned[1], w + 1)
                    if wq == 0 and not (first and nn // QB < HP):
                        act.wait_ge(pv_done, HP * i + nn // QB - 1)
                    nc.scalar.activation(pt[:, hs, 4:8, wq * P:(wq + 1) * P],
                                         g.ps[:, 5, :].rearrange("p (m q) -> p m q", m=4), ACT.Copy).then_inc(pt_done[1], 1)
                if not tail and n % QB == SKEW + 1:
                    s = n // QB
                    if s == 1:
                        store(HP * i, 0)
                    elif not first:
                        store(HP * i - 1, 1)

            over_pairs(act, step)
            for n in range(U, U + SKEW):
                step(NI - 1, n, tail=True)
            store(B * H - 1, 1)

        @block.gpsimd
        def _(pool):
            def put_q(j, s, b, loads):
                pool.wait_ge(kq_loaded[s], 32 * loads)
                nc.gpsimd.tensor_tensor(q[:, s, :], q[:, s, :], rq[:, b * S:(b + 1) * S], ALU.mult).then_inc(q_done, 1)

            def step(i, n, b=0, nb=0, first=False):
                u = U * i + n
                s, qb = divmod(n, QB)
                pool.wait_ge(rinv_done, u + 1)
                for m, (lo, hi) in enumerate(SPANS):
                    ins = nc.gpsimd.tensor_tensor(prob[:, n % PR, lo:hi], prob[:, n % PR, lo:hi],
                                                  rinv[:, n % PR, m:m + 1].to_broadcast([P, hi - lo]), ALU.mult)
                ins.then_inc(prob_done, 1)
                if qb == 2:
                    if s == 0 and not first:
                        put_q(HP * i + 1, 1, b, i + 1)
                    if s == 1 and nb is not None:
                        put_q(HP * i + 2, 0, nb, i + 2)

            put_q(0, 0, 0, 1)
            put_q(1, 1, 0, 1)
            over_pairs(pool, step)


def store_residual(nc, g, out):
    with Stage(nc, "store") as st:
        stored = st.sem("stored")
        with nc.Block() as block:
            @block.sync
            def _(sp):
                sp.dma_start(out.rearrange("(t p) d -> p t d", p=P), g.x[:, :, :]).then_inc(stored, 16)
                sp.wait_ge(stored, 16)


def decoder_kernel(nc, a, out, stages=6):
    with ExitStack() as stack:
        g = Shared()

        def sb(name, shape, dt=F32):
            return stack.enter_context(nc.sbuf_tensor(name, shape, dt))

        g.x = sb("residual", [P, NT, D])
        g.xt = sb("normed", [P, KC, T])
        g.ident, g.ident16, g.ones = sb("identity", [P, P]), sb("identity16", [P, P], BF16), sb("all_ones", [P, P])
        g.ln_eps, g.rms_eps = sb("ln_eps", [P, 1]), sb("rms_eps", [P, 1])
        g.ps = stack.enter_context(nc.psum_tensor("ps", [P, 8, 512], F32))
        load_constants(nc, g, a["x"], a["ident"], a["ones"])
        if 1 in stages:
            layer_norm(nc, g, "ln0a")
            self_attention(nc, g, "sa0", a["wqkv0"], a["wo0"], (a["cos"], a["sin"], a["swap"]), a["mask"])
        if 2 in stages:
            layer_norm(nc, g, "ln0b", turn=False)
            cross_attention0(nc, g, "xa0", a["ctxt"], a["L0_xattn_wq"], a["bq0_cols"], a["wkvt0"],
                             a["bk0_cols"], a["L0_xattn_bkv"],
                             a["L0_xattn_wp"], a["L0_xattn_bp"])
        if 3 in stages:
            layer_norm(nc, g, "ln0c")
            moe0(nc, g, "moe0", a["wgt0"], a["L0_ffn_w1"], a["L0_ffn_w2"], a["iota"])
        if 4 in stages:
            layer_norm(nc, g, "ln1a")
            self_attention(nc, g, "sa1", a["wqkv1"], a["wo1"], None, a["mask"])
        if 5 in stages:
            layer_norm(nc, g, "ln1b")
            cross_attention1(nc, g, "xa1", a)
        if 6 in stages:
            layer_norm(nc, g, "ln1c")
            moe1(nc, g, "moe1", a["L1_ffn_sw1"], a["L1_ffn_sb1"], a["L1_ffn_sw2"], a["L1_ffn_sb2"], a["L1_ffn_rw1"],
                 a["L1_ffn_rb1"], a["L1_ffn_rw2"], a["L1_ffn_rb2"], a["L1_ffn_router_w"], a["L1_ffn_router_b"], a["iota"])
        store_residual(nc, g, out)


def lay_out(inputs):
    a = {}
    for name in ("L0_xattn_wq", "L0_xattn_bkv", "L0_xattn_wp", "L0_xattn_bp", "L0_ffn_w1", "L0_ffn_w2",
                 "L1_xattn_q_w", "L1_xattn_k_w", "L1_xattn_v_w", "L1_xattn_v_b",
                 "L1_xattn_ki_w", "L1_xattn_vi_w", "L1_xattn_vi_b", "L1_xattn_o_w", "L1_xattn_o_b",
                 "L1_ffn_sw1", "L1_ffn_sb1", "L1_ffn_sw2",
                 "L1_ffn_sb2", "L1_ffn_rw1", "L1_ffn_rb1", "L1_ffn_rw2", "L1_ffn_rb2", "L1_ffn_router_w",
                 "L1_ffn_router_b"):
        a[name] = np.asarray(inputs[name])
    a["x"] = np.asarray(inputs["x"]).reshape(T, D)
    a["ctxt"] = np.asarray(inputs["ctx_2048"]).reshape(B * CTX, D).T
    a["wqkv0"] = np.concatenate([np.asarray(inputs[f"L0_attn_W{c}"]).T for c in "qkv"], axis=1)
    a["wo0"] = np.asarray(inputs["L0_attn_Wo"]).T
    a["wkvt0"] = np.asarray(inputs["L0_xattn_wkv"]).T
    a["wgt0"] = np.asarray(inputs["L0_ffn_wg"]).T
    a["wqkv1"] = np.asarray(inputs["L1_attn_w_project"]).T
    a["wo1"] = np.asarray(inputs["L1_attn_w_out"]).T
    def columns(v):
        return v.reshape(-1, P).T

    a["bq0_cols"] = columns(np.asarray(inputs["L0_xattn_bq"]))
    a["bk0_cols"] = columns(np.asarray(inputs["L0_xattn_bkv"])[0:D])
    for name in ("q_b", "k_b", "ki_b", "nq_s", "nkt_s", "nki_s"):
        a[name + "_cols"] = columns(np.asarray(inputs["L1_xattn_" + name]))
    freq = np.float32(10000.0) ** (-np.arange(0, DH, 2, dtype=np.float32) / np.float32(DH))
    angles = np.arange(S, dtype=np.float32)[:, None] * freq[None, :]
    a["cos"] = np.tile(np.repeat(np.cos(angles).T, 2, axis=0), (HPC, 1)).astype(np.float32)
    a["sin"] = np.tile(np.repeat(np.sin(angles).T, 2, axis=0), (HPC, 1)).astype(np.float32)
    even = np.arange(0, P, 2)
    swap = np.zeros((P, P), np.float32)
    swap[even + 1, even] = -1.0
    swap[even, even + 1] = 1.0
    a["swap"] = swap
    a["mask"] = np.triu(np.full((P, P), MASKED, np.float32), 1)
    a["ident"] = np.eye(P, dtype=np.float32)
    a["ones"] = np.ones((P, P), np.float32)
    a["iota"] = np.arange(P, dtype=np.float32)
    return {name: np.ascontiguousarray(v) for name, v in a.items()}


def kernel(**inputs):
    import concourse.bacc as bacc
    from concourse.bass_utils import run_bass_kernel_spmd

    nc = bacc.Bacc("TRN2", target_bir_lowering=False, num_devices=1)
    arrays = lay_out(inputs)
    aps = {name: nc.dram_tensor(name, v.shape, mybir.dt.from_np(v.dtype), kind="ExternalInput").ap()
           for name, v in arrays.items()}
    out = nc.dram_tensor("out", (T, D), F32, kind="ExternalOutput").ap()
    decoder_kernel(nc, aps, out, stages=(1, 2, 3, 4, 5, 6))
    result = run_bass_kernel_spmd(nc, [arrays], core_ids=[0])
    return result.results[0]["out"].reshape(B, S, D)
```

```python
from contextlib import ExitStack

import numpy as np

import concourse.bass as bass
from concourse import mybir

P = 128
B, S, D = 2, 512, 512
T = B * S
NT = T // P
KC = D // P
H = 16
DH = D // H
HPC = P // DH
CTX = 1024
NE0, NE1, NSH = 8, 32, 2
TOP0, TOP1 = 2, 6
F = 352
FCH = [(0, 128), (128, 128), (256, 96)]
DX = 128
INNER = H * DX
NIMG = 257
LN_EPS = 1e-5
RMS_EPS = 1e-6
TOPK_EPS = 1e-20
MASKED = -1.0e30
ROUND = 12582912.0

ALU = mybir.AluOpType
ACT = mybir.ActivationFunctionType
F32 = mybir.dt.float32
F32R = mybir.dt.float32r
BF16 = mybir.dt.bfloat16
U32 = mybir.dt.uint32
X_AXIS = mybir.AxisListType.X


class Stage:

    def __init__(self, nc, name):
        self.nc, self.name, self.stack, self.sems = nc, name, ExitStack(), []

    def sbuf(self, name, shape, dt=F32):
        return self.stack.enter_context(self.nc.sbuf_tensor(f"{self.name}_{name}", shape, dt))

    def sem(self, name):
        s = self.nc.alloc_semaphore(f"{self.name}_{name}")
        self.sems.append(s)
        return s

    def __enter__(self):
        return self

    def __exit__(self, *exc):
        if exc[0] is None:
            self.nc.clear_and_free_semaphores(self.sems)
            self.nc.all_engine_barrier()
        return self.stack.__exit__(*exc)


class Shared:
    pass


def load_constants(nc, g, x, ident, ones):
    with Stage(nc, "init") as st:
        loaded = st.sem("loaded")
        cast = st.sem("cast")
        with nc.Block() as block:
            @block.sync
            def _(sp):
                sp.dma_start(g.x[:, :, :], x.rearrange("(t p) d -> p t d", p=P)).then_inc(loaded, 16)
                sp.dma_start(g.ident[:, :], ident).then_inc(loaded, 16)
                sp.dma_start(g.ones[:, :], ones).then_inc(loaded, 16)

            @block.vector
            def _(dve):
                dve.wait_ge(loaded, 48)
                nc.vector.tensor_copy(g.ident16[:, :], g.ident[:, :]).then_inc(cast, 1)
                nc.vector.memset(g.ln_eps[:, :], LN_EPS).then_inc(cast, 1)
                nc.vector.memset(g.rms_eps[:, :], RMS_EPS).then_inc(cast, 1)
                dve.wait_ge(cast, 3)


def layer_norm(nc, g, name, turn=True, rows_dram=None):
    with Stage(nc, name) as st:
        stats = st.sbuf("stats", [P, NT, 6])
        mv = st.sbuf("mv", [P, NT, 2])
        std = st.sbuf("std", [P, NT])
        rstd = st.sbuf("rstd", [P, NT])
        xn = st.sbuf("xn", [P, NT, D]) if turn else g.xt[:, :, :].rearrange("p k (a d) -> p (k a) d", d=D)
        stats_done, mean_done, std_done = st.sem("stats_done"), st.sem("mean_done"), st.sem("std_done")
        rstd_done, normed, turned, copied = st.sem("rstd_done"), st.sem("normed"), st.sem("turned"), st.sem("copied")
        rows_stored = st.sem("rows_stored")
        with nc.Block() as block:
            if rows_dram is not None:
                @block.sync
                def _(sp):
                    for half in range(2):
                        a, b = half * NT // 2, (half + 1) * NT // 2
                        sp.wait_ge(normed, b)
                        sp.dma_start(rows_dram[a * P:b * P, :].rearrange("(t p) d -> p t d", p=P),
                                     xn[:, a:b, :]).then_inc(rows_stored, 16)
                    sp.wait_ge(rows_stored, 32)

            @block.vector
            def _(dve):
                for t in range(NT):
                    nc.vector.bn_stats(stats[:, t, :], g.x[:, t, :]).then_inc(stats_done, 1)
                for t in range(NT):
                    dve.wait_ge(stats_done, t + 1)
                    nc.vector.bn_aggr(mv[:, t, :], stats[:, t, :]).then_inc(mean_done, 1)
                dve.wait_ge(std_done, 1)
                nc.vector.reciprocal(rstd[:, :], std[:, :]).then_inc(rstd_done, 1)
                dve.wait_ge(rstd_done, 1)
                for t in range(NT):
                    nc.vector.tensor_scalar(xn[:, t, :], g.x[:, t, :], mv[:, t, 0:1], rstd[:, t:t + 1],
                                            ALU.subtract, ALU.mult).then_inc(normed, 1)

            @block.scalar
            def _(act):
                act.wait_ge(mean_done, NT)
                nc.scalar.activation(std[:, :], mv[:, :, 1], ACT.Sqrt, bias=g.ln_eps[:, 0:1]).then_inc(std_done, 1)
                for t in range(NT if turn else 0):
                    act.wait_ge(turned, t + 1)
                    nc.scalar.activation(g.xt[:, :, t * P:(t + 1) * P],
                                         g.ps[:, t % 4, :].rearrange("p (k c) -> p k c", k=KC),
                                         ACT.Copy).then_inc(copied, 1)

            @block.tensor
            def _(pe):
                for t in range(NT if turn else 0):
                    pe.wait_ge(normed, t + 1)
                    if t >= 4:
                        pe.wait_ge(copied, t - 3)
                    for k in range(KC):
                        mm = nc.tensor.transpose(g.ps[:, t % 4, k * P:(k + 1) * P], xn[:, t, k * P:(k + 1) * P],
                                                 g.ident[:, :])
                    mm.then_inc(turned, 1)


def self_attention(nc, g, name, wqkv, wo, rope, mask):
    with Stage(nc, name) as st:
        qt = st.sbuf("qt", [P, B * KC, S])
        kt = st.sbuf("kt", [P, B * KC, S])
        v = st.sbuf("v", [P, B * KC, S // P, P])
        ot = st.sbuf("ot", [P, B * KC, S])
        wos = st.sbuf("wo", [P, KC, D])
        masks = st.sbuf("mask", [P, P])
        wo_loaded = st.sem("wo_loaded")
        with Stage(nc, name + "_proj") as pr:
            project_self(nc, g, pr, wqkv, rope, qt, kt, v, wos, wo, wo_loaded, masks, mask)
        with Stage(nc, name + "_core") as co:
            attention_core(nc, g, co, qt, kt, v, ot, S // P, masks)
        with Stage(nc, name + "_out") as ou:
            made, added = ou.sem("made"), ou.sem("added")
            with nc.Block() as block:
                @block.tensor
                def _(pe):
                    pe.wait_ge(wo_loaded, 16)
                    for t in range(NT):
                        b, s = divmod(t * P, S)
                        if t >= 4:
                            pe.wait_ge(added, t - 3)
                        for k in range(KC):
                            mm = nc.tensor.matmul(g.ps[:, t % 4, :], ot[:, b * KC + k, s:s + P], wos[:, k, :],
                                                  start=(k == 0), stop=(k == KC - 1))
                        mm.then_inc(made, 1)

                @block.vector
                def _(dve):
                    for t in range(NT):
                        dve.wait_ge(made, t + 1)
                        nc.vector.tensor_tensor(g.x[:, t, :], g.x[:, t, :], g.ps[:, t % 4, :],
                                                ALU.add).then_inc(added, 1)


def project_self(nc, g, st, wqkv, rope, qt, kt, v, wos, wo, wo_loaded, masks, mask):
    w = st.sbuf("w", [P, KC, 3 * D])
    w_loaded, made, copied = st.sem("w_loaded"), st.sem("made"), st.sem("copied")
    v_made, v_copied = st.sem("v_made"), st.sem("v_copied")
    units = [(c, b, dst, part) for part, dst in enumerate((qt, kt)) for c in range(KC) for b in range(B)]
    RAW = 3
    if rope:
        cos, sin, swap = st.sbuf("cos", [P, S]), st.sbuf("sin", [P, S]), st.sbuf("swap", [P, P])
        raw, rc, rs = st.sbuf("raw", [P, RAW, S]), st.sbuf("rc", [P, 2, S]), st.sbuf("rs", [P, 2, S])
        swapped, cos_done, sin_done, rotated = (st.sem("swapped"), st.sem("cos_done"), st.sem("sin_done"),
                                                st.sem("rotated"))
    r_loaded = st.sem("r_loaded")
    with nc.Block() as block:
        @block.sync
        def _(sp):
            for part in range(3):
                sp.dma_start(w[:, :, part * D:(part + 1) * D],
                             wqkv[:, part * D:(part + 1) * D].rearrange("(k p) n -> p k n", p=P)).then_inc(w_loaded, 16)
                if rope and part == 0:
                    sp.dma_start(cos[:, :], rope[0]).then_inc(r_loaded, 16)
                    sp.dma_start(sin[:, :], rope[1]).then_inc(r_loaded, 16)
                    sp.dma_start(swap[:, :], rope[2]).then_inc(r_loaded, 16)
            sp.dma_start(wos[:, :, :], wo.rearrange("(k p) n -> p k n", p=P)).then_inc(wo_loaded, 16)
            sp.dma_start(masks[:, :], mask).then_inc(wo_loaded, 16)
            sp.wait_ge(wo_loaded, 32)

        @block.tensor
        def _(pe):
            def swap_pairs(j):
                pe.wait_ge(copied, j + 1)
                if j == 0:
                    pe.wait_ge(r_loaded, 48)
                if j >= 2:
                    pe.wait_ge(sin_done, j - 1)
                nc.tensor.matmul(g.ps[:, 4 + j % 2, :], swap[:, :], raw[:, j % RAW, :], start=True,
                                 stop=True).then_inc(swapped, 1)

            for j, (c, b, dst, part) in enumerate(units):
                if j % 8 == 0:
                    pe.wait_ge(w_loaded, 48)
                if j >= 4:
                    pe.wait_ge(copied, j - 3)
                for k in range(KC):
                    mm = nc.tensor.matmul(g.ps[:, j % 4, :], w[:, k, part * D + c * P:part * D + (c + 1) * P],
                                          g.xt[:, k, b * S:(b + 1) * S], start=(k == 0), stop=(k == KC - 1))
                mm.then_inc(made, 1)
                if rope and j >= 1:
                    swap_pairs(j - 1)
            if rope:
                swap_pairs(len(units) - 1)
            for t in range(NT):
                if t >= 2:
                    pe.wait_ge(v_copied, t - 1)
                for k in range(KC):
                    mm = nc.tensor.matmul(g.ps[:, 6 + t % 2, :], g.xt[:, k, t * P:(t + 1) * P], w[:, k, 2 * D:3 * D],
                                          start=(k == 0), stop=(k == KC - 1))
                mm.then_inc(v_made, 1)

        @block.scalar
        def _(act):
            for j, (c, b, dst, part) in enumerate(units):
                act.wait_ge(made, j + 1)
                if rope and j >= RAW:
                    act.wait_ge(cos_done, j - RAW + 1)
                    act.wait_ge(swapped, j - RAW + 1)
                out = raw[:, j % RAW, :] if rope else dst[:, b * KC + c, :]
                nc.scalar.activation(out, g.ps[:, j % 4, :], ACT.Copy,
                                     scale=DH ** -0.5 if part == 0 else 1.0).then_inc(copied, 1)
            for t in range(NT):
                b, kb = divmod(t, S // P)
                act.wait_ge(v_made, t + 1)
                nc.scalar.activation(v[:, b * KC:(b + 1) * KC, kb, :],
                                     g.ps[:, 6 + t % 2, :].rearrange("p (c d) -> p c d", c=KC),
                                     ACT.Copy).then_inc(v_copied, 1)

        if rope:
            @block.gpsimd
            def _(pool):
                pool.wait_ge(r_loaded, 48)
                for j in range(len(units)):
                    pool.wait_ge(copied, j + 1)
                    if j >= 2:
                        pool.wait_ge(rotated, j - 1)
                    nc.gpsimd.tensor_tensor(rc[:, j % 2, :], raw[:, j % RAW, :], cos[:, :],
                                            ALU.mult).then_inc(cos_done, 1)

            @block.vector
            def _(dve):
                dve.wait_ge(r_loaded, 48)
                for j, (c, b, dst, part) in enumerate(units):
                    dve.wait_ge(swapped, j + 1)
                    nc.vector.tensor_tensor(rs[:, j % 2, :], g.ps[:, 4 + j % 2, :], sin[:, :],
                                            ALU.mult).then_inc(sin_done, 1)
                    dve.wait_ge(sin_done, j + 1)
                    dve.wait_ge(cos_done, j + 1)
                    nc.vector.tensor_tensor(dst[:, b * KC + c, :], rc[:, j % 2, :], rs[:, j % 2, :],
                                            ALU.add).then_inc(rotated, 1)


def attention_core(nc, g, st, qt, kt, v, ot, nkt, masks=None):
    causal = masks is not None
    NI, U, QB = B * KC, HPC * (S // P), S // P
    NK = nkt * P
    SB = 4 if causal else 2
    sbank = (lambda k: k % SB) if causal else (lambda k: 2 * (k % SB))
    SKEW = 5 if causal else 3
    SPLIT = 4 if causal else 6
    PR = 8 if causal else 4
    HALVES = 1 if causal else 2
    LAG = 3 if causal else 1
    KB = NK // S
    parts = st.sbuf("parts", [P, 2 + 2 * KB, S], F32R)
    packed = st.sbuf("packed", [P, HPC, 1 + KB, S], F32R)
    high = [parts[:, 0, :], parts[:, 2:2 + KB, :].rearrange("p a n -> p (a n)")]
    low = [parts[:, 1, :], parts[:, 2 + KB:2 + 2 * KB, :].rearrange("p a n -> p (a n)")]
    moves = []
    for r, (qp, kp) in enumerate(((0, 0), (1, 0), (0, 1), (1, 1))):
        if KB == 1:
            moves.append((r, slice(0, 2), slice(qp, 3 + kp, 2 + kp - qp)))
        else:
            moves.append((r, slice(0, 1), slice(qp, qp + 1)))
            moves.append((r, slice(1, 1 + KB), slice(2 + KB * kp, 2 + KB * (kp + 1))))
    PACK = 16 * len(moves)
    vm = st.sbuf("vm", [P, nkt, P])
    prob = g.xt[:, :, :].rearrange("p k (a n) -> p (k a) n", n=NK)
    pt = st.sbuf("pt", [P, 2, nkt, S])
    nmax, rsum, rinv = st.sbuf("nmax", [P, PR]), st.sbuf("rsum", [P, PR]), st.sbuf("rinv", [P, PR])
    scores = st.sem("scores")
    max_done = st.sem("max_done")
    exp_done = st.sem("exp_done")
    rinv_done = st.sem("rinv_done")
    prob_done = st.sem("prob_done")
    turned = [st.sem(f"turned{n}") for n in range(HALVES)]
    pt_done = [st.sem(f"pt_done{n}") for n in range(HALVES)]
    pv_done = st.sem("pv_done")
    ot_done = st.sem("ot_done")
    high_done = st.sem("high_done")
    low_done = st.sem("low_done")
    packed_in = [st.sem(f"packed_in{h}") for h in range(HPC)]
    vm_done = st.sem("vm_done")
    width = (lambda qb: (qb + 1) * P) if causal else (lambda qb: NK)

    def s_ps(k, n):
        return g.ps[:, sbank(k):sbank(k) + (1 if causal else 2), :].rearrange("p a n -> p (a n)")[:, 0:n]

    def t_bank(k, half):
        return 4 + k % 2 if causal else 4 + half

    with nc.Block() as block:
        @block.sync
        def _(sp):
            def pack(i, first=False):
                sp.wait_ge(low_done, 2 * i + 2)
                for h in range(HPC):
                    if not first:
                        sp.wait_ge(scores, U * (i - 1) + QB * (h + 1))
                    for r, dst, src in moves:
                        sp.dma_start(packed[r * DH:(r + 1) * DH, h, dst, :].bitcast(F32),
                                     parts[h * DH:(h + 1) * DH, src, :].bitcast(F32)).then_inc(packed_in[h], 16)

            pack(0, first=True)
            with sp.Fori(1, NI) as i:
                pack(i)

        @block.tensor
        def _(pe):
            def step(i, k, first=False, tail=False):
                u = U * i + k
                h, qb = divmod(k, QB)
                if not tail:
                    if qb == 0:
                        pe.wait_ge(packed_in[h], PACK * (i + 1))
                    if not (first and k < SB):
                        pe.wait_ge(exp_done, u - SB + 1)
                    n = width(qb)
                    for a in range(0, n, 512):
                        e = min(n, a + 512)
                        mm = nc.tensor.matmul(s_ps(k, n)[:, a:e], packed[:, h, 0, qb * P:(qb + 1) * P],
                                              packed[:, h, 1 + a // S, 0:e - a],
                                              start=True, stop=not causal)
                    if causal:
                        mm = nc.tensor.matmul(s_ps(k, n)[:, qb * P:n], g.ident[:, :], masks[:, :], start=False,
                                              stop=True)
                    mm.then_inc(scores, 1)
                kk = k - SKEW
                if first and kk < 0:
                    return
                w = u - SKEW
                if not tail or kk < U:
                    wq = kk % QB
                    pe.wait_ge(prob_done, w + 1)
                    for half in range(HALVES):
                        if causal:
                            if not (first and kk < 2):
                                pe.wait_ge(pt_done[0], w - 1)
                            tiles = range(wq + 1)
                        else:
                            if not (first and kk < 1):
                                pe.wait_ge(pt_done[half], w)
                            tiles = range(4 * half, 4 * half + 4)
                        for n, j in enumerate(tiles):
                            mm = nc.tensor.transpose(g.ps[:, t_bank(kk, half), n * P:(n + 1) * P],
                                                     prob[:, kk % PR, j * P:(j + 1) * P], g.ident[:, :])
                        mm.then_inc(turned[half], 1)
                if kk % QB == LAG and not (first and kk < QB):
                    hh = (kk // QB - 1) % HPC
                    heads = HPC * i + kk // QB
                    for half in range(HALVES):
                        pe.wait_ge(pt_done[half], w - LAG)
                    pe.wait_ge(vm_done, heads)
                    if hh == 0 and not first:
                        pe.wait_ge(ot_done, i)
                    for j in range(nkt):
                        a = j * P if causal else 0
                        mm = nc.tensor.matmul(g.ps[hh * DH:(hh + 1) * DH, 6, a:S], vm[:, j, hh * DH:(hh + 1) * DH],
                                              pt[:, hh % 2, j, a:S], start=(j == 0), stop=(j == nkt - 1))
                    mm.then_inc(pv_done, 1)

            for k in range(U):
                step(0, k, first=True)
            with pe.Fori(1, NI) as i:
                for k in range(U):
                    step(i, k)
            for k in range(U, U + SKEW + LAG + 1):
                step(NI - 1, k, tail=True)

        @block.vector
        def _(dve):
            def low_parts(i):
                for x, hi, lo in zip((qt, kt), high, low):
                    nc.vector.tensor_tensor(lo, x[:, i, :], hi, ALU.subtract).then_inc(low_done, 1)

            def step(i, k, first=False, tail=False, last=False):
                u = U * i + k
                if not tail:
                    dve.wait_ge(scores, u + 1)
                    nc.vector.tensor_reduce(nmax[:, k % PR:k % PR + 1], s_ps(k, width(k % QB)), X_AXIS, ALU.max,
                                            negate=True).then_inc(max_done, 1)
                if not (first and k < 1) and k <= U:
                    dve.wait_ge(exp_done, u)
                    s = (k - 1) % PR
                    nc.vector.reciprocal(rinv[:, s:s + 1], rsum[:, s:s + 1]).then_inc(rinv_done, 1)
                kk = k - SKEW
                if (first and kk < 0) or kk >= U:
                    return
                w = u - SKEW
                hh, wq = divmod(kk % U, QB)
                if k == SPLIT + 2 and not last:
                    dve.wait_ge(high_done, 2 * i + 4)
                dve.wait_ge(turned[0], w + 1)
                if wq == 0 and not (first and hh < 2):
                    dve.wait_ge(pv_done, HPC * i + kk // QB - 1)
                n = wq + 1 if causal else 4
                nc.vector.tensor_copy(pt[:, hh % 2, 0:n, wq * P:(wq + 1) * P],
                                      g.ps[:, t_bank(kk, 0), 0:n * P].rearrange("p (j q) -> p j q", j=n)
                                      ).then_inc(pt_done[0], 1)
                if k == SPLIT + 2 and not last:
                    low_parts(i + 1)

            dve.wait_ge(high_done, 2)
            low_parts(0)
            for k in range(U):
                step(0, k, first=True)
            with dve.Fori(1, NI - 1) as i:
                for k in range(U):
                    step(i, k)
            for k in range(U):
                step(NI - 1, k, last=True)
            for k in range(U, U + SKEW):
                step(NI - 1, k, tail=True)

        @block.scalar
        def _(act):
            def store(iters):
                act.wait_ge(pv_done, HPC * iters)
                nc.scalar.activation(ot[:, iters - 1, :], g.ps[:, 6, :], ACT.Copy).then_inc(ot_done, 1)

            def high_parts(i):
                for x, hi in zip((qt, kt), high):
                    nc.scalar.activation(hi, x[:, i, :], ACT.Copy).then_inc(high_done, 1)

            def step(i, k, first=False, tail=False, last=False):
                u = U * i + k
                if not tail:
                    if k == SPLIT and not last:
                        for h in range(HPC):
                            act.wait_ge(packed_in[h], PACK * (i + 1))
                    act.wait_ge(max_done, u + 1)
                    if not (first and k < PR):
                        for half in range(HALVES):
                            act.wait_ge(turned[half], u - PR + 1)
                    s = k % PR
                    n = width(k % QB)
                    nc.scalar.activation(prob[:, s, 0:n], s_ps(k, n), ACT.Exp, bias=nmax[:, s:s + 1],
                                         accum_out=rsum[:, s:s + 1]).then_inc(exp_done, 1)
                    if k == SPLIT and not last:
                        high_parts(i + 1)
                kk = k - SKEW
                if not causal and not (first and kk < 0) and kk < U:
                    w = u - SKEW
                    hh, wq = divmod(kk % U, QB)
                    act.wait_ge(turned[1], w + 1)
                    if wq == 0 and not (first and hh < 2):
                        act.wait_ge(pv_done, HPC * i + kk // QB - 1)
                    nc.scalar.activation(pt[:, hh % 2, 4:8, wq * P:(wq + 1) * P],
                                         g.ps[:, t_bank(kk, 1), :].rearrange("p (j q) -> p j q", j=4),
                                         ACT.Copy).then_inc(pt_done[1], 1)
                if k == SKEW + LAG + 2 and not first and not tail:
                    store(i)

            high_parts(0)
            for k in range(U):
                step(0, k, first=True)
            with act.Fori(1, NI - 1) as i:
                for k in range(U):
                    step(i, k)
            for k in range(U):
                step(NI - 1, k, last=True)
            for k in range(U, U + SKEW):
                step(NI - 1, k, tail=True)
            store(NI)

        @block.gpsimd
        def _(pool):
            def put_v(i, h):
                nc.gpsimd.tensor_copy(vm[:, :, h * DH:(h + 1) * DH], v[:, i, :, h * DH:(h + 1) * DH]).then_inc(vm_done, 1)

            def step(i, k, first=False, last=False):
                u = U * i + k
                h, qb = divmod(k, QB)
                n = width(qb)
                pool.wait_ge(rinv_done, u + 1)
                nc.gpsimd.tensor_tensor(prob[:, k % PR, 0:n], prob[:, k % PR, 0:n],
                                        rinv[:, k % PR:k % PR + 1].to_broadcast([P, n]), ALU.mult).then_inc(prob_done, 1)
                if qb == QB - 1:
                    if h < 2 and not first:
                        pool.wait_ge(pv_done, HPC * (i - 1) + h + 3)
                        put_v(i, h + 2)
                    if h >= 2 and not last:
                        pool.wait_ge(pv_done, HPC * i + h - 1)
                        put_v(i + 1, h - 2)

            for h in range(HPC):
                put_v(0, h)
            for k in range(U):
                step(0, k, first=True)
            with pool.Fori(1, NI - 1) as i:
                for k in range(U):
                    step(i, k)
            for k in range(U):
                step(NI - 1, k, last=True)


def cross_attention0(nc, g, name, ctxt, wq, bq_cols, wkvt, bk_cols, bkv, wp, bp):
    xn = g.xt[:, :, :].rearrange("p k (a d) -> p (k a) d", d=D)
    NKT = CTX // P
    with Stage(nc, name) as st:
        qt = st.sbuf("qt", [P, B * KC, S])
        kt = st.sbuf("kt", [P, B * KC, CTX])
        v = st.sbuf("v", [P, B * KC, NKT, P])
        wpt = st.sbuf("wpt", [P, KC, D], BF16)
        wp_scale = st.sbuf("wp_scale", [P, KC])
        with Stage(nc, name + "_proj") as pr:
            project_cross0(nc, g, pr, xn, ctxt, wq, bq_cols, wkvt, bk_cols, bkv, wp, qt, kt, v, wpt, wp_scale)
        ot = st.sbuf("ot", [P, B * KC, S])
        with Stage(nc, name + "_core") as co:
            attention_core(nc, g, co, qt, kt, v, ot, NKT)
        with Stage(nc, name + "_out") as ou:
            output_cross0(nc, g, ou, ot, wpt, wp_scale, bp)


def project_cross0(nc, g, st, xn, ctxt, wq, bq_cols, wkvt, bk_cols, bkv, wp, qt, kt, v, wpt, wp_scale):
    NKT = CTX // P
    NCH = B * CTX // 512
    RING = 2
    w_rows = [st.sbuf("wq_rows", [P, KC, D]), st.sbuf("wp_rows", [P, KC, D])]
    w_int = [st.sbuf("wq_int", [P, KC, D], BF16), st.sbuf("wp_int", [P, KC, D], BF16)]
    wqt = st.sbuf("wqt", [P, KC, D], BF16)
    wts = [wqt, wpt]
    wq_scale = st.sbuf("wq_scale", [P, KC])
    wkv = st.sbuf("wkv", [P, KC, 2 * D])
    ctx = st.sbuf("ctx", [P, RING, KC, 512])
    x_int = st.sbuf("x_int", [P, NT, D], BF16)
    xqt = st.sbuf("xqt", [P, KC, T], BF16)
    rounded = st.sbuf("rounded", [P, 2, D])
    top = st.sbuf("top", [P, NT + 2 * KC])
    scale = st.sbuf("scale", [P, NT + 2 * KC])
    inv = st.sbuf("inv", [P, NT + 2 * KC])
    diag = st.sbuf("diag", [P, 2, P])
    xs_row = st.sbuf("xs_row", [P, T])
    bqs, bks = st.sbuf("bqs", [P, KC]), st.sbuf("bks", [P, KC])
    bqss = st.sbuf("bqss", [P, KC])
    bv = st.sbuf("bv", [P, D])
    qs = rounded
    w_loaded = [st.sem("wq_loaded"), st.sem("wp_loaded")]
    wkv_loaded, b_loaded = st.sem("wkv_loaded"), st.sem("b_loaded")
    ctx_loaded = [st.sem(f"ctx_loaded{n}") for n in range(RING)]
    tops, scaled, inverted, shifted, clipped = (st.sem("tops"), st.sem("scaled"), st.sem("inverted"),
                                                st.sem("shifted"), st.sem("clipped"))
    ints = st.sem("ints")
    turned, turned_done = st.sem("turned"), st.sem("turned_done")
    diag_done, row_made, row_done = st.sem("diag_done"), st.sem("row_made"), st.sem("row_done")
    q_made, q_scaled, q_done, bias_done = st.sem("q_made"), st.sem("q_scaled"), st.sem("q_done"), st.sem("bias_done")
    k_made, k_done, v_made, v_done = st.sem("k_made"), st.sem("k_done"), st.sem("v_made"), st.sem("v_done")
    jobs = [(w_rows[0][:, c, :], w_int[0][:, c, :], c) for c in range(KC)]
    jobs += [(xn[:, t, :], x_int[:, t, :], KC + t) for t in range(NT)]
    jobs += [(w_rows[1][:, c, :], w_int[1][:, c, :], KC + NT + c) for c in range(KC)]
    NJ = len(jobs)
    with nc.Block() as block:
        @block.sync
        def _(sp):
            sp.dma_start(wkv[:, :, 0:D], wkvt[:, 0:D].rearrange("(k p) n -> p k n", p=P)).then_inc(wkv_loaded, 16)
            for n in range(NCH):
                if n >= RING:
                    sp.wait_ge(k_made, KC * (n - RING + 1))
                    sp.wait_ge(v_made, 4 * (n - RING + 1))
                sp.dma_start(ctx[:, n % RING, :, :],
                             ctxt[:, n * 512:(n + 1) * 512].rearrange("(k p) n -> p k n", p=P)
                             ).then_inc(ctx_loaded[n % RING], 16)
                if n == 0:
                    sp.dma_start(bks[:, :], bk_cols).then_inc(b_loaded, 16)
                    sp.dma_start(bqs[:, :], bq_cols).then_inc(b_loaded, 16)
                    sp.dma_start(bv[:, :], bkv[D:2 * D].partition_broadcast(P)).then_inc(b_loaded, 16)
                    sp.dma_start(wkv[:, :, D:2 * D],
                                 wkvt[:, D:2 * D].rearrange("(k p) n -> p k n", p=P)).then_inc(wkv_loaded, 16)
                    for n, src in enumerate((wq, wp)):
                        sp.dma_start(w_rows[n][:, :, :], src.rearrange("(c p) n -> p c n", p=P)).then_inc(w_loaded[n], 16)

        @block.vector
        def _(dve):
            def round_rows(first, n, group):
                for j in range(first, first + n):
                    nc.vector.tensor_reduce(top[:, j:j + 1], jobs[j][0], X_AXIS, ALU.max,
                                            apply_absolute_value=True).then_inc(tops, 1)
                dve.wait_ge(tops, first + n)
                nc.vector.tensor_scalar(scale[:, first:first + n], top[:, first:first + n], 1.0 / 127.0, 1e-8,
                                        ALU.mult, ALU.max).then_inc(scaled, 1)
                dve.wait_ge(scaled, group + 1)
                nc.vector.reciprocal(inv[:, first:first + n], scale[:, first:first + n]).then_inc(inverted, 1)
                dve.wait_ge(inverted, group + 1)
                for j in range(first, first + n):
                    if j >= 2:
                        dve.wait_ge(ints, j - 1)
                    nc.vector.tensor_scalar(rounded[:, j % 2, :], jobs[j][0], inv[:, j:j + 1], ROUND, ALU.mult,
                                            ALU.add).then_inc(shifted, 1)
                    dve.wait_ge(shifted, j + 1)
                    nc.vector.tensor_scalar(rounded[:, j % 2, :], rounded[:, j % 2, :], ROUND - 127.0, ROUND + 127.0,
                                            ALU.max, ALU.min).then_inc(clipped, 1)

            def values(n):
                for t in range(4):
                    m = 4 * n + t
                    b, kb = divmod(m, NKT)
                    dve.wait_ge(v_made, m + 1)
                    nc.vector.tensor_tensor(v[:, b * KC:(b + 1) * KC, kb, :],
                                            g.ps[:, 4 + m % 2, :].rearrange("p (c d) -> p c d", c=KC),
                                            bv[:, :].rearrange("p (c d) -> p c d", c=KC), ALU.add).then_inc(v_done, 1)

            dve.wait_ge(b_loaded, 48)
            nc.vector.tensor_scalar(bqss[:, :], bqs[:, :], DH ** -0.5, None, ALU.mult).then_inc(bias_done, 1)
            values(0)
            dve.wait_ge(w_loaded[0], 16)
            round_rows(0, KC, 0)
            values(1)
            round_rows(KC, NT, 1)
            values(2)
            dve.wait_ge(w_loaded[1], 16)
            round_rows(KC + NT, KC, 2)
            nc.vector.tensor_copy(wp_scale[:, :], scale[:, KC + NT:NJ]).then_inc(bias_done, 1)
            nc.vector.tensor_copy(wq_scale[:, :], scale[:, 0:KC]).then_inc(bias_done, 1)
            values(3)
            for t in range(NT):
                if t >= 2:
                    dve.wait_ge(row_made, t - 1)
                nc.vector.tensor_scalar(diag[:, t % 2, :], g.ident[:, :], scale[:, KC + t:KC + t + 1], None,
                                        ALU.mult).then_inc(diag_done, 1)
            dve.wait_ge(bias_done, 3)
            dve.wait_ge(row_done, 2)
            for j in range(2 * KC):
                c, b = divmod(j, B)
                dve.wait_ge(q_made, j + 1)
                if j >= 2:
                    dve.wait_ge(q_done, j - 1)
                nc.vector.scalar_tensor_tensor(qs[:, j % 2, :], g.ps[:, j % 4, :], wq_scale[:, c:c + 1],
                                               xs_row[:, b * S:(b + 1) * S], ALU.mult, ALU.mult).then_inc(q_scaled, 1)

        @block.scalar
        def _(act):
            def keys(n):
                b, half = divmod(n, CTX // 512)
                for c in range(KC):
                    m = KC * n + c
                    act.wait_ge(k_made, m + 1)
                    nc.scalar.activation(kt[:, b * KC + c, half * 512:(half + 1) * 512], g.ps[:, m % 4, :], ACT.Identity,
                                         bias=bks[:, c:c + 1]).then_inc(k_done, 1)

            def whole(first, n):
                for j in range(first, first + n):
                    act.wait_ge(clipped, j + 1)
                    nc.scalar.activation(jobs[j][1], rounded[:, j % 2, :], ACT.Copy, bias=-ROUND).then_inc(ints, 1)

            def turn(n, dst):
                act.wait_ge(turned, n + 1)
                nc.scalar.activation(dst, g.ps[:, 6 + n % 2, 0:256].bitcast(BF16).rearrange("p (k c) -> p k c", k=KC),
                                     ACT.Copy).then_inc(turned_done, 1)

            act.wait_ge(b_loaded, 48)
            keys(0)
            whole(0, KC)
            keys(1)
            whole(KC, NT)
            keys(2)
            whole(KC + NT, KC)
            keys(3)
            for n, c in enumerate(range(KC)):
                turn(n, wqt[:, :, c * P:(c + 1) * P])
            for t in range(NT):
                turn(KC + t, xqt[:, :, t * P:(t + 1) * P])
            for c in range(KC):
                turn(KC + NT + c, wpt[:, :, c * P:(c + 1) * P])
            for n in range(2):
                act.wait_ge(row_made, 4 * (n + 1))
                nc.scalar.activation(xs_row[:, n * 512:(n + 1) * 512], g.ps[:, 4 + n, :], ACT.Copy).then_inc(row_done, 1)
            act.wait_ge(bias_done, 1)
            for j in range(2 * KC):
                c, b = divmod(j, B)
                act.wait_ge(q_scaled, j + 1)
                nc.scalar.activation(qt[:, b * KC + c, :], qs[:, j % 2, :], ACT.Identity, bias=bqss[:, c:c + 1],
                                     scale=DH ** -0.5).then_inc(q_done, 1)

        @block.tensor
        def _(pe):
            for n in range(NCH):
                pe.wait_ge(ctx_loaded[n % RING], 16 * (n // RING + 1))
                pe.wait_ge(wkv_loaded, 32)
                for c in range(KC):
                    m = KC * n + c
                    if m >= 4:
                        pe.wait_ge(k_done, m - 3)
                    for k in range(KC):
                        mm = nc.tensor.matmul(g.ps[:, m % 4, :], wkv[:, k, c * P:(c + 1) * P], ctx[:, n % RING, k, :],
                                              start=(k == 0), stop=(k == KC - 1))
                    mm.then_inc(k_made, 1)
                for t in range(4):
                    m = 4 * n + t
                    if m >= 2:
                        pe.wait_ge(v_done, m - 1)
                    for k in range(KC):
                        mm = nc.tensor.matmul(g.ps[:, 4 + m % 2, :], ctx[:, n % RING, k, t * P:(t + 1) * P],
                                              wkv[:, k, D:2 * D], start=(k == 0), stop=(k == KC - 1))
                    mm.then_inc(v_made, 1)
            for n, (_, whole, _) in enumerate(jobs):
                pe.wait_ge(ints, n + 1)
                if n >= 2:
                    pe.wait_ge(turned_done, n - 1)
                for k in range(KC):
                    mm = nc.tensor.transpose(g.ps[:, 6 + n % 2, 0:256].bitcast(BF16)[:, k * P:(k + 1) * P],
                                             whole[:, k * P:(k + 1) * P], g.ident16[:, :])
                mm.then_inc(turned, 1)
            for t in range(NT):
                pe.wait_ge(diag_done, t + 1)
                if t == 0:
                    pe.wait_ge(v_done, B * NKT)
                nc.tensor.matmul(g.ps[:, 4 + t // 4, t % 4 * P:(t % 4 + 1) * P], g.ones[:, :], diag[:, t % 2, :],
                                 start=True, stop=True).then_inc(row_made, 1)
            pe.wait_ge(turned_done, NJ)
            pe.wait_ge(k_done, KC * NCH)
            for j in range(2 * KC):
                c, b = divmod(j, B)
                if j >= 4:
                    pe.wait_ge(q_scaled, j - 3)
                for k in range(KC):
                    mm = nc.tensor.matmul(g.ps[:, j % 4, :], wqt[:, k, c * P:(c + 1) * P],
                                          xqt[:, k, b * S:(b + 1) * S], start=(k == 0), stop=(k == KC - 1))
                mm.then_inc(q_made, 1)


def output_cross0(nc, g, st, ot, wpt, wp_scale, bp):
    o_int = st.sbuf("o_int", [P, NT, D], BF16)
    oqt = st.sbuf("oqt", [P, NT, KC, P], BF16)
    rounded = st.sbuf("rounded", [P, NT, D])
    top, scale, inv = st.sbuf("top", [P, NT]), st.sbuf("scale", [P, NT]), st.sbuf("inv", [P, NT])
    diag = st.sbuf("diag", [P, KC, P])
    ws_row, bps = st.sbuf("ws_row", [P, D]), st.sbuf("bps", [P, D])
    y = st.sbuf("y", [P, 2, D])
    b_loaded, diag_done, row_made, row_done = st.sem("b_loaded"), st.sem("diag_done"), st.sem("row_made"), st.sem("row_done")
    rows, tops, scaled, inverted = st.sem("rows"), st.sem("tops"), st.sem("scaled"), st.sem("inverted")
    shifted, clipped, ints = st.sem("shifted"), st.sem("clipped"), st.sem("ints")
    turned, turned_done, made, y_done, added = (st.sem("turned"), st.sem("turned_done"), st.sem("made"),
                                                st.sem("y_done"), st.sem("added"))
    biased = st.sem("biased")
    with nc.Block() as block:
        @block.sync
        def _(sp):
            sp.dma_start(bps[:, :], bp.partition_broadcast(P)).then_inc(b_loaded, 16)

        @block.gpsimd
        def _(pool):
            pool.wait_ge(b_loaded, 16)
            for t in range(NT):
                nc.gpsimd.tensor_tensor(g.x[:, t, :], g.x[:, t, :], bps[:, :], ALU.add).then_inc(biased, 1)

        def project(pe, t):
            pe.wait_ge(turned_done, t + 1)
            if t >= 2:
                pe.wait_ge(y_done, t - 1)
            for k in range(KC):
                mm = nc.tensor.matmul(g.ps[:, 2 + t % 2, :], oqt[:, t, k, :], wpt[:, k, :], start=(k == 0),
                                      stop=(k == KC - 1))
            mm.then_inc(made, 1)

        @block.tensor
        def _(pe):
            for c in range(KC):
                pe.wait_ge(diag_done, c + 1)
                mm = nc.tensor.matmul(g.ps[:, 7, c * P:(c + 1) * P], g.ones[:, :], diag[:, c, :], start=True, stop=True)
            mm.then_inc(row_made, 1)
            pe.wait_ge(row_done, 1)
            for t in range(NT):
                b, s = divmod(t * P, S)
                for k in range(KC):
                    mm = nc.tensor.transpose(g.ps[:, t, k * P:(k + 1) * P], ot[:, b * KC + k, s:s + P], g.ident[:, :])
                mm.then_inc(rows, 1)
            for t in range(NT):
                pe.wait_ge(ints, t + 1)
                if t == 0:
                    pe.wait_ge(clipped, 4)
                if t >= 2:
                    pe.wait_ge(turned_done, t - 1)
                for k in range(KC):
                    mm = nc.tensor.transpose(g.ps[:, t % 2, 0:256].bitcast(BF16)[:, k * P:(k + 1) * P],
                                             o_int[:, t, k * P:(k + 1) * P], g.ident16[:, :])
                mm.then_inc(turned, 1)
                if t >= 1:
                    project(pe, t - 1)
            project(pe, NT - 1)

        @block.vector
        def _(dve):
            for c in range(KC):
                nc.vector.tensor_scalar(diag[:, c, :], g.ident[:, :], wp_scale[:, c:c + 1], None,
                                        ALU.mult).then_inc(diag_done, 1)
            for t in range(NT):
                dve.wait_ge(rows, t + 1)
                nc.vector.tensor_reduce(top[:, t:t + 1], g.ps[:, t, :], X_AXIS, ALU.max,
                                        apply_absolute_value=True).then_inc(tops, 1)
            dve.wait_ge(tops, NT)
            nc.vector.tensor_scalar(scale[:, :], top[:, :], 1.0 / 127.0, 1e-8, ALU.mult, ALU.max).then_inc(scaled, 1)
            dve.wait_ge(scaled, 1)
            nc.vector.reciprocal(inv[:, :], scale[:, :]).then_inc(inverted, 1)
            dve.wait_ge(inverted, 1)
            for t in range(NT):
                nc.vector.tensor_scalar(rounded[:, t, :], g.ps[:, t, :], inv[:, t:t + 1], ROUND, ALU.mult,
                                        ALU.add).then_inc(shifted, 1)
                dve.wait_ge(shifted, t + 1)
                nc.vector.tensor_scalar(rounded[:, t, :], rounded[:, t, :], ROUND - 127.0, ROUND + 127.0, ALU.max,
                                        ALU.min).then_inc(clipped, 1)
            for t in range(NT):
                dve.wait_ge(made, t + 1)
                if t == 0:
                    dve.wait_ge(row_done, 1)
                nc.vector.scalar_tensor_tensor(y[:, t % 2, :], g.ps[:, 2 + t % 2, :], scale[:, t:t + 1], ws_row[:, :],
                                               ALU.mult, ALU.mult).then_inc(y_done, 1)
                dve.wait_ge(y_done, t + 1)
                dve.wait_ge(biased, t + 1)
                nc.vector.tensor_tensor(g.x[:, t, :], g.x[:, t, :], y[:, t % 2, :], ALU.add).then_inc(added, 1)

        def put(act, t):
            act.wait_ge(turned, t + 1)
            nc.scalar.activation(oqt[:, t, :, :],
                                 g.ps[:, t % 2, 0:256].bitcast(BF16).rearrange("p (k c) -> p k c", k=KC),
                                 ACT.Copy).then_inc(turned_done, 1)

        @block.scalar
        def _(act):
            act.wait_ge(row_made, 1)
            nc.scalar.activation(ws_row[:, :], g.ps[:, 7, :], ACT.Copy).then_inc(row_done, 1)
            for t in range(NT):
                act.wait_ge(clipped, t + 1)
                nc.scalar.activation(o_int[:, t, :], rounded[:, t, :], ACT.Copy, bias=-ROUND).then_inc(ints, 1)
                if t >= 1:
                    put(act, t - 1)
            put(act, NT - 1)



def router(nc, g, st, name, wr, bias, experts, top_k, gates, iota_e, pick, best):
    w = st.sbuf("w", [P, KC, experts])
    bs = st.sbuf("bs", [P, experts])
    logit = st.sbuf("logit", [P, NT, experts])
    top = st.sbuf("top", [P, NT])
    total, inv = st.sbuf("total", [P, NT]), st.sbuf("inv", [P, NT])
    at, atf = st.sbuf("at", [P, NT, 8], U32), st.sbuf("atf", [P, NT, 8])
    ksum, kinv = st.sbuf("ksum", [P, NT]), st.sbuf("kinv", [P, NT])
    part = st.sbuf("part", [P, NT, experts])
    iota = st.sbuf("iota", [P, experts])
    loaded, made, exped, step = st.sem("loaded"), st.sem("made"), st.sem("exped"), st.sem("step")
    shape = [P, NT, experts]

    def over(a):
        return a.rearrange("p (t o) -> p t o", o=1).to_broadcast(shape)

    with nc.Block() as block:
        @block.sync
        def _(sp):
            sp.dma_start(w[:, :, :], wr.rearrange("(k p) e -> p k e", p=P)).then_inc(loaded, 16)
            sp.dma_start(iota[:, :], iota_e[0:experts].partition_broadcast(P)).then_inc(loaded, 16)
            if bias is not None:
                sp.dma_start(bs[:, :], bias.partition_broadcast(P)).then_inc(loaded, 16)

        @block.tensor
        def _(pe):
            pe.wait_ge(loaded, 32 if bias is None else 48)
            for t in range(NT):
                for k in range(KC):
                    mm = nc.tensor.matmul(g.ps[:, 0, t * experts:(t + 1) * experts], g.xt[:, k, t * P:(t + 1) * P],
                                          w[:, k, :], start=(k == 0), stop=(k == KC - 1))
            mm.then_inc(made, 1)

        @block.scalar
        def _(act):
            act.wait_ge(step, 3)
            nc.scalar.activation(logit[:, :, :], logit[:, :, :], ACT.Exp).then_inc(exped, 1)

        @block.vector
        def _(dve):
            done = [0]

            def then(ins):
                ins.then_inc(step, 1)
                done[0] += 1
                dve.wait_ge(step, done[0])

            raw = g.ps[:, 0, 0:NT * experts].rearrange("p (t e) -> p t e", t=NT)
            dve.wait_ge(made, 1)
            if bias is None:
                then(nc.vector.tensor_copy(logit[:, :, :], raw))
            else:
                dve.wait_ge(loaded, 48)
                then(nc.vector.tensor_tensor(logit[:, :, :], raw,
                                             bs[:, :].rearrange("p (o e) -> p o e", o=1).to_broadcast(shape), ALU.add))
            then(nc.vector.tensor_reduce(top[:, :], logit[:, :, :], X_AXIS, ALU.max))
            then(nc.vector.tensor_tensor(logit[:, :, :], logit[:, :, :], over(top[:, :]), ALU.subtract))
            dve.wait_ge(exped, 1)
            then(nc.vector.tensor_reduce(total[:, :], logit[:, :, :], X_AXIS, ALU.add))
            then(nc.vector.reciprocal(inv[:, :], total[:, :]))
            then(nc.vector.tensor_tensor(logit[:, :, :], logit[:, :, :], over(inv[:, :]), ALU.mult))
            for t in range(NT):
                then(nc.vector.max(best[:, t, :], logit[:, t, :]))
                then(nc.vector.max_index(at[:, t, :], best[:, t, :], logit[:, t, :]))
            then(nc.vector.tensor_copy(atf[:, :, :], at[:, :, :]))
            then(nc.vector.tensor_reduce(ksum[:, :], best[:, :, 0:top_k], X_AXIS, ALU.add))
            then(nc.vector.tensor_scalar(ksum[:, :], ksum[:, :], TOPK_EPS, None, ALU.add))
            then(nc.vector.reciprocal(kinv[:, :], ksum[:, :]))
            then(nc.vector.tensor_tensor(best[:, :, :], best[:, :, :],
                                         kinv[:, :].rearrange("p (t o) -> p t o", o=1).to_broadcast([P, NT, 8]), ALU.mult))
            for k in range(top_k):
                then(nc.vector.tensor_tensor(pick[:, k], iota[:, :].rearrange("p (o e) -> p o e", o=1).to_broadcast(shape),
                                             atf[:, :, k:k + 1].to_broadcast(shape), ALU.is_equal))
                then(nc.vector.tensor_tensor(gates if k == 0 else part[:, :, :], pick[:, k],
                                             best[:, :, k:k + 1].to_broadcast(shape), ALU.mult))
                if k:
                    then(nc.vector.tensor_tensor(gates, gates, part[:, :, :], ALU.add))


def experts_all_tokens(nc, g, st, w1, w2, experts, gates, gated, b1_rows=None, b2_rows=None, pool_work=None):
    NF = len(FCH)
    HU = 2 * NF
    W1 = 2 * F if gated else F
    w1s = [st.sbuf(f"w1_{n}", [P, KC, W1]) for n in range(2)]
    w2s = [st.sbuf(f"w2_{n}", [P, NF, D]) for n in range(2)]
    ht = [st.sbuf(f"ht{n}", [P, NF, T]) for n in range(2)]
    silu = st.sbuf("silu", [P, 2, 512]) if gated else None
    w1_loaded = [st.sem(f"w1_loaded{n}") for n in range(2)]
    w2_loaded = [st.sem(f"w2_loaded{n}") for n in range(2)]
    h_made = st.sem("h_made")
    h_done = st.sem("h_done")
    silu_done = st.sem("silu_done")
    y_made = st.sem("y_made")
    y_added = st.sem("y_added")
    b_loaded, b_turned, b_done, bias_made, bias_added = (st.sem("b_loaded"), st.sem("b_turned"), st.sem("b_done"),
                                                         st.sem("bias_made"), st.sem("bias_added"))
    if not gated:
        b1 = st.sbuf("b1", [P, 2, NF])
        b1_put = st.sem("b1_put")
        b1r, b1t = st.sbuf("b1r", [experts, F]), st.sbuf("b1t", [P, NF, experts])
        b2r = st.sbuf("b2r", [experts, D])
        gt = st.sbuf("gt", [experts, T])
    bank = lambda u, half: (2 * (u % 2) + half) if gated else u % 4
    with nc.Block() as block:
        @block.sync
        def _(sp):
            def load(e, slot, first=False):
                if not first:
                    sp.wait_ge(h_made, HU * (e - 1))
                sp.dma_start(w1s[slot][:, :, :], w1[e].rearrange("(k p) f -> p k f", p=P)).then_inc(w1_loaded[slot], 16)
                if not first:
                    sp.wait_ge(y_made, NT * (e - 1))
                sp.dma_start(w2s[slot][:, 0:2, :], w2[e, 0:256, :].rearrange("(c p) n -> p c n", p=P)
                             ).then_inc(w2_loaded[slot], 16)
                sp.dma_start(w2s[slot][0:FCH[2][1], 2, :], w2[e, 256:F, :]).then_inc(w2_loaded[slot], 16)

            load(0, 0, first=True)
            if not gated:
                sp.dma_start(b1r[:, :], b1_rows).then_inc(b_loaded, 16)
                sp.dma_start(b2r[:, :], b2_rows).then_inc(b_loaded, 16)
            load(1, 1, first=True)
            if experts > 2:
                with sp.Fori(1, experts // 2) as i:
                    load(2 * i, 0)
                    load(2 * i + 1, 1)

        if pool_work is not None:
            @block.gpsimd
            def _(pool):
                pool_work(pool)

        @block.tensor
        def _(pe):
            def expert(i, slot, first=False):
                e = 2 * i + slot
                pe.wait_ge(w1_loaded[slot], 16 * i + 16)
                for u in range(HU):
                    half, f = divmod(u, NF)
                    f0, fn = FCH[f]
                    free = 2 if gated else 4
                    if not (first and slot == 0 and u < free):
                        pe.wait_ge(h_done, HU * e + u - free + 1)
                    for part in range(2 if gated else 1):
                        for k in range(KC):
                            mm = nc.tensor.matmul(g.ps[0:fn, bank(u, part), :],
                                                  w1s[slot][:, k, part * F + f0:part * F + f0 + fn],
                                                  g.xt[:, k, half * 512:(half + 1) * 512], start=(k == 0),
                                                  stop=(k == KC - 1))
                    mm.then_inc(h_made, 1)
                pe.wait_ge(w2_loaded[slot], 32 * i + 32)
                for t in range(NT):
                    if t % 4 == 0:
                        pe.wait_ge(h_done, HU * e + NF * (t // 4 + 1))
                    if not (first and slot == 0 and t < 4):
                        pe.wait_ge(y_added, NT * e + t - 3)
                    for f, (f0, fn) in enumerate(FCH):
                        mm = nc.tensor.matmul(g.ps[:, 4 + t % 4, :], ht[slot][0:fn, f, t * P:(t + 1) * P],
                                              w2s[slot][0:fn, f, :], start=(f == 0), stop=(f == NF - 1))
                    mm.then_inc(y_made, 1)

            if not gated:
                pe.wait_ge(b_loaded, 32)
                for f, (f0, fn) in enumerate(FCH):
                    mm = nc.tensor.transpose(g.ps[0:fn, 0, f * experts:(f + 1) * experts], b1r[:, f0:f0 + fn],
                                             g.ident[0:experts, 0:experts])
                for t in range(NT):
                    mm = nc.tensor.transpose(g.ps[0:experts, 1 + t // 4, t % 4 * P:(t % 4 + 1) * P], gates[:, t, :],
                                             g.ident[:, :])
                mm.then_inc(b_turned, 1)
                pe.wait_ge(b_done, 3)
                for t in range(NT):
                    if t >= 4:
                        pe.wait_ge(bias_added, t - 3)
                    nc.tensor.matmul(g.ps[:, 4 + t % 4, :], gt[:, t * P:(t + 1) * P], b2r[:, :], start=True,
                                     stop=True).then_inc(bias_made, 1)
                pe.wait_ge(bias_added, NT)
            expert(0, 0, first=True)
            expert(0, 1, first=True)
            if experts > 2:
                with pe.Fori(1, experts // 2) as i:
                    expert(i, 0)
                    expert(i, 1)

        @block.scalar
        def _(act):
            if not gated:
                act.wait_ge(b_turned, 1)
                for f, (f0, fn) in enumerate(FCH):
                    if f != 1:
                        a, n = (0, 2) if f == 0 else (2, 1)
                        nc.scalar.activation(b1t[0:fn, a:a + n, :],
                                             g.ps[0:fn, 0, a * experts:(a + n) * experts].rearrange(
                                                 "p (f e) -> p f e", f=n), ACT.Copy).then_inc(b_done, 1)
                nc.scalar.activation(gt[:, :], g.ps[0:experts, 1:3, :].rearrange("p a n -> p (a n)"),
                                     ACT.Copy).then_inc(b_done, 1)

            def expert(i, slot, first=False):
                e = 2 * i + slot
                if not gated:
                    for rows, lo, hi in ((P, 0, NF - 1), (FCH[-1][1], NF - 1, NF)):
                        nc.scalar.activation(b1[0:rows, slot, lo:hi],
                                             b1t[0:rows, lo:hi, bass.ds(e, 1)].rearrange("p f o -> p (f o)"),
                                             ACT.Copy).then_inc(b1_put, 1)
                    act.wait_ge(b1_put, 2 * e + 2)
                for u in range(HU):
                    half, f = divmod(u, NF)
                    f0, fn = FCH[f]
                    act.wait_ge(h_made, HU * e + u + 1)
                    if gated:
                        if not (first and slot == 0 and u < 2):
                            act.wait_ge(h_done, HU * e + u - 1)
                        nc.scalar.activation(silu[0:fn, u % 2, :], g.ps[0:fn, bank(u, 0), :], ACT.Silu).then_inc(silu_done, 1)
                    else:
                        if u == 0 and not first:
                            act.wait_ge(y_made, NT * (e - 1))
                        nc.scalar.activation(ht[slot][0:fn, f, half * 512:(half + 1) * 512], g.ps[0:fn, bank(u, 0), :],
                                             ACT.Relu, bias=b1[0:fn, slot, f:f + 1]).then_inc(h_done, 1)

            if not gated:
                act.wait_ge(b_done, 3)
            expert(0, 0, first=True)
            expert(0, 1, first=True)
            if experts > 2:
                with act.Fori(1, experts // 2) as i:
                    expert(i, 0)
                    expert(i, 1)

        @block.vector
        def _(dve):
            def expert(i, slot, first=False):
                e = 2 * i + slot
                if gated:
                    for u in range(HU):
                        half, f = divmod(u, NF)
                        f0, fn = FCH[f]
                        dve.wait_ge(silu_done, HU * e + u + 1)
                        if u == 0 and not first:
                            dve.wait_ge(y_made, NT * (e - 1))
                        nc.vector.tensor_tensor(ht[slot][0:fn, f, half * 512:(half + 1) * 512], g.ps[0:fn, bank(u, 1), :],
                                                silu[0:fn, u % 2, :], ALU.mult).then_inc(h_done, 1)
                for t in range(NT):
                    dve.wait_ge(y_made, NT * e + t + 1)
                    if not (first and slot == 0):
                        dve.wait_ge(y_added, NT * e + t - NT + 1)
                    nc.vector.scalar_tensor_tensor(g.x[:, t, :], g.ps[:, 4 + t % 4, :], gates[:, t, bass.ds(e, 1)],
                                                   g.x[:, t, :], ALU.mult, ALU.add).then_inc(y_added, 1)

            if not gated:
                for t in range(NT):
                    dve.wait_ge(bias_made, t + 1)
                    nc.vector.tensor_tensor(g.x[:, t, :], g.x[:, t, :], g.ps[:, 4 + t % 4, :],
                                            ALU.add).then_inc(bias_added, 1)
                dve.wait_ge(bias_added, NT)
            expert(0, 0, first=True)
            expert(0, 1, first=True)
            if experts > 2:
                with dve.Fori(1, experts // 2) as i:
                    expert(i, 0)
                    expert(i, 1)


def blocks_bound(experts, top_k):
    most = (T * top_k + experts * (P - 1)) // P
    return -(-most // 4) * 4


def place_tokens(nc, g, st, a, experts, top_k, pick, places, block_row, blocks, zeros_stored, table):
    mine = st.sbuf("mine", [P, NT, experts])
    earlier = st.sbuf("earlier", [P, P])
    iota = st.sbuf("iota", [P, P])
    limits = st.sbuf("limits", [P, NT])
    above = st.sbuf("above", [P, experts, NT])
    counts = st.sbuf("counts", [P, experts])
    need = st.sbuf("need", [P, experts])
    ends = [st.sbuf(f"ends{n}", [P, experts]) for n in range(2)]
    begin = st.sbuf("begin", [P, experts])
    base = st.sbuf("base", [P, NT, experts])
    spread = st.sbuf("spread", [P, top_k, NT * experts])
    place = st.sbuf("place", [P, top_k * NT])
    past = st.sbuf("past", [1, blocks, experts])
    row = st.sbuf("row", [1, blocks])
    zeros = st.sbuf("zeros", [P, blocks])
    loaded, step, ranked, zeroed = st.sem("loaded"), st.sem("step"), st.sem("ranked"), st.sem("zeroed")
    with nc.Block() as block:
        @block.sync
        def _(sp):
            sp.dma_start(earlier[:, :], a["earlier"]).then_inc(loaded, 16)
            sp.dma_start(iota[:, :], a["iota"].partition_broadcast(P)).then_inc(loaded, 16)
            sp.wait_ge(zeroed, 1)
            sp.dma_start(table.rearrange("(p n) o -> p (n o)", p=P), zeros[:, :]).then_inc(zeros_stored, 16)

        @block.gpsimd
        def _(pool):
            nc.gpsimd.memset(zeros[:, :], 0.0).then_inc(zeroed, 1)

        @block.tensor
        def _(pe):
            pe.wait_ge(loaded, 32)
            pe.wait_ge(step, 1)
            for t in range(NT):
                for j in range(t + 1):
                    nc.tensor.matmul(g.ps[:, 1, t * experts:(t + 1) * experts],
                                     earlier[:, :] if j == t else g.ones[:, :], mine[:, j, :], start=(j == 0),
                                     stop=(j == t))
            for j in range(NT):
                mm = nc.tensor.matmul(g.ps[:, 2, 0:experts], g.ones[:, :], mine[:, j, :], start=(j == 0),
                                      stop=(j == NT - 1))
            mm.then_inc(ranked, 1)

        @block.vector
        def _(dve):
            done = [0]

            def then(ins):
                ins.then_inc(step, 1)
                done[0] += 1
                dve.wait_ge(step, done[0])

            then(nc.vector.tensor_reduce(mine[:, :, :], pick.rearrange("p k t e -> p t e k"), X_AXIS, ALU.add))
            dve.wait_ge(loaded, 32)
            then(nc.vector.tensor_scalar(limits[:, :], iota[:, 0:NT], float(P), None, ALU.mult))
            dve.wait_ge(ranked, 1)
            then(nc.vector.tensor_copy(counts[:, :], g.ps[:, 2, 0:experts]))
            then(nc.vector.tensor_tensor(above[:, :, :],
                                         counts[:, :].rearrange("p (e o) -> p e o", o=1).to_broadcast([P, experts, NT]),
                                         limits[:, :].rearrange("p (o n) -> p o n", o=1).to_broadcast([P, experts, NT]),
                                         ALU.is_gt))
            then(nc.vector.tensor_reduce(need[:, :], above[:, :, :], X_AXIS, ALU.add))
            then(nc.vector.tensor_copy(ends[0][:, :], need[:, :]))
            w, n = 1, 0
            while w < experts:
                then(nc.vector.tensor_copy(ends[1 - n][:, 0:w], ends[n][:, 0:w]))
                then(nc.vector.tensor_tensor(ends[1 - n][:, w:experts], ends[n][:, w:experts], ends[n][:, 0:experts - w],
                                             ALU.add))
                w, n = 2 * w, 1 - n
            end = ends[n]
            then(nc.vector.tensor_tensor(begin[:, :], end[:, :], need[:, :], ALU.subtract))
            then(nc.vector.tensor_scalar(begin[:, :], begin[:, :], float(P), None, ALU.mult))
            then(nc.vector.tensor_tensor(base[:, :, :],
                                         g.ps[:, 1, 0:NT * experts].rearrange("p (t e) -> p t e", t=NT),
                                         begin[:, :].rearrange("p (o e) -> p o e", o=1).to_broadcast([P, NT, experts]),
                                         ALU.add))
            then(nc.vector.tensor_tensor(spread[:, :, :], pick.rearrange("p k t e -> p k (t e)"),
                                         base[:, :, :].rearrange("p (o t) e -> p o (t e)", o=1).to_broadcast(
                                             [P, top_k, NT * experts]), ALU.mult))
            then(nc.vector.tensor_reduce(place[:, :], spread[:, :, :].rearrange("p k (t e) -> p (k t) e", t=NT), X_AXIS,
                                         ALU.add))
            then(nc.vector.tensor_copy(places[:, :], place[:, :]))
            then(nc.vector.tensor_tensor(past[:, :, :],
                                         iota[0:1, 0:blocks].rearrange("p (b o) -> p b o", o=1).to_broadcast(
                                             [1, blocks, experts]),
                                         end[0:1, :].rearrange("p (o e) -> p o e", o=1).to_broadcast(
                                             [1, blocks, experts]), ALU.is_ge))
            then(nc.vector.tensor_reduce(row[:, :], past[:, :, :], X_AXIS, ALU.add))
            then(nc.vector.tensor_scalar(row[:, :], row[:, :], float(experts - 1), None, ALU.min))
            then(nc.vector.tensor_copy(block_row[:, :], row[:, :]))


def place_tokens_back(nc, g, st, table, blocks, scattered, top_k, index):
    rows = st.sbuf("rows", [blocks, P])
    loaded, turned, done = st.sem("loaded"), st.sem("turned"), st.sem("done")
    with nc.Block() as block:
        @block.sync
        def _(sp):
            sp.wait_ge(scattered, 16 * top_k * NT)
            sp.dma_start(rows[:, :], table.rearrange("(n p) o -> n (p o)", p=P)).then_inc(loaded, 16)

        @block.tensor
        def _(pe):
            pe.wait_ge(loaded, 16)
            nc.tensor.transpose(g.ps[:, 0, 0:blocks], rows[:, :], g.ident[0:blocks, 0:blocks]).then_inc(turned, 1)

        @block.vector
        def _(dve):
            dve.wait_ge(turned, 1)
            nc.vector.tensor_copy(index[:, :], g.ps[:, 0, 0:blocks]).then_inc(done, 1)
            dve.wait_ge(done, 1)


def experts_by_block(nc, g, st, w1, w2, b1_cols, gated, blocks, block_row, index, rows_dram, y_dram):
    NF = len(FCH)
    W1 = 2 * F if gated else F
    R = 4
    NR = blocks // R
    NH = 2 * 2 if gated else 0
    w1s = [st.sbuf(f"w1_{n}", [P, KC, W1]) for n in range(R)]
    w2s = [st.sbuf(f"w2_{n}", [P, NF, D]) for n in range(R)]
    b1s = st.sbuf("b1s", [P, R, NF])
    idx = st.sbuf("idx", [P, R], U32)
    xg = st.sbuf("xg", [P, R, D])
    xgt = st.sbuf("xgt", [P, 2, KC, P])
    ht = st.sbuf("ht", [P, 2, NF, P])
    silu = st.sbuf("silu", [P, 2, NF, P]) if gated else None
    y = st.sbuf("y", [P, R, D])
    LOADS = 3 if gated else 4
    HD = 2 if gated else NF
    w_loaded = [st.sem(f"w_loaded{n}") for n in range(R)]
    xg_loaded = [st.sem(f"xg_loaded{n}") for n in range(R)]
    y_stored = [st.sem(f"y_stored{n}") for n in range(R)]
    idx_put = st.sem("idx_put")
    x_turned = st.sem("x_turned")
    xt_done = st.sem("xt_done")
    h_made = st.sem("h_made")
    silu_done = st.sem("silu_done")
    h_done = st.sem("h_done")
    y_made = st.sem("y_made")
    y_done = st.sem("y_done")
    FULL = [(P, 0, NF - 1), (FCH[-1][1], NF - 1, NF)]

    def rings(eng, step, before=None, after=None):
        for s in range(R):
            step(0, s, first=True)
        with eng.Fori(1, NR - 1) as i:
            for s in range(R):
                step(i, s)
        for s in range(R):
            step(NR - 1, s, last=(s == R - 1))

    with nc.Block() as block:
        @block.sync
        def _(sp):
            def step(i, s, first=False, last=False):
                j = R * i + s
                if not first:
                    sp.wait_ge(y_made, j - R + 1)
                e = sp.value_load(block_row[0:1, bass.ds(j, 1)], min_val=0, max_val=w1.shape[0] - 1)
                sp.dma_start(w1s[s][:, :, :], w1[e, :, :].rearrange("(k p) f -> p k f", p=P)).then_inc(w_loaded[s], 16)
                sp.dma_start(w2s[s][:, 0:2, :], w2[e, 0:256, :].rearrange("(c p) n -> p c n", p=P)).then_inc(w_loaded[s], 16)
                sp.dma_start(w2s[s][0:FCH[2][1], 2, :], w2[e, 256:F, :]).then_inc(w_loaded[s], 16)
                if not gated:
                    sp.dma_start(b1s[:, s, :], b1_cols[e, :, :]).then_inc(w_loaded[s], 16)

            rings(sp, step)

        @block.gpsimd
        def _(pool):
            def put(i, s):
                nc.gpsimd.tensor_copy(idx[:, s:s + 1], index[:, bass.ds(R * i + s, 1)]).then_inc(idx_put, 1)

            def step(i, s, first=False, last=False):
                j = R * i + s
                if not first or s == R - 1:
                    pool.wait_ge(x_turned, j - R + 2)
                pool.wait_ge(idx_put, j + 1)
                if s < R - 1:
                    put(i, s + 1)
                elif not last:
                    put(i + 1, 0)
                nc.gpsimd.indirect_dma_start(xg[:, s, :], None, rows_dram[:, :],
                                             bass.IndirectOffsetOnAxis(ap=idx[:, s:s + 1], axis=0)).then_inc(xg_loaded[s], 16)

            put(0, 0)
            rings(pool, step)

        @block.tensor
        def _(pe):
            def turn(i, s, free):
                j = R * i + s
                pe.wait_ge(xg_loaded[s], 16 * i + 16)
                if free:
                    pe.wait_ge(xt_done, j - 1)
                for k in range(KC):
                    mm = nc.tensor.transpose(g.ps[:, s % 2, k * P:(k + 1) * P], xg[:, s, k * P:(k + 1) * P], g.ident[:, :])
                mm.then_inc(x_turned, 1)

            def outputs(i, s, free):
                j = R * i + s
                pe.wait_ge(h_done, HD * j + HD)
                if free:
                    pe.wait_ge(y_done, j - 1)
                for f, (f0, fn) in enumerate(FCH):
                    mm = nc.tensor.matmul(g.ps[:, 6 + s % 2, :], ht[0:fn, s % 2, f, :], w2s[s][0:fn, f, :], start=(f == 0),
                                          stop=(f == NF - 1))
                mm.then_inc(y_made, 1)

            def step(i, s, first=False, last=False):
                j = R * i + s
                if not last:
                    if s < R - 1:
                        turn(i, s + 1, not (first and s < 1))
                    else:
                        turn(i + 1, 0, True)
                pe.wait_ge(xt_done, j + 1)
                pe.wait_ge(w_loaded[s], 16 * LOADS * i + 16 * LOADS)
                if not (first and s < 2):
                    pe.wait_ge(h_done, HD * j - HD)
                for half in range(2 if gated else 1):
                    for f, (f0, fn) in enumerate(FCH):
                        for k in range(KC):
                            mm = nc.tensor.matmul(g.ps[0:fn, 2 + s % 2 + 2 * half, f * P:(f + 1) * P],
                                                  w1s[s][:, k, half * F + f0:half * F + f0 + fn], xgt[:, s % 2, k, :],
                                                  start=(k == 0), stop=(k == KC - 1))
                mm.then_inc(h_made, 1)
                if s > 0:
                    outputs(i, s - 1, not (first and s - 1 < 2))
                elif not first:
                    outputs(i - 1, R - 1, True)

            turn(0, 0, False)
            rings(pe, step)
            outputs(NR - 1, R - 1, True)

        @block.scalar
        def _(act):
            def rows(i, s, free):
                j = R * i + s
                act.wait_ge(x_turned, j + 1)
                if free:
                    act.wait_ge(h_made, j - 1)
                nc.scalar.activation(xgt[:, s % 2, :, :], g.ps[:, s % 2, :].rearrange("p (k c) -> p k c", k=KC),
                                     ACT.Copy).then_inc(xt_done, 1)

            def store(i, s):
                j = R * i + s
                act.wait_ge(y_done, j + 1)
                act.dma_start(y_dram[bass.ds(j * P, P), :], y[:, s, :]).then_inc(y_stored[s], 16)

            def step(i, s, first=False, last=False):
                j = R * i + s
                if not last:
                    if s < R - 1:
                        rows(i, s + 1, not (first and s < 1))
                    else:
                        rows(i + 1, 0, True)
                act.wait_ge(h_made, j + 1)
                free = not (first and s < 2)
                if gated:
                    if free:
                        act.wait_ge(h_done, HD * j - HD)
                    for rws, lo, hi in FULL:
                        nc.scalar.activation(silu[0:rws, s % 2, lo:hi, :],
                                             g.ps[0:rws, 2 + s % 2, lo * P:hi * P].rearrange("p (f c) -> p f c", f=hi - lo),
                                             ACT.Silu).then_inc(silu_done, 1)
                else:
                    act.wait_ge(w_loaded[s], 16 * LOADS * i + 16 * LOADS)
                    if free:
                        act.wait_ge(y_made, j - 1)
                    for f, (f0, fn) in enumerate(FCH):
                        nc.scalar.activation(ht[0:fn, s % 2, f, :], g.ps[0:fn, 2 + s % 2, f * P:(f + 1) * P], ACT.Relu,
                                             bias=b1s[0:fn, s, f:f + 1]).then_inc(h_done, 1)
                if s >= 2:
                    store(i, s - 2)
                elif not first:
                    store(i - 1, s + R - 2)

            rows(0, 0, False)
            rings(act, step)
            store(NR - 1, R - 2)
            store(NR - 1, R - 1)
            for s in range(R):
                act.wait_ge(y_stored[s], 16 * NR)

        @block.vector
        def _(dve):
            def out(i, s, free):
                j = R * i + s
                dve.wait_ge(y_made, j + 1)
                if free:
                    dve.wait_ge(y_stored[s], 16 * i)
                nc.vector.tensor_copy(y[:, s, :], g.ps[:, 6 + s % 2, :]).then_inc(y_done, 1)

            def step(i, s, first=False, last=False):
                j = R * i + s
                if gated:
                    for n, (rws, lo, hi) in enumerate(FULL):
                        dve.wait_ge(silu_done, 2 * j + n + 1)
                        dve.wait_ge(h_made, j + 1)
                        if not (first and s < 2):
                            dve.wait_ge(y_made, j - 1)
                        nc.vector.tensor_tensor(ht[0:rws, s % 2, lo:hi, :],
                                                g.ps[0:rws, 4 + s % 2, lo * P:hi * P].rearrange("p (f c) -> p f c", f=hi - lo),
                                                silu[0:rws, s % 2, lo:hi, :], ALU.mult).then_inc(h_done, 1)
                if s > 0:
                    out(i, s - 1, not first)
                elif not first:
                    out(i - 1, R - 1, True) if not isinstance(i, int) or i > 1 else out(i - 1, R - 1, False)

            rings(dve, step)
            out(NR - 1, R - 1, True)


def combine(nc, g, st, top_k, places, best, y_dram):
    RING = 8
    rows = st.sbuf("rows", [P, RING, D])
    loaded = [st.sem(f"loaded{n}") for n in range(RING)]
    added = st.sem("added")
    with nc.Block() as block:
        @block.gpsimd
        def _(pool):
            for n in range(top_k * NT):
                if n >= RING:
                    pool.wait_ge(added, n - RING + 1)
                nc.gpsimd.indirect_dma_start(rows[:, n % RING, :], None, y_dram[:, :],
                                             bass.IndirectOffsetOnAxis(ap=places[:, n:n + 1], axis=0)
                                             ).then_inc(loaded[n % RING], 16)

        @block.vector
        def _(dve):
            for n in range(top_k * NT):
                k, t = divmod(n, NT)
                dve.wait_ge(loaded[n % RING], 16 * (n // RING + 1))
                if k:
                    dve.wait_ge(added, n - NT + 1)
                nc.vector.scalar_tensor_tensor(g.x[:, t, :], rows[:, n % RING, :], best[:, t, k:k + 1], g.x[:, t, :],
                                               ALU.mult, ALU.add).then_inc(added, 1)


def scatter_tokens(nc, pool, top_k, ids, places, table, zeros_stored, scattered):
    pool.wait_ge(zeros_stored, 16)
    for n in range(top_k * NT):
        nc.gpsimd.indirect_dma_start(table[:, :], bass.IndirectOffsetOnAxis(ap=places[:, n:n + 1], axis=0),
                                     ids[:, n % NT:n % NT + 1], None).then_inc(scattered, 16)


def moe(nc, g, name, a, experts, top_k, wr, br, w1, w2, b1_cols, b2_rows, gated, shared=None):
    blocks = blocks_bound(experts, top_k)
    table = nc.dram_tensor(name + "_table", (blocks * P, 1), F32, kind="Internal").ap()
    y_dram = nc.dram_tensor(name + "_y", (blocks * P, D), F32, kind="Internal").ap()
    rows_dram = nc.dram_tensor(name + "_rows", (T, D), F32, kind="Internal").ap()
    layer_norm(nc, g, name + "_ln", rows_dram=rows_dram)
    with Stage(nc, name) as st:
        gates = st.sbuf("gates", [P, NT, experts])
        best = st.sbuf("best", [P, NT, 8])
        places = st.sbuf("places", [P, top_k * NT], U32)
        block_row = st.sbuf("block_row", [1, blocks], U32)
        index = st.sbuf("index", [P, blocks], U32)
        ids = st.sbuf("ids", [P, NT])
        even = st.sbuf("even", [P, NT, NSH])
        zeros_stored, scattered, ids_loaded = st.sem("zeros_stored"), st.sem("scattered"), st.sem("ids_loaded")
        with Stage(nc, name + "_pick") as pi:
            pick = pi.sbuf("pick", [P, top_k, NT, experts])
            with Stage(nc, name + "_route") as ro:
                router(nc, g, ro, name, wr, br, experts, top_k, gates[:, :, :], a["iota"], pick, best)
            with Stage(nc, name + "_place") as pl:
                place_tokens(nc, g, pl, a, experts, top_k, pick[:, :, :, :], places, block_row, blocks, zeros_stored, table)
        with Stage(nc, name + "_ids") as il:
            set_ = il.sem("set")
            with nc.Block() as block:
                @block.sync
                def _(sp):
                    sp.dma_start(ids[:, :], a["ids"]).then_inc(ids_loaded, 16)
                    sp.wait_ge(ids_loaded, 16)

                @block.vector
                def _(dve):
                    nc.vector.memset(even[:, :, :], 1.0 / NSH).then_inc(set_, 1)
                    dve.wait_ge(set_, 1)

        def scatter(pool):
            scatter_tokens(nc, pool, top_k, ids, places, table, zeros_stored, scattered)

        if shared is not None:
            sw1, sb1, sw2, sb2 = shared
            with Stage(nc, name + "_shared") as sh:
                experts_all_tokens(nc, g, sh, sw1, sw2, NSH, even, False, sb1, sb2, pool_work=scatter)
            with Stage(nc, name + "_bias") as bi:
                second_biases(nc, g, bi, experts, gates, b2_rows)
        else:
            with nc.Block() as block:
                @block.gpsimd
                def _(pool):
                    scatter(pool)
        with Stage(nc, name + "_back") as bk:
            place_tokens_back(nc, g, bk, table, blocks, scattered, top_k, index)
        with Stage(nc, name + "_blocks") as bl:
            experts_by_block(nc, g, bl, w1, w2, b1_cols, gated, blocks, block_row, index, rows_dram, y_dram)
        with Stage(nc, name + "_sum") as su:
            combine(nc, g, su, top_k, places, best, y_dram)


def second_biases(nc, g, st, experts, gates, b2_rows):
    b2 = st.sbuf("b2", [experts, D])
    gt = st.sbuf("gt", [experts, T])
    loaded, turned, done, made, added = (st.sem("loaded"), st.sem("turned"), st.sem("done"), st.sem("made"),
                                         st.sem("added"))
    with nc.Block() as block:
        @block.sync
        def _(sp):
            sp.dma_start(b2[:, :], b2_rows).then_inc(loaded, 16)

        @block.tensor
        def _(pe):
            for t in range(NT):
                mm = nc.tensor.transpose(g.ps[0:experts, t // 4, t % 4 * P:(t % 4 + 1) * P], gates[:, t, :], g.ident[:, :])
            mm.then_inc(turned, 1)
            pe.wait_ge(loaded, 16)
            pe.wait_ge(done, 1)
            for t in range(NT):
                if t >= 4:
                    pe.wait_ge(added, t - 3)
                nc.tensor.matmul(g.ps[:, 4 + t % 4, :], gt[:, t * P:(t + 1) * P], b2[:, :], start=True,
                                 stop=True).then_inc(made, 1)

        @block.scalar
        def _(act):
            act.wait_ge(turned, 1)
            nc.scalar.activation(gt[:, :], g.ps[0:experts, 0:2, :].rearrange("p a n -> p (a n)"),
                                 ACT.Copy).then_inc(done, 1)

        @block.vector
        def _(dve):
            for t in range(NT):
                dve.wait_ge(made, t + 1)
                nc.vector.tensor_tensor(g.x[:, t, :], g.x[:, t, :], g.ps[:, 4 + t % 4, :], ALU.add).then_inc(added, 1)


def cross_attention1(nc, g, name, a):
    NKT = CTX // P
    k_dram = nc.dram_tensor("k_raw", (B * H, P, CTX), F32, kind="Internal").ap()
    q_dram = nc.dram_tensor("q_raw", (B * H, P, S), F32, kind="Internal").ap()
    v_dram = nc.dram_tensor("v_rows", (B * H, NKT, P, DX), F32, kind="Internal").ap()
    with Stage(nc, name) as st:
        rk = st.sbuf("rk", [P, B * CTX])
        rq = st.sbuf("rq", [P, T])
        k_scale = st.sbuf("k_scale", [P, 2, B * H])
        with Stage(nc, name + "_made") as md:
            ctx = md.sbuf("ctx", [P, KC, B * CTX])
            ctx_loaded = md.sem("ctx_loaded")
            with Stage(nc, name + "_kq") as kq:
                project_kq1(nc, g, kq, a, ctx, ctx_loaded, k_dram, q_dram, rk, rq, k_scale)
            with Stage(nc, name + "_v") as vs:
                project_v1(nc, g, vs, a, ctx, v_dram)
        ot = st.sbuf("ot", [P, B * H, S])
        wo = st.sbuf("wo", [P, H, D])
        bo = st.sbuf("bo", [P, D])
        o_loaded = st.sem("o_loaded")
        with Stage(nc, name + "_core") as co:
            attention_core1(nc, g, co, a, k_dram, q_dram, v_dram, rk, rq, k_scale, ot, wo, bo, o_loaded)
        with Stage(nc, name + "_out") as ou:
            made, added, biased = ou.sem("made"), ou.sem("added"), ou.sem("biased")
            with nc.Block() as block:
                @block.gpsimd
                def _(pool):
                    pool.wait_ge(o_loaded, 32)
                    for t in range(NT):
                        nc.gpsimd.tensor_tensor(g.x[:, t, :], g.x[:, t, :], bo[:, :], ALU.add).then_inc(biased, 1)

                @block.tensor
                def _(pe):
                    pe.wait_ge(o_loaded, 32)
                    for t in range(NT):
                        b, s = divmod(t * P, S)
                        if t >= 4:
                            pe.wait_ge(added, t - 3)
                        for h in range(H):
                            mm = nc.tensor.matmul(g.ps[:, t % 4, :], ot[:, b * H + h, s:s + P], wo[:, h, :],
                                                  start=(h == 0), stop=(h == H - 1))
                        mm.then_inc(made, 1)

                @block.vector
                def _(dve):
                    for t in range(NT):
                        dve.wait_ge(made, t + 1)
                        dve.wait_ge(biased, t + 1)
                        nc.vector.tensor_tensor(g.x[:, t, :], g.x[:, t, :], g.ps[:, t % 4, :],
                                                ALU.add).then_inc(added, 1)


def project_kq1(nc, g, st, a, ctx, ctx_loaded, k_dram, q_dram, rk, rq, k_scale):
    UH = 6
    NS = B * CTX + T
    ki_w, k_w, q_w = a["L1_xattn_ki_w"], a["L1_xattn_k_w"], a["L1_xattn_q_w"]
    w = [st.sbuf(f"w{n}", [P, 3, KC, DX]) for n in range(2)]
    cols = st.sbuf("cols", [P, 3, H])
    bias = st.sbuf("bias", [P, 2, 3])
    bias_put = st.sem("bias_put")
    norm_cols = st.sbuf("norm_cols", [P, 3, H])
    raw = st.sbuf("raw", [P, UH, 512])
    sq = st.sbuf("sq", [P, 2, 512])
    sums = st.sbuf("sums", [P, NS])
    rms = st.sbuf("rms", [P, 2, 512])
    eps_q = st.sbuf("eps_q", [P, 1])
    w_loaded = [st.sem(f"w_loaded{n}") for n in range(2)]
    b_loaded, made, done = st.sem("b_loaded"), st.sem("made"), st.sem("done")
    squared, summed, zeroed = st.sem("squared"), st.sem("summed"), st.sem("zeroed")
    stored = [st.sem(f"stored{n}") for n in range(UH)]
    total, rooted, inverted, scaled = st.sem("total"), st.sem("rooted"), st.sem("inverted"), st.sem("scaled")
    with nc.Block() as block:
        @block.sync
        def _(sp):
            def load(h, slot, first=False):
                if not first:
                    sp.wait_ge(made, UH * (h - 1))
                for n, src in enumerate((ki_w, k_w, q_w)):
                    sp.dma_start(w[slot][:, n, :, :],
                                 src[:, bass.ds(h * DX, DX)].rearrange("(k p) n -> p k n", p=P)).then_inc(w_loaded[slot], 16)

            def store(h):
                for u in range(UH):
                    sp.wait_ge(done, UH * h + u + 1)
                    if u < 4:
                        b, half = divmod(u, 2)
                        dst = k_dram[h + b * H, :, half * 512:(half + 1) * 512]
                    else:
                        dst = q_dram[h + (u - 4) * H, :, :]
                    sp.dma_start(dst, raw[:, u, :]).then_inc(stored[u], 16)

            load(0, 0, first=True)
            for c in range(B * 2):
                sp.dma_start(ctx[:, :, c * 512:(c + 1) * 512],
                             a["ctxt"][:, c * 512:(c + 1) * 512].rearrange("(k p) n -> p k n", p=P)).then_inc(ctx_loaded, 16)
                if c == 0:
                    for n, b in enumerate(("ki_b", "k_b", "q_b")):
                        sp.dma_start(cols[:, n, :], a[b + "_cols"]).then_inc(b_loaded, 16)
                    for n, b in enumerate(("nq_s", "nki_s", "nkt_s")):
                        sp.dma_start(norm_cols[:, n, :], a[b + "_cols"]).then_inc(b_loaded, 16)
            load(1, 1, first=True)
            store(0)
            load(2, 0)
            store(1)
            load(3, 1)
            with sp.Fori(1, H // 2 - 1) as i:
                store(2 * i)
                load(2 * i + 2, 0)
                store(2 * i + 1)
                load(2 * i + 3, 1)
            store(H - 2)
            store(H - 1)
            for u in range(UH):
                sp.wait_ge(stored[u], 16 * H)

        @block.tensor
        def _(pe):
            def head(i, slot, first=False):
                h = 2 * i + slot
                pe.wait_ge(w_loaded[slot], 48 * i + 48)
                for u in range(UH):
                    if not (first and slot == 0):
                        pe.wait_ge(done, UH * h + u - UH + 1)
                    if u == 0:
                        parts = [(0, 0, NIMG), (1, NIMG, 512)]
                    elif u == 2:
                        parts = [(0, CTX, CTX + NIMG), (1, CTX + NIMG, CTX + 512)]
                    else:
                        parts = [(1, u * 512, (u + 1) * 512)]
                    for k in range(KC if u >= 4 else 0):
                        mm = nc.tensor.matmul(g.ps[:, u, :], w[slot][:, 2, k, :], g.xt[:, k, (u - 4) * S:(u - 3) * S],
                                              start=(k == 0), stop=(k == KC - 1))
                    for n, lo, hi in parts if u < 4 else ():
                        for k in range(KC):
                            mm = nc.tensor.matmul(g.ps[:, u, lo - u * 512:hi - u * 512], w[slot][:, n, k, :],
                                                  ctx[:, k, lo:hi], start=(k == 0), stop=(k == KC - 1))
                    mm.then_inc(made, 1)

            pe.wait_ge(ctx_loaded, 64)
            head(0, 0, first=True)
            head(0, 1, first=True)
            with pe.Fori(1, H // 2) as i:
                head(i, 0)
                head(i, 1)
            pe.wait_ge(summed, UH * H)
            for c in range(NS // 512):
                nc.tensor.matmul(g.ps[:, c, :], g.ones[:, :], sums[:, c * 512:(c + 1) * 512], start=True,
                                 stop=True).then_inc(total, 1)

        @block.scalar
        def _(act):
            def head(i, slot, first=False):
                h = 2 * i + slot
                nc.scalar.activation(bias[:, slot, :], cols[:, :, bass.ds(h, 1)].rearrange("p n o -> p (n o)"),
                                     ACT.Copy).then_inc(bias_put, 1)
                act.wait_ge(bias_put, h + 1)
                for u in range(UH):
                    act.wait_ge(made, UH * h + u + 1)
                    if not (first and slot == 0):
                        act.wait_ge(stored[u], 16 * h)
                        act.wait_ge(squared, UH * h + u - UH + 1)
                    parts = [(0, 0, NIMG), (1, NIMG, 512)] if u in (0, 2) else [(1 if u < 4 else 2, 0, 512)]
                    for n, lo, hi in parts:
                        ins = nc.scalar.activation(raw[:, u, lo:hi], g.ps[:, u, lo:hi], ACT.Identity,
                                                   bias=bias[:, slot, n:n + 1])
                    ins.then_inc(done, 1)

            act.wait_ge(b_loaded, 96)
            head(0, 0, first=True)
            head(0, 1, first=True)
            with act.Fori(1, H // 2) as i:
                head(i, 0)
                head(i, 1)
            act.wait_ge(zeroed, 2)
            for c in range(NS // 512):
                act.wait_ge(total, c + 1)
                if c >= 2:
                    act.wait_ge(inverted, c - 1)
                keys = c < B * 2
                nc.scalar.activation(rms[:, c % 2, :], g.ps[:, c, :], ACT.Sqrt,
                                     scale=1.0 / INNER if keys else float(DX) / INNER,
                                     bias=g.rms_eps[:, 0:1] if keys else eps_q[:, 0:1]).then_inc(rooted, 1)

        @block.vector
        def _(dve):
            def head(i, slot, first=False):
                h = 2 * i + slot
                for u in range(UH):
                    dve.wait_ge(done, UH * h + u + 1)
                    if not (first and slot == 0 and u < 2):
                        dve.wait_ge(summed, UH * h + u - 1)
                    nc.vector.tensor_tensor(sq[:, u % 2, :], raw[:, u, :], raw[:, u, :], ALU.mult).then_inc(squared, 1)

            nc.vector.memset(eps_q[:, :], RMS_EPS * DX).then_inc(zeroed, 1)
            dve.wait_ge(b_loaded, 96)
            for n in range(2):
                for b in range(B):
                    nc.vector.tensor_tensor(k_scale[:, n, b * H:(b + 1) * H], norm_cols[:, 0, :], norm_cols[:, 1 + n, :],
                                            ALU.mult).then_inc(scaled, 1)
            head(0, 0, first=True)
            head(0, 1, first=True)
            with dve.Fori(1, H // 2) as i:
                head(i, 0)
                head(i, 1)
            for c in range(NS // 512):
                dve.wait_ge(rooted, c + 1)
                dst = rk[:, c * 512:(c + 1) * 512] if c < B * 2 else rq[:, (c - B * 2) * 512:(c - B * 2 + 1) * 512]
                nc.vector.reciprocal(dst, rms[:, c % 2, :]).then_inc(inverted, 1)

        @block.gpsimd
        def _(pool):
            def head(i, slot, first=False):
                h = 2 * i + slot
                for u in range(UH):
                    pool.wait_ge(squared, UH * h + u + 1)
                    if not (first and slot == 0):
                        pool.wait_ge(summed, UH * h + u - UH + 1)
                    nc.gpsimd.tensor_tensor(sums[:, u * 512:(u + 1) * 512], sums[:, u * 512:(u + 1) * 512],
                                            sq[:, u % 2, :], ALU.add).then_inc(summed, 1)

            nc.gpsimd.memset(sums[:, :], 0.0).then_inc(zeroed, 1)
            pool.wait_ge(zeroed, 2)
            head(0, 0, first=True)
            head(0, 1, first=True)
            with pool.Fori(1, H // 2) as i:
                head(i, 0)
                head(i, 1)


def project_v1(nc, g, st, a, ctx, v_dram):
    NKT = CTX // P
    HG = 512 // DX
    NG = H // HG
    EDGE, REST = divmod(NIMG, P)
    assert REST == 1
    RING = 4
    w = [st.sbuf(f"w{n}", [P, 2, KC, 512]) for n in range(2)]
    bias = st.sbuf("bias", [P, 2, INNER])
    rows = st.sbuf("rows", [P, RING, 512])
    w_loaded = [st.sem(f"w_loaded{n}") for n in range(2)]
    b_loaded, made, done, edged = st.sem("b_loaded"), st.sem("made"), st.sem("done"), st.sem("edged")
    stored = [st.sem(f"stored{n}") for n in range(RING)]
    UT = B * NKT
    with nc.Block() as block:
        @block.sync
        def _(sp):
            def load(n, slot, first=False):
                if not first:
                    sp.wait_ge(made, UT * (n - 1))
                for m, src in enumerate((a["L1_xattn_vi_w"], a["L1_xattn_v_w"])):
                    sp.dma_start(w[slot][:, m, :, :],
                                 src[:, bass.ds(n * 512, 512)].rearrange("(k p) n -> p k n", p=P)).then_inc(w_loaded[slot], 16)

            def store(n):
                for t in range(UT):
                    b, kb = divmod(t, NKT)
                    sp.wait_ge(done, UT * n + t + 1)
                    sp.dma_start(v_dram[bass.ds(n * HG + b * H, HG), kb, :, :].rearrange("h p d -> p h d"),
                                 rows[:, t % RING, :].rearrange("p (h d) -> p h d", h=HG)).then_inc(stored[t % RING], 16)

            load(0, 0, first=True)
            sp.dma_start(bias[:, 0, :], a["L1_xattn_vi_b"].partition_broadcast(P)).then_inc(b_loaded, 16)
            sp.dma_start(bias[:, 1, :], a["L1_xattn_v_b"].partition_broadcast(P)).then_inc(b_loaded, 16)
            load(1, 1, first=True)
            with sp.Fori(0, NG // 2 - 1) as i:
                store(2 * i)
                load(2 * i + 2, 0)
                store(2 * i + 1)
                load(2 * i + 3, 1)
            store(NG - 2)
            store(NG - 1)
            for r in range(RING):
                sp.wait_ge(stored[r], 16 * NG * UT // RING)

        @block.tensor
        def _(pe):
            def group(i, slot, first=False):
                n = 2 * i + slot
                pe.wait_ge(w_loaded[slot], 32 * i + 32)
                for t in range(UT):
                    b, kb = divmod(t, NKT)
                    if not (first and slot == 0 and t < 4):
                        pe.wait_ge(done, UT * n + t - 3)
                    kind = 0 if kb < EDGE else 1
                    for k in range(KC):
                        mm = nc.tensor.matmul(g.ps[:, t % 4, :], ctx[:, k, t * P:(t + 1) * P], w[slot][:, kind, k, :],
                                              start=(k == 0), stop=(k == KC - 1))
                    if kb == EDGE:
                        for k in range(KC):
                            mm = nc.tensor.matmul(g.ps[0:1, 4 + b, :], ctx[:, k, t * P:t * P + 1], w[slot][:, 0, k, :],
                                                  start=(k == 0), stop=(k == KC - 1))
                    mm.then_inc(made, 1)

            group(0, 0, first=True)
            group(0, 1, first=True)
            with pe.Fori(1, NG // 2) as i:
                group(i, 0)
                group(i, 1)

        @block.vector
        def _(dve):
            def group(i, slot, first=False):
                n = 2 * i + slot
                for t in range(UT):
                    b, kb = divmod(t, NKT)
                    dve.wait_ge(made, UT * n + t + 1)
                    r = t % RING
                    if not (first and slot == 0 and t < RING):
                        dve.wait_ge(stored[r], (UT // RING * n + t // RING) * 16)
                    kind = 0 if kb < EDGE else 1
                    ins = nc.vector.tensor_tensor(rows[:, r, :], g.ps[:, t % 4, :], bias[:, kind, bass.ds(n * 512, 512)],
                                                  ALU.add)
                    if kb == EDGE:
                        ins.then_inc(edged, 1)
                        dve.wait_ge(edged, B * n + b + 1)
                        ins = nc.vector.tensor_tensor(rows[0:1, r, :], g.ps[0:1, 4 + b, :],
                                                      bias[0:1, 0, bass.ds(n * 512, 512)], ALU.add)
                    ins.then_inc(done, 1)

            dve.wait_ge(b_loaded, 32)
            group(0, 0, first=True)
            group(0, 1, first=True)
            with dve.Fori(1, NG // 2) as i:
                group(i, 0)
                group(i, 1)


def attention_core1(nc, g, st, a, k_dram, q_dram, v_dram, rk, rq, k_scale, ot, wo, bo, o_loaded):
    NKT, QB = CTX // P, S // P
    HP, U = 2, 2 * QB
    NI = B * H // HP
    NB = NI // B
    SB, SKEW, PR = 2, 2, 4
    SPANS = [(0, NIMG), (NIMG, CTX)]
    k = st.sbuf("k", [P, HP, CTX])
    q = st.sbuf("q", [P, HP, S])
    v = st.sbuf("v", [P, HP, NKT, DX])
    prob = g.xt
    pt = st.sbuf("pt", [P, HP, NKT, S])
    nmax, rsum, rinv = st.sbuf("nmax", [P, PR, 2]), st.sbuf("rsum", [P, PR, 2]), st.sbuf("rinv", [P, PR, 2])
    kq_loaded = [st.sem(f"kq_loaded{n}") for n in range(HP)]
    v_loaded = [st.sem(f"v_loaded{n}") for n in range(HP)]
    k_done, q_done = st.sem("k_done"), st.sem("q_done")
    scores = st.sem("scores")
    max_done = st.sem("max_done")
    exp_done = st.sem("exp_done")
    rinv_done = st.sem("rinv_done")
    prob_done = st.sem("prob_done")
    turned = [st.sem(f"turned{n}") for n in range(2)]
    pt_done = [st.sem(f"pt_done{n}") for n in range(2)]
    pv_done = st.sem("pv_done")
    ot_done = st.sem("ot_done")

    def s_ps(n):
        return g.ps[:, 2 * (n % SB):2 * (n % SB) + 2, :].rearrange("p a n -> p (a n)")

    def over_pairs(eng, step):
        for n in range(U):
            step(0, n, 0, 0, first=True)
        with eng.Fori(1, NB - 1) as i:
            for n in range(U):
                step(i, n, 0, 0)
        for n in range(U):
            step(NB - 1, n, 0, 1)
        with eng.Fori(NB, NI - 1) as i:
            for n in range(U):
                step(i, n, 1, 1)
        for n in range(U):
            step(NI - 1, n, 1, None)

    with nc.Block() as block:
        @block.sync
        def _(sp):
            def load(i, s, first=False):
                j = HP * i + s
                if not first:
                    sp.wait_ge(scores, QB * (j - 1))
                sp.dma_start(k[:, s, :], k_dram[j, :, :]).then_inc(kq_loaded[s], 16)
                sp.dma_start(q[:, s, :], q_dram[j, :, :]).then_inc(kq_loaded[s], 16)
                if not first:
                    sp.wait_ge(pv_done, j - 1)
                sp.dma_start(v[:, s, :, :], v_dram[j, :, :, :].rearrange("t p d -> p t d")).then_inc(v_loaded[s], 16)

            load(0, 0, first=True)
            load(0, 1, first=True)
            sp.dma_start(wo[:, :, :], a["L1_xattn_o_w"].rearrange("(h p) n -> p h n", p=P)).then_inc(o_loaded, 16)
            sp.dma_start(bo[:, :], a["L1_xattn_o_b"].partition_broadcast(P)).then_inc(o_loaded, 16)
            with sp.Fori(1, NI) as i:
                load(i, 0)
                load(i, 1)
            sp.wait_ge(o_loaded, 32)

        @block.tensor
        def _(pe):
            def step(i, n, b=0, nb=0, first=False, tail=False):
                u = U * i + n
                s, qb = divmod(n % U, QB)
                if not tail:
                    if qb == 0:
                        pe.wait_ge(k_done, HP * i + s + 1)
                        pe.wait_ge(q_done, HP * i + s + 1)
                    if not (first and n < SB):
                        pe.wait_ge(exp_done, u - SB + 1)
                    for c in range(0, CTX, 512):
                        mm = nc.tensor.matmul(s_ps(n)[:, c:c + 512], q[:, s, qb * P:(qb + 1) * P], k[:, s, c:c + 512],
                                              start=True, stop=True)
                    mm.then_inc(scores, 1)
                nn = n - SKEW
                if first and nn < 0:
                    return
                w = u - SKEW
                if nn < U:
                    pe.wait_ge(prob_done, w + 1)
                    for half in range(2):
                        if not (first and nn < 1):
                            pe.wait_ge(pt_done[half], w)
                        for m in range(4):
                            c = (4 * half + m) * P
                            mm = nc.tensor.transpose(g.ps[:, 4 + half, m * P:(m + 1) * P], prob[:, nn % PR, c:c + P],
                                                     g.ident[:, :])
                        mm.then_inc(turned[half], 1)
                if nn % QB == 0 and not (first and nn == 0):
                    hs = (nn // QB - 1) % HP
                    heads = HP * i + nn // QB
                    for half in range(2):
                        pe.wait_ge(pt_done[half], w)
                    pe.wait_ge(v_loaded[hs], 16 * (i + (nn // QB + 1) // HP))
                    if not (first and nn // QB - 1 < HP):
                        pe.wait_ge(ot_done, heads - HP)
                    for m in range(NKT):
                        mm = nc.tensor.matmul(g.ps[:, 6 + hs, :], v[:, hs, m, :], pt[:, hs, m, :], start=(m == 0),
                                              stop=(m == NKT - 1))
                    mm.then_inc(pv_done, 1)

            over_pairs(pe, step)
            for n in range(U, U + SKEW + 1):
                step(NI - 1, n, tail=True)

        @block.vector
        def _(dve):
            def put_k(j, s, b, loads):
                dve.wait_ge(kq_loaded[s], 32 * loads)
                for m, (lo, hi) in enumerate(SPANS):
                    ins = nc.vector.scalar_tensor_tensor(k[:, s, lo:hi], k[:, s, lo:hi], k_scale[:, m, bass.ds(j, 1)],
                                                         rk[:, b * CTX + lo:b * CTX + hi], ALU.mult, ALU.mult)
                ins.then_inc(k_done, 1)

            def step(i, n, b=0, nb=0, first=False, tail=False):
                u = U * i + n
                s, qb = divmod(n % U, QB)
                if not tail:
                    dve.wait_ge(scores, u + 1)
                    for m, (lo, hi) in enumerate(SPANS):
                        ins = nc.vector.tensor_reduce(nmax[:, n % PR, m:m + 1], s_ps(n)[:, lo:hi], X_AXIS, ALU.max,
                                                      negate=True)
                    ins.then_inc(max_done, 1)
                if not (first and n < 1) and n <= U:
                    dve.wait_ge(exp_done, u)
                    nc.vector.reciprocal(rinv[:, (n - 1) % PR, :], rsum[:, (n - 1) % PR, :]).then_inc(rinv_done, 1)
                nn = n - SKEW
                if not (first and nn < 0) and nn < U:
                    w = u - SKEW
                    hs, wq = divmod(nn % U, QB)
                    dve.wait_ge(turned[0], w + 1)
                    if wq == 0 and not (first and nn // QB < HP):
                        dve.wait_ge(pv_done, HP * i + nn // QB - 1)
                    nc.vector.tensor_copy(pt[:, hs, 0:4, wq * P:(wq + 1) * P],
                                          g.ps[:, 4, :].rearrange("p (m q) -> p m q", m=4)).then_inc(pt_done[0], 1)
                if not tail and qb == 2:
                    if s == 0 and not first:
                        put_k(HP * i + 1, 1, b, i + 1)
                    if s == 1 and nb is not None:
                        put_k(HP * i + 2, 0, nb, i + 2)

            put_k(0, 0, 0, 1)
            put_k(1, 1, 0, 1)
            over_pairs(dve, step)
            for n in range(U, U + SKEW):
                step(NI - 1, n, tail=True)

        @block.scalar
        def _(act):
            def store(j, s):
                act.wait_ge(pv_done, j + 1)
                nc.scalar.activation(ot[:, j, :], g.ps[:, 6 + s, :], ACT.Copy).then_inc(ot_done, 1)

            def step(i, n, b=0, nb=0, first=False, tail=False):
                u = U * i + n
                if not tail:
                    act.wait_ge(max_done, u + 1)
                    if not (first and n < PR):
                        for half in range(2):
                            act.wait_ge(turned[half], u - PR + 1)
                    for m, (lo, hi) in enumerate(SPANS):
                        ins = nc.scalar.activation(prob[:, n % PR, lo:hi], s_ps(n)[:, lo:hi], ACT.Exp,
                                                   bias=nmax[:, n % PR, m:m + 1], accum_out=rsum[:, n % PR, m:m + 1])
                    ins.then_inc(exp_done, 1)
                nn = n - SKEW
                if not (first and nn < 0) and nn < U:
                    w = u - SKEW
                    hs, wq = divmod(nn % U, QB)
                    act.wait_ge(turned[1], w + 1)
                    if wq == 0 and not (first and nn // QB < HP):
                        act.wait_ge(pv_done, HP * i + nn // QB - 1)
                    nc.scalar.activation(pt[:, hs, 4:8, wq * P:(wq + 1) * P],
                                         g.ps[:, 5, :].rearrange("p (m q) -> p m q", m=4), ACT.Copy).then_inc(pt_done[1], 1)
                if not tail and n % QB == SKEW + 1:
                    s = n // QB
                    if s == 1:
                        store(HP * i, 0)
                    elif not first:
                        store(HP * i - 1, 1)

            over_pairs(act, step)
            for n in range(U, U + SKEW):
                step(NI - 1, n, tail=True)
            store(B * H - 1, 1)

        @block.gpsimd
        def _(pool):
            def put_q(j, s, b, loads):
                pool.wait_ge(kq_loaded[s], 32 * loads)
                nc.gpsimd.tensor_tensor(q[:, s, :], q[:, s, :], rq[:, b * S:(b + 1) * S], ALU.mult).then_inc(q_done, 1)

            def step(i, n, b=0, nb=0, first=False):
                u = U * i + n
                s, qb = divmod(n, QB)
                pool.wait_ge(rinv_done, u + 1)
                for m, (lo, hi) in enumerate(SPANS):
                    ins = nc.gpsimd.tensor_tensor(prob[:, n % PR, lo:hi], prob[:, n % PR, lo:hi],
                                                  rinv[:, n % PR, m:m + 1].to_broadcast([P, hi - lo]), ALU.mult)
                ins.then_inc(prob_done, 1)
                if qb == 2:
                    if s == 0 and not first:
                        put_q(HP * i + 1, 1, b, i + 1)
                    if s == 1 and nb is not None:
                        put_q(HP * i + 2, 0, nb, i + 2)

            put_q(0, 0, 0, 1)
            put_q(1, 1, 0, 1)
            over_pairs(pool, step)


def store_residual(nc, g, out):
    with Stage(nc, "store") as st:
        stored = st.sem("stored")
        with nc.Block() as block:
            @block.sync
            def _(sp):
                sp.dma_start(out.rearrange("(t p) d -> p t d", p=P), g.x[:, :, :]).then_inc(stored, 16)
                sp.wait_ge(stored, 16)


def decoder_kernel(nc, a, out, stages=6):
    with ExitStack() as stack:
        g = Shared()

        def sb(name, shape, dt=F32):
            return stack.enter_context(nc.sbuf_tensor(name, shape, dt))

        g.x = sb("residual", [P, NT, D])
        g.xt = sb("normed", [P, KC, T])
        g.ident, g.ident16, g.ones = sb("identity", [P, P]), sb("identity16", [P, P], BF16), sb("all_ones", [P, P])
        g.ln_eps, g.rms_eps = sb("ln_eps", [P, 1]), sb("rms_eps", [P, 1])
        g.ps = stack.enter_context(nc.psum_tensor("ps", [P, 8, 512], F32))
        load_constants(nc, g, a["x"], a["ident"], a["ones"])
        if 1 in stages:
            layer_norm(nc, g, "ln0a")
            self_attention(nc, g, "sa0", a["wqkv0"], a["wo0"], (a["cos"], a["sin"], a["swap"]), a["mask"])
        if 2 in stages:
            layer_norm(nc, g, "ln0b", turn=False)
            cross_attention0(nc, g, "xa0", a["ctxt"], a["L0_xattn_wq"], a["bq0_cols"], a["wkvt0"],
                             a["bk0_cols"], a["L0_xattn_bkv"],
                             a["L0_xattn_wp"], a["L0_xattn_bp"])
        if 3 in stages:
            moe(nc, g, "moe0", a, NE0, TOP0, a["wgt0"], None, a["L0_ffn_w1"], a["L0_ffn_w2"], None, None, True)
        if 4 in stages:
            layer_norm(nc, g, "ln1a")
            self_attention(nc, g, "sa1", a["wqkv1"], a["wo1"], None, a["mask"])
        if 5 in stages:
            layer_norm(nc, g, "ln1b")
            cross_attention1(nc, g, "xa1", a)
        if 6 in stages:
            moe(nc, g, "moe1", a, NE1, TOP1, a["L1_ffn_router_w"], a["L1_ffn_router_b"], a["L1_ffn_rw1"],
                a["L1_ffn_rw2"], a["rb1_cols"], a["L1_ffn_rb2"], False,
                shared=(a["L1_ffn_sw1"], a["L1_ffn_sb1"], a["L1_ffn_sw2"], a["L1_ffn_sb2"]))
        store_residual(nc, g, out)


def lay_out(inputs):
    a = {}
    for name in ("L0_xattn_wq", "L0_xattn_bkv", "L0_xattn_wp", "L0_xattn_bp", "L0_ffn_w1", "L0_ffn_w2",
                 "L1_xattn_q_w", "L1_xattn_k_w", "L1_xattn_v_w", "L1_xattn_v_b",
                 "L1_xattn_ki_w", "L1_xattn_vi_w", "L1_xattn_vi_b", "L1_xattn_o_w", "L1_xattn_o_b",
                 "L1_ffn_sw1", "L1_ffn_sb1", "L1_ffn_sw2",
                 "L1_ffn_sb2", "L1_ffn_rw1", "L1_ffn_rw2", "L1_ffn_rb2", "L1_ffn_router_w",
                 "L1_ffn_router_b"):
        a[name] = np.asarray(inputs[name])
    a["x"] = np.asarray(inputs["x"]).reshape(T, D)
    a["ctxt"] = np.asarray(inputs["ctx_2048"]).reshape(B * CTX, D).T
    a["wqkv0"] = np.concatenate([np.asarray(inputs[f"L0_attn_W{c}"]).T for c in "qkv"], axis=1)
    a["wo0"] = np.asarray(inputs["L0_attn_Wo"]).T
    a["wkvt0"] = np.asarray(inputs["L0_xattn_wkv"]).T
    a["wgt0"] = np.asarray(inputs["L0_ffn_wg"]).T
    a["wqkv1"] = np.asarray(inputs["L1_attn_w_project"]).T
    a["wo1"] = np.asarray(inputs["L1_attn_w_out"]).T
    def columns(v):
        return v.reshape(-1, P).T

    a["bq0_cols"] = columns(np.asarray(inputs["L0_xattn_bq"]))
    a["bk0_cols"] = columns(np.asarray(inputs["L0_xattn_bkv"])[0:D])
    for name in ("q_b", "k_b", "ki_b", "nq_s", "nkt_s", "nki_s"):
        a[name + "_cols"] = columns(np.asarray(inputs["L1_xattn_" + name]))
    rb1 = np.asarray(inputs["L1_ffn_rb1"])
    a["rb1_cols"] = np.concatenate([rb1, np.zeros((NE1, len(FCH) * P - F), rb1.dtype)], axis=1
                                   ).reshape(NE1, len(FCH), P).transpose(0, 2, 1)
    freq = np.float32(10000.0) ** (-np.arange(0, DH, 2, dtype=np.float32) / np.float32(DH))
    angles = np.arange(S, dtype=np.float32)[:, None] * freq[None, :]
    a["cos"] = np.tile(np.repeat(np.cos(angles).T, 2, axis=0), (HPC, 1)).astype(np.float32)
    a["sin"] = np.tile(np.repeat(np.sin(angles).T, 2, axis=0), (HPC, 1)).astype(np.float32)
    even = np.arange(0, P, 2)
    swap = np.zeros((P, P), np.float32)
    swap[even + 1, even] = -1.0
    swap[even, even + 1] = 1.0
    a["swap"] = swap
    a["mask"] = np.triu(np.full((P, P), MASKED, np.float32), 1)
    a["ident"] = np.eye(P, dtype=np.float32)
    a["ones"] = np.ones((P, P), np.float32)
    a["earlier"] = np.triu(np.ones((P, P), np.float32), 1)
    a["ids"] = np.arange(T, dtype=np.float32).reshape(NT, P).T
    a["iota"] = np.arange(P, dtype=np.float32)
    return {name: np.ascontiguousarray(v) for name, v in a.items()}


def kernel(**inputs):
    import concourse.bacc as bacc
    from concourse.bass_utils import run_bass_kernel_spmd

    nc = bacc.Bacc("TRN2", target_bir_lowering=False, num_devices=1)
    arrays = lay_out(inputs)
    aps = {name: nc.dram_tensor(name, v.shape, mybir.dt.from_np(v.dtype), kind="ExternalInput").ap()
           for name, v in arrays.items()}
    out = nc.dram_tensor("out", (T, D), F32, kind="ExternalOutput").ap()
    decoder_kernel(nc, aps, out, stages=(1, 2, 3, 4, 5, 6))
    result = run_bass_kernel_spmd(nc, [arrays], core_ids=[0])
    return result.results[0]["out"].reshape(B, S, D)
```

```python
from contextlib import ExitStack

import numpy as np

import concourse.bass as bass
from concourse import mybir

P = 128
B, S, D = 2, 512, 512
T = B * S
NT = T // P
KC = D // P
H = 16
DH = D // H
HPC = P // DH
CTX = 1024
NE0, NE1, NSH = 8, 32, 2
TOP0, TOP1 = 2, 6
F = 352
FCH = [(0, 128), (128, 128), (256, 96)]
DX = 128
INNER = H * DX
NIMG = 257
LN_EPS = 1e-5
RMS_EPS = 1e-6
TOPK_EPS = 1e-20
MASKED = -1.0e30
ROUND = 12582912.0

ALU = mybir.AluOpType
ACT = mybir.ActivationFunctionType
F32 = mybir.dt.float32
F32R = mybir.dt.float32r
BF16 = mybir.dt.bfloat16
U32 = mybir.dt.uint32
X_AXIS = mybir.AxisListType.X


class Stage:

    def __init__(self, nc, name):
        self.nc, self.name, self.stack, self.sems = nc, name, ExitStack(), []

    def sbuf(self, name, shape, dt=F32):
        return self.stack.enter_context(self.nc.sbuf_tensor(f"{self.name}_{name}", shape, dt))

    def sem(self, name):
        s = self.nc.alloc_semaphore(f"{self.name}_{name}")
        self.sems.append(s)
        return s

    def __enter__(self):
        return self

    def __exit__(self, *exc):
        if exc[0] is None:
            self.nc.clear_and_free_semaphores(self.sems)
            self.nc.all_engine_barrier()
        return self.stack.__exit__(*exc)


class Shared:
    pass


def load_constants(nc, g, x, ident, ones):
    with Stage(nc, "init") as st:
        loaded = st.sem("loaded")
        cast = st.sem("cast")
        with nc.Block() as block:
            @block.sync
            def _(sp):
                sp.dma_start(g.x[:, :, :], x.rearrange("(t p) d -> p t d", p=P)).then_inc(loaded, 16)
                sp.dma_start(g.ident[:, :], ident).then_inc(loaded, 16)
                sp.dma_start(g.ones[:, :], ones).then_inc(loaded, 16)

            @block.vector
            def _(dve):
                dve.wait_ge(loaded, 48)
                nc.vector.tensor_copy(g.ident16[:, :], g.ident[:, :]).then_inc(cast, 1)
                nc.vector.memset(g.ln_eps[:, :], LN_EPS).then_inc(cast, 1)
                nc.vector.memset(g.rms_eps[:, :], RMS_EPS).then_inc(cast, 1)
                dve.wait_ge(cast, 3)


def layer_norm(nc, g, name, turn=True, rows_dram=None, prefetch=None):
    with Stage(nc, name) as st:
        stats = st.sbuf("stats", [P, NT, 6])
        mv = st.sbuf("mv", [P, NT, 2])
        std = st.sbuf("std", [P, NT])
        rstd = st.sbuf("rstd", [P, NT])
        xn = st.sbuf("xn", [P, NT, D]) if turn else g.xt[:, :, :].rearrange("p k (a d) -> p (k a) d", d=D)
        stats_done, mean_done, std_done = st.sem("stats_done"), st.sem("mean_done"), st.sem("std_done")
        rstd_done, normed, turned, copied = st.sem("rstd_done"), st.sem("normed"), st.sem("turned"), st.sem("copied")
        rows_stored = st.sem("rows_stored")
        with nc.Block() as block:
            if prefetch is not None:
                @block.sync
                def _(sp):
                    prefetch(sp)

            if rows_dram is not None:
                @block.sync
                def _(sp):
                    for half in range(2):
                        a, b = half * NT // 2, (half + 1) * NT // 2
                        sp.wait_ge(normed, b)
                        sp.dma_start(rows_dram[a * P:b * P, :].rearrange("(t p) d -> p t d", p=P),
                                     xn[:, a:b, :]).then_inc(rows_stored, 16)
                    sp.wait_ge(rows_stored, 32)

            @block.vector
            def _(dve):
                for t in range(NT):
                    nc.vector.bn_stats(stats[:, t, :], g.x[:, t, :]).then_inc(stats_done, 1)
                for t in range(NT):
                    dve.wait_ge(stats_done, t + 1)
                    nc.vector.bn_aggr(mv[:, t, :], stats[:, t, :]).then_inc(mean_done, 1)
                dve.wait_ge(std_done, 1)
                nc.vector.reciprocal(rstd[:, :], std[:, :]).then_inc(rstd_done, 1)
                dve.wait_ge(rstd_done, 1)
                for t in range(NT):
                    nc.vector.tensor_scalar(xn[:, t, :], g.x[:, t, :], mv[:, t, 0:1], rstd[:, t:t + 1],
                                            ALU.subtract, ALU.mult).then_inc(normed, 1)

            @block.scalar
            def _(act):
                act.wait_ge(mean_done, NT)
                nc.scalar.activation(std[:, :], mv[:, :, 1], ACT.Sqrt, bias=g.ln_eps[:, 0:1]).then_inc(std_done, 1)
                for t in range(NT if turn else 0):
                    act.wait_ge(turned, t + 1)
                    nc.scalar.activation(g.xt[:, :, t * P:(t + 1) * P],
                                         g.ps[:, t % 4, :].rearrange("p (k c) -> p k c", k=KC),
                                         ACT.Copy).then_inc(copied, 1)

            @block.tensor
            def _(pe):
                for t in range(NT if turn else 0):
                    pe.wait_ge(normed, t + 1)
                    if t >= 4:
                        pe.wait_ge(copied, t - 3)
                    for k in range(KC):
                        mm = nc.tensor.transpose(g.ps[:, t % 4, k * P:(k + 1) * P], xn[:, t, k * P:(k + 1) * P],
                                                 g.ident[:, :])
                    mm.then_inc(turned, 1)


def self_attention(nc, g, name, wqkv, wo, rope, mask):
    with Stage(nc, name) as st:
        qt = st.sbuf("qt", [P, B * KC, S])
        kt = st.sbuf("kt", [P, B * KC, S])
        v = st.sbuf("v", [P, B * KC, S // P, P])
        ot = st.sbuf("ot", [P, B * KC, S])
        wos = st.sbuf("wo", [P, KC, D])
        masks = st.sbuf("mask", [P, P])
        wo_loaded = st.sem("wo_loaded")
        w = st.sbuf("w", [P, KC, 3 * D])
        w_loaded = [st.sem(f"w_loaded{n}") for n in range(3)]

        def load_weights(sp):
            for part in range(3):
                sp.dma_start(w[:, :, part * D:(part + 1) * D],
                             wqkv[:, part * D:(part + 1) * D].rearrange("(k p) n -> p k n", p=P)
                             ).then_inc(w_loaded[part], 16)

        layer_norm(nc, g, name + "_ln", prefetch=load_weights)
        with Stage(nc, name + "_proj") as pr:
            project_self(nc, g, pr, w, w_loaded, rope, qt, kt, v, wos, wo, wo_loaded, masks, mask)
        with Stage(nc, name + "_core") as co:
            attention_core(nc, g, co, qt, kt, v, ot, S // P, masks)
        with Stage(nc, name + "_out") as ou:
            made, added = ou.sem("made"), ou.sem("added")
            with nc.Block() as block:
                @block.tensor
                def _(pe):
                    pe.wait_ge(wo_loaded, 16)
                    for t in range(NT):
                        b, s = divmod(t * P, S)
                        if t >= 4:
                            pe.wait_ge(added, t - 3)
                        for k in range(KC):
                            mm = nc.tensor.matmul(g.ps[:, t % 4, :], ot[:, b * KC + k, s:s + P], wos[:, k, :],
                                                  start=(k == 0), stop=(k == KC - 1))
                        mm.then_inc(made, 1)

                @block.vector
                def _(dve):
                    for t in range(NT):
                        dve.wait_ge(made, t + 1)
                        nc.vector.tensor_tensor(g.x[:, t, :], g.x[:, t, :], g.ps[:, t % 4, :],
                                                ALU.add).then_inc(added, 1)


def project_self(nc, g, st, w, w_loaded, rope, qt, kt, v, wos, wo, wo_loaded, masks, mask):
    made, copied = st.sem("made"), st.sem("copied")
    v_made, v_copied = st.sem("v_made"), st.sem("v_copied")
    units = [(c, b, dst, part) for part, dst in enumerate((qt, kt)) for c in range(KC) for b in range(B)]
    RAW = 3
    if rope:
        cos, sin, swap = st.sbuf("cos", [P, S]), st.sbuf("sin", [P, S]), st.sbuf("swap", [P, P])
        raw, rc, rs = st.sbuf("raw", [P, RAW, S]), st.sbuf("rc", [P, 2, S]), st.sbuf("rs", [P, 2, S])
        swapped, cos_done, sin_done, rotated = (st.sem("swapped"), st.sem("cos_done"), st.sem("sin_done"),
                                                st.sem("rotated"))
    r_loaded = st.sem("r_loaded")
    with nc.Block() as block:
        @block.sync
        def _(sp):
            if rope:
                sp.dma_start(cos[:, :], rope[0]).then_inc(r_loaded, 16)
                sp.dma_start(sin[:, :], rope[1]).then_inc(r_loaded, 16)
                sp.dma_start(swap[:, :], rope[2]).then_inc(r_loaded, 16)
            sp.dma_start(wos[:, :, :], wo.rearrange("(k p) n -> p k n", p=P)).then_inc(wo_loaded, 16)
            sp.dma_start(masks[:, :], mask).then_inc(wo_loaded, 16)
            sp.wait_ge(wo_loaded, 32)

        @block.tensor
        def _(pe):
            def swap_pairs(j):
                pe.wait_ge(copied, j + 1)
                if j == 0:
                    pe.wait_ge(r_loaded, 48)
                if j >= 2:
                    pe.wait_ge(sin_done, j - 1)
                nc.tensor.matmul(g.ps[:, 4 + j % 2, :], swap[:, :], raw[:, j % RAW, :], start=True,
                                 stop=True).then_inc(swapped, 1)

            for j, (c, b, dst, part) in enumerate(units):
                if j % 8 == 0:
                    pe.wait_ge(w_loaded[part], 16)
                if j >= 4:
                    pe.wait_ge(copied, j - 3)
                for k in range(KC):
                    mm = nc.tensor.matmul(g.ps[:, j % 4, :], w[:, k, part * D + c * P:part * D + (c + 1) * P],
                                          g.xt[:, k, b * S:(b + 1) * S], start=(k == 0), stop=(k == KC - 1))
                mm.then_inc(made, 1)
                if rope and j >= 1:
                    swap_pairs(j - 1)
            if rope:
                swap_pairs(len(units) - 1)
            pe.wait_ge(w_loaded[2], 16)
            for t in range(NT):
                if t >= 2:
                    pe.wait_ge(v_copied, t - 1)
                for k in range(KC):
                    mm = nc.tensor.matmul(g.ps[:, 6 + t % 2, :], g.xt[:, k, t * P:(t + 1) * P], w[:, k, 2 * D:3 * D],
                                          start=(k == 0), stop=(k == KC - 1))
                mm.then_inc(v_made, 1)

        @block.scalar
        def _(act):
            for j, (c, b, dst, part) in enumerate(units):
                act.wait_ge(made, j + 1)
                if rope and j >= RAW:
                    act.wait_ge(cos_done, j - RAW + 1)
                    act.wait_ge(swapped, j - RAW + 1)
                out = raw[:, j % RAW, :] if rope else dst[:, b * KC + c, :]
                nc.scalar.activation(out, g.ps[:, j % 4, :], ACT.Copy,
                                     scale=DH ** -0.5 if part == 0 else 1.0).then_inc(copied, 1)
            for t in range(NT):
                b, kb = divmod(t, S // P)
                act.wait_ge(v_made, t + 1)
                nc.scalar.activation(v[:, b * KC:(b + 1) * KC, kb, :],
                                     g.ps[:, 6 + t % 2, :].rearrange("p (c d) -> p c d", c=KC),
                                     ACT.Copy).then_inc(v_copied, 1)

        if rope:
            @block.gpsimd
            def _(pool):
                pool.wait_ge(r_loaded, 48)
                for j in range(len(units)):
                    pool.wait_ge(copied, j + 1)
                    if j >= 2:
                        pool.wait_ge(rotated, j - 1)
                    nc.gpsimd.tensor_tensor(rc[:, j % 2, :], raw[:, j % RAW, :], cos[:, :],
                                            ALU.mult).then_inc(cos_done, 1)

            @block.vector
            def _(dve):
                dve.wait_ge(r_loaded, 48)
                for j, (c, b, dst, part) in enumerate(units):
                    dve.wait_ge(swapped, j + 1)
                    nc.vector.tensor_tensor(rs[:, j % 2, :], g.ps[:, 4 + j % 2, :], sin[:, :],
                                            ALU.mult).then_inc(sin_done, 1)
                    dve.wait_ge(sin_done, j + 1)
                    dve.wait_ge(cos_done, j + 1)
                    nc.vector.tensor_tensor(dst[:, b * KC + c, :], rc[:, j % 2, :], rs[:, j % 2, :],
                                            ALU.add).then_inc(rotated, 1)


def attention_core(nc, g, st, qt, kt, v, ot, nkt, masks=None):
    causal = masks is not None
    NI, U, QB = B * KC, HPC * (S // P), S // P
    NK = nkt * P
    SB = 4 if causal else 2
    sbank = (lambda k: k % SB) if causal else (lambda k: 2 * (k % SB))
    SKEW = 5 if causal else 3
    SPLIT = 4 if causal else 6
    PR = 8 if causal else 4
    HALVES = 1 if causal else 2
    LAG = 3 if causal else 1
    KB = NK // S
    parts = st.sbuf("parts", [P, 2 + 2 * KB, S], F32R)
    packed = st.sbuf("packed", [P, HPC, 1 + KB, S], F32R)
    high = [parts[:, 0, :], parts[:, 2:2 + KB, :].rearrange("p a n -> p (a n)")]
    low = [parts[:, 1, :], parts[:, 2 + KB:2 + 2 * KB, :].rearrange("p a n -> p (a n)")]
    moves = []
    for r, (qp, kp) in enumerate(((0, 0), (1, 0), (0, 1), (1, 1))):
        if KB == 1:
            moves.append((r, slice(0, 2), slice(qp, 3 + kp, 2 + kp - qp)))
        else:
            moves.append((r, slice(0, 1), slice(qp, qp + 1)))
            moves.append((r, slice(1, 1 + KB), slice(2 + KB * kp, 2 + KB * (kp + 1))))
    PACK = 16 * len(moves)
    vm = st.sbuf("vm", [P, nkt, P])
    prob = g.xt[:, :, :].rearrange("p k (a n) -> p (k a) n", n=NK)
    pt = st.sbuf("pt", [P, 2, nkt, S])
    nmax, rsum, rinv = st.sbuf("nmax", [P, PR]), st.sbuf("rsum", [P, PR]), st.sbuf("rinv", [P, PR])
    scores = st.sem("scores")
    max_done = st.sem("max_done")
    exp_done = st.sem("exp_done")
    rinv_done = st.sem("rinv_done")
    prob_done = st.sem("prob_done")
    turned = [st.sem(f"turned{n}") for n in range(HALVES)]
    pt_done = [st.sem(f"pt_done{n}") for n in range(HALVES)]
    pv_done = st.sem("pv_done")
    ot_done = st.sem("ot_done")
    high_done = st.sem("high_done")
    low_done = st.sem("low_done")
    packed_in = [st.sem(f"packed_in{h}") for h in range(HPC)]
    vm_done = st.sem("vm_done")
    width = (lambda qb: (qb + 1) * P) if causal else (lambda qb: NK)

    def s_ps(k, n):
        return g.ps[:, sbank(k):sbank(k) + (1 if causal else 2), :].rearrange("p a n -> p (a n)")[:, 0:n]

    def t_bank(k, half):
        return 4 + k % 2 if causal else 4 + half

    with nc.Block() as block:
        @block.sync
        def _(sp):
            def pack(i, first=False):
                sp.wait_ge(low_done, 2 * i + 2)
                for h in range(HPC):
                    if not first:
                        sp.wait_ge(scores, U * (i - 1) + QB * (h + 1))
                    for r, dst, src in moves:
                        sp.dma_start(packed[r * DH:(r + 1) * DH, h, dst, :].bitcast(F32),
                                     parts[h * DH:(h + 1) * DH, src, :].bitcast(F32)).then_inc(packed_in[h], 16)

            pack(0, first=True)
            with sp.Fori(1, NI) as i:
                pack(i)

        @block.tensor
        def _(pe):
            def step(i, k, first=False, tail=False):
                u = U * i + k
                h, qb = divmod(k, QB)
                if not tail:
                    if qb == 0:
                        pe.wait_ge(packed_in[h], PACK * (i + 1))
                    if not (first and k < SB):
                        pe.wait_ge(exp_done, u - SB + 1)
                    n = width(qb)
                    for a in range(0, n, 512):
                        e = min(n, a + 512)
                        mm = nc.tensor.matmul(s_ps(k, n)[:, a:e], packed[:, h, 0, qb * P:(qb + 1) * P],
                                              packed[:, h, 1 + a // S, 0:e - a],
                                              start=True, stop=not causal)
                    if causal:
                        mm = nc.tensor.matmul(s_ps(k, n)[:, qb * P:n], g.ident[:, :], masks[:, :], start=False,
                                              stop=True)
                    mm.then_inc(scores, 1)
                kk = k - SKEW
                if first and kk < 0:
                    return
                w = u - SKEW
                if not tail or kk < U:
                    wq = kk % QB
                    pe.wait_ge(prob_done, w + 1)
                    for half in range(HALVES):
                        if causal:
                            if not (first and kk < 2):
                                pe.wait_ge(pt_done[0], w - 1)
                            tiles = range(wq + 1)
                        else:
                            if not (first and kk < 1):
                                pe.wait_ge(pt_done[half], w)
                            tiles = range(4 * half, 4 * half + 4)
                        for n, j in enumerate(tiles):
                            mm = nc.tensor.transpose(g.ps[:, t_bank(kk, half), n * P:(n + 1) * P],
                                                     prob[:, kk % PR, j * P:(j + 1) * P], g.ident[:, :])
                        mm.then_inc(turned[half], 1)
                if kk % QB == LAG and not (first and kk < QB):
                    hh = (kk // QB - 1) % HPC
                    heads = HPC * i + kk // QB
                    for half in range(HALVES):
                        pe.wait_ge(pt_done[half], w - LAG)
                    pe.wait_ge(vm_done, heads)
                    if hh == 0 and not first:
                        pe.wait_ge(ot_done, i)
                    for j in range(nkt):
                        a = j * P if causal else 0
                        mm = nc.tensor.matmul(g.ps[hh * DH:(hh + 1) * DH, 6, a:S], vm[:, j, hh * DH:(hh + 1) * DH],
                                              pt[:, hh % 2, j, a:S], start=(j == 0), stop=(j == nkt - 1))
                    mm.then_inc(pv_done, 1)

            for k in range(U):
                step(0, k, first=True)
            with pe.Fori(1, NI) as i:
                for k in range(U):
                    step(i, k)
            for k in range(U, U + SKEW + LAG + 1):
                step(NI - 1, k, tail=True)

        @block.vector
        def _(dve):
            def low_parts(i):
                for x, hi, lo in zip((qt, kt), high, low):
                    nc.vector.tensor_tensor(lo, x[:, i, :], hi, ALU.subtract).then_inc(low_done, 1)

            def step(i, k, first=False, tail=False, last=False):
                u = U * i + k
                if not tail:
                    dve.wait_ge(scores, u + 1)
                    nc.vector.tensor_reduce(nmax[:, k % PR:k % PR + 1], s_ps(k, width(k % QB)), X_AXIS, ALU.max,
                                            negate=True).then_inc(max_done, 1)
                if not (first and k < 1) and k <= U:
                    dve.wait_ge(exp_done, u)
                    s = (k - 1) % PR
                    nc.vector.reciprocal(rinv[:, s:s + 1], rsum[:, s:s + 1]).then_inc(rinv_done, 1)
                kk = k - SKEW
                if (first and kk < 0) or kk >= U:
                    return
                w = u - SKEW
                hh, wq = divmod(kk % U, QB)
                if k == SPLIT + 2 and not last:
                    dve.wait_ge(high_done, 2 * i + 4)
                dve.wait_ge(turned[0], w + 1)
                if wq == 0 and not (first and hh < 2):
                    dve.wait_ge(pv_done, HPC * i + kk // QB - 1)
                n = wq + 1 if causal else 4
                nc.vector.tensor_copy(pt[:, hh % 2, 0:n, wq * P:(wq + 1) * P],
                                      g.ps[:, t_bank(kk, 0), 0:n * P].rearrange("p (j q) -> p j q", j=n)
                                      ).then_inc(pt_done[0], 1)
                if k == SPLIT + 2 and not last:
                    low_parts(i + 1)

            dve.wait_ge(high_done, 2)
            low_parts(0)
            for k in range(U):
                step(0, k, first=True)
            with dve.Fori(1, NI - 1) as i:
                for k in range(U):
                    step(i, k)
            for k in range(U):
                step(NI - 1, k, last=True)
            for k in range(U, U + SKEW):
                step(NI - 1, k, tail=True)

        @block.scalar
        def _(act):
            def store(iters):
                act.wait_ge(pv_done, HPC * iters)
                nc.scalar.activation(ot[:, iters - 1, :], g.ps[:, 6, :], ACT.Copy).then_inc(ot_done, 1)

            def high_parts(i):
                for x, hi in zip((qt, kt), high):
                    nc.scalar.activation(hi, x[:, i, :], ACT.Copy).then_inc(high_done, 1)

            def step(i, k, first=False, tail=False, last=False):
                u = U * i + k
                if not tail:
                    if k == SPLIT and not last:
                        for h in range(HPC):
                            act.wait_ge(packed_in[h], PACK * (i + 1))
                    act.wait_ge(max_done, u + 1)
                    if not (first and k < PR):
                        for half in range(HALVES):
                            act.wait_ge(turned[half], u - PR + 1)
                    s = k % PR
                    n = width(k % QB)
                    nc.scalar.activation(prob[:, s, 0:n], s_ps(k, n), ACT.Exp, bias=nmax[:, s:s + 1],
                                         accum_out=rsum[:, s:s + 1]).then_inc(exp_done, 1)
                    if k == SPLIT and not last:
                        high_parts(i + 1)
                kk = k - SKEW
                if not causal and not (first and kk < 0) and kk < U:
                    w = u - SKEW
                    hh, wq = divmod(kk % U, QB)
                    act.wait_ge(turned[1], w + 1)
                    if wq == 0 and not (first and hh < 2):
                        act.wait_ge(pv_done, HPC * i + kk // QB - 1)
                    nc.scalar.activation(pt[:, hh % 2, 4:8, wq * P:(wq + 1) * P],
                                         g.ps[:, t_bank(kk, 1), :].rearrange("p (j q) -> p j q", j=4),
                                         ACT.Copy).then_inc(pt_done[1], 1)
                if k == SKEW + LAG + 2 and not first and not tail:
                    store(i)

            high_parts(0)
            for k in range(U):
                step(0, k, first=True)
            with act.Fori(1, NI - 1) as i:
                for k in range(U):
                    step(i, k)
            for k in range(U):
                step(NI - 1, k, last=True)
            for k in range(U, U + SKEW):
                step(NI - 1, k, tail=True)
            store(NI)

        @block.gpsimd
        def _(pool):
            def put_v(i, h):
                nc.gpsimd.tensor_copy(vm[:, :, h * DH:(h + 1) * DH], v[:, i, :, h * DH:(h + 1) * DH]).then_inc(vm_done, 1)

            def step(i, k, first=False, last=False):
                u = U * i + k
                h, qb = divmod(k, QB)
                n = width(qb)
                pool.wait_ge(rinv_done, u + 1)
                nc.gpsimd.tensor_tensor(prob[:, k % PR, 0:n], prob[:, k % PR, 0:n],
                                        rinv[:, k % PR:k % PR + 1].to_broadcast([P, n]), ALU.mult).then_inc(prob_done, 1)
                if qb == QB - 1:
                    if h < 2 and not first:
                        pool.wait_ge(pv_done, HPC * (i - 1) + h + 3)
                        put_v(i, h + 2)
                    if h >= 2 and not last:
                        pool.wait_ge(pv_done, HPC * i + h - 1)
                        put_v(i + 1, h - 2)

            for h in range(HPC):
                put_v(0, h)
            for k in range(U):
                step(0, k, first=True)
            with pool.Fori(1, NI - 1) as i:
                for k in range(U):
                    step(i, k)
            for k in range(U):
                step(NI - 1, k, last=True)


def cross_attention0(nc, g, name, ctxt, wq, bq_cols, wkvt, bk_cols, bkv, wp, bp):
    xn = g.xt[:, :, :].rearrange("p k (a d) -> p (k a) d", d=D)
    NKT = CTX // P
    with Stage(nc, name) as st:
        qt = st.sbuf("qt", [P, B * KC, S])
        kt = st.sbuf("kt", [P, B * KC, CTX])
        v = st.sbuf("v", [P, B * KC, NKT, P])
        wpt = st.sbuf("wpt", [P, KC, D], BF16)
        wp_scale = st.sbuf("wp_scale", [P, KC])
        with Stage(nc, name + "_proj") as pr:
            project_cross0(nc, g, pr, xn, ctxt, wq, bq_cols, wkvt, bk_cols, bkv, wp, qt, kt, v, wpt, wp_scale)
        ot = st.sbuf("ot", [P, B * KC, S])
        with Stage(nc, name + "_core") as co:
            attention_core(nc, g, co, qt, kt, v, ot, NKT)
        with Stage(nc, name + "_out") as ou:
            output_cross0(nc, g, ou, ot, wpt, wp_scale, bp)


def project_cross0(nc, g, st, xn, ctxt, wq, bq_cols, wkvt, bk_cols, bkv, wp, qt, kt, v, wpt, wp_scale):
    NKT = CTX // P
    NCH = B * CTX // 512
    RING = 2
    w_rows = [st.sbuf("wq_rows", [P, KC, D]), st.sbuf("wp_rows", [P, KC, D])]
    w_int = [st.sbuf("wq_int", [P, KC, D], BF16), st.sbuf("wp_int", [P, KC, D], BF16)]
    wqt = st.sbuf("wqt", [P, KC, D], BF16)
    wts = [wqt, wpt]
    wq_scale = st.sbuf("wq_scale", [P, KC])
    wkv = st.sbuf("wkv", [P, KC, 2 * D])
    ctx = st.sbuf("ctx", [P, RING, KC, 512])
    x_int = st.sbuf("x_int", [P, NT, D], BF16)
    xqt = st.sbuf("xqt", [P, KC, T], BF16)
    rounded = st.sbuf("rounded", [P, 2, D])
    top = st.sbuf("top", [P, NT + 2 * KC])
    scale = st.sbuf("scale", [P, NT + 2 * KC])
    inv = st.sbuf("inv", [P, NT + 2 * KC])
    diag = st.sbuf("diag", [P, 2, P])
    xs_row = st.sbuf("xs_row", [P, T])
    bqs, bks = st.sbuf("bqs", [P, KC]), st.sbuf("bks", [P, KC])
    bqss = st.sbuf("bqss", [P, KC])
    bv = st.sbuf("bv", [P, D])
    qs = rounded
    w_loaded = [st.sem("wq_loaded"), st.sem("wp_loaded")]
    wkv_loaded, b_loaded = st.sem("wkv_loaded"), st.sem("b_loaded")
    ctx_loaded = [st.sem(f"ctx_loaded{n}") for n in range(RING)]
    tops, scaled, inverted, shifted, clipped = (st.sem("tops"), st.sem("scaled"), st.sem("inverted"),
                                                st.sem("shifted"), st.sem("clipped"))
    ints = st.sem("ints")
    turned, turned_done = st.sem("turned"), st.sem("turned_done")
    diag_done, row_made, row_done = st.sem("diag_done"), st.sem("row_made"), st.sem("row_done")
    q_made, q_scaled, q_done, bias_done = st.sem("q_made"), st.sem("q_scaled"), st.sem("q_done"), st.sem("bias_done")
    k_made, k_done, v_made, v_done = st.sem("k_made"), st.sem("k_done"), st.sem("v_made"), st.sem("v_done")
    jobs = [(w_rows[0][:, c, :], w_int[0][:, c, :], c) for c in range(KC)]
    jobs += [(xn[:, t, :], x_int[:, t, :], KC + t) for t in range(NT)]
    jobs += [(w_rows[1][:, c, :], w_int[1][:, c, :], KC + NT + c) for c in range(KC)]
    NJ = len(jobs)

    def load_chunk(sp, n):
        sp.dma_start(ctx[:, n % RING, :, :], ctxt[:, n * 512:(n + 1) * 512].rearrange("(k p) n -> p k n", p=P)
                     ).then_inc(ctx_loaded[n % RING], 16)

    def load_first(sp):
        sp.dma_start(wkv[:, :, 0:D], wkvt[:, 0:D].rearrange("(k p) n -> p k n", p=P)).then_inc(wkv_loaded, 16)
        load_chunk(sp, 0)
        sp.dma_start(bks[:, :], bk_cols).then_inc(b_loaded, 16)
        sp.dma_start(bqs[:, :], bq_cols).then_inc(b_loaded, 16)
        sp.dma_start(bv[:, :], bkv[D:2 * D].partition_broadcast(P)).then_inc(b_loaded, 16)
        sp.dma_start(wkv[:, :, D:2 * D], wkvt[:, D:2 * D].rearrange("(k p) n -> p k n", p=P)).then_inc(wkv_loaded, 16)
        for n, src in enumerate((wq, wp)):
            sp.dma_start(w_rows[n][:, :, :], src.rearrange("(c p) n -> p c n", p=P)).then_inc(w_loaded[n], 16)
        load_chunk(sp, 1)

    layer_norm(nc, g, st.name + "_ln", turn=False, prefetch=load_first)
    with nc.Block() as block:
        @block.sync
        def _(sp):
            for n in range(RING, NCH):
                sp.wait_ge(k_made, KC * (n - RING + 1))
                sp.wait_ge(v_made, 4 * (n - RING + 1))
                load_chunk(sp, n)

        @block.vector
        def _(dve):
            def round_rows(first, n, group):
                for j in range(first, first + n):
                    nc.vector.tensor_reduce(top[:, j:j + 1], jobs[j][0], X_AXIS, ALU.max,
                                            apply_absolute_value=True).then_inc(tops, 1)
                dve.wait_ge(tops, first + n)
                nc.vector.tensor_scalar(scale[:, first:first + n], top[:, first:first + n], 1.0 / 127.0, 1e-8,
                                        ALU.mult, ALU.max).then_inc(scaled, 1)
                dve.wait_ge(scaled, group + 1)
                nc.vector.reciprocal(inv[:, first:first + n], scale[:, first:first + n]).then_inc(inverted, 1)
                dve.wait_ge(inverted, group + 1)
                for j in range(first, first + n):
                    if j >= 2:
                        dve.wait_ge(ints, j - 1)
                    nc.vector.tensor_scalar(rounded[:, j % 2, :], jobs[j][0], inv[:, j:j + 1], ROUND, ALU.mult,
                                            ALU.add).then_inc(shifted, 1)
                    dve.wait_ge(shifted, j + 1)
                    nc.vector.tensor_scalar(rounded[:, j % 2, :], rounded[:, j % 2, :], ROUND - 127.0, ROUND + 127.0,
                                            ALU.max, ALU.min).then_inc(clipped, 1)

            def values(n):
                for t in range(4):
                    m = 4 * n + t
                    b, kb = divmod(m, NKT)
                    dve.wait_ge(v_made, m + 1)
                    nc.vector.tensor_tensor(v[:, b * KC:(b + 1) * KC, kb, :],
                                            g.ps[:, 4 + m % 2, :].rearrange("p (c d) -> p c d", c=KC),
                                            bv[:, :].rearrange("p (c d) -> p c d", c=KC), ALU.add).then_inc(v_done, 1)

            dve.wait_ge(b_loaded, 48)
            nc.vector.tensor_scalar(bqss[:, :], bqs[:, :], DH ** -0.5, None, ALU.mult).then_inc(bias_done, 1)
            values(0)
            dve.wait_ge(w_loaded[0], 16)
            round_rows(0, KC, 0)
            values(1)
            round_rows(KC, NT, 1)
            values(2)
            dve.wait_ge(w_loaded[1], 16)
            round_rows(KC + NT, KC, 2)
            nc.vector.tensor_copy(wp_scale[:, :], scale[:, KC + NT:NJ]).then_inc(bias_done, 1)
            nc.vector.tensor_copy(wq_scale[:, :], scale[:, 0:KC]).then_inc(bias_done, 1)
            values(3)
            for t in range(NT):
                if t >= 2:
                    dve.wait_ge(row_made, t - 1)
                nc.vector.tensor_scalar(diag[:, t % 2, :], g.ident[:, :], scale[:, KC + t:KC + t + 1], None,
                                        ALU.mult).then_inc(diag_done, 1)
            dve.wait_ge(bias_done, 3)
            dve.wait_ge(row_done, 2)
            for j in range(2 * KC):
                c, b = divmod(j, B)
                dve.wait_ge(q_made, j + 1)
                if j >= 2:
                    dve.wait_ge(q_done, j - 1)
                nc.vector.scalar_tensor_tensor(qs[:, j % 2, :], g.ps[:, j % 4, :], wq_scale[:, c:c + 1],
                                               xs_row[:, b * S:(b + 1) * S], ALU.mult, ALU.mult).then_inc(q_scaled, 1)

        @block.scalar
        def _(act):
            def keys(n):
                b, half = divmod(n, CTX // 512)
                for c in range(KC):
                    m = KC * n + c
                    act.wait_ge(k_made, m + 1)
                    nc.scalar.activation(kt[:, b * KC + c, half * 512:(half + 1) * 512], g.ps[:, m % 4, :], ACT.Identity,
                                         bias=bks[:, c:c + 1]).then_inc(k_done, 1)

            def whole(first, n):
                for j in range(first, first + n):
                    act.wait_ge(clipped, j + 1)
                    nc.scalar.activation(jobs[j][1], rounded[:, j % 2, :], ACT.Copy, bias=-ROUND).then_inc(ints, 1)

            def turn(n, dst):
                act.wait_ge(turned, n + 1)
                nc.scalar.activation(dst, g.ps[:, 6 + n % 2, 0:256].bitcast(BF16).rearrange("p (k c) -> p k c", k=KC),
                                     ACT.Copy).then_inc(turned_done, 1)

            act.wait_ge(b_loaded, 48)
            keys(0)
            whole(0, KC)
            keys(1)
            whole(KC, NT)
            keys(2)
            whole(KC + NT, KC)
            keys(3)
            for n, c in enumerate(range(KC)):
                turn(n, wqt[:, :, c * P:(c + 1) * P])
            for t in range(NT):
                turn(KC + t, xqt[:, :, t * P:(t + 1) * P])
            for c in range(KC):
                turn(KC + NT + c, wpt[:, :, c * P:(c + 1) * P])
            for n in range(2):
                act.wait_ge(row_made, 4 * (n + 1))
                nc.scalar.activation(xs_row[:, n * 512:(n + 1) * 512], g.ps[:, 4 + n, :], ACT.Copy).then_inc(row_done, 1)
            act.wait_ge(bias_done, 1)
            for j in range(2 * KC):
                c, b = divmod(j, B)
                act.wait_ge(q_scaled, j + 1)
                nc.scalar.activation(qt[:, b * KC + c, :], qs[:, j % 2, :], ACT.Identity, bias=bqss[:, c:c + 1],
                                     scale=DH ** -0.5).then_inc(q_done, 1)

        @block.tensor
        def _(pe):
            for n in range(NCH):
                pe.wait_ge(ctx_loaded[n % RING], 16 * (n // RING + 1))
                pe.wait_ge(wkv_loaded, 32)
                for c in range(KC):
                    m = KC * n + c
                    if m >= 4:
                        pe.wait_ge(k_done, m - 3)
                    for k in range(KC):
                        mm = nc.tensor.matmul(g.ps[:, m % 4, :], wkv[:, k, c * P:(c + 1) * P], ctx[:, n % RING, k, :],
                                              start=(k == 0), stop=(k == KC - 1))
                    mm.then_inc(k_made, 1)
                for t in range(4):
                    m = 4 * n + t
                    if m >= 2:
                        pe.wait_ge(v_done, m - 1)
                    for k in range(KC):
                        mm = nc.tensor.matmul(g.ps[:, 4 + m % 2, :], ctx[:, n % RING, k, t * P:(t + 1) * P],
                                              wkv[:, k, D:2 * D], start=(k == 0), stop=(k == KC - 1))
                    mm.then_inc(v_made, 1)
            for n, (_, whole, _) in enumerate(jobs):
                pe.wait_ge(ints, n + 1)
                if n >= 2:
                    pe.wait_ge(turned_done, n - 1)
                for k in range(KC):
                    mm = nc.tensor.transpose(g.ps[:, 6 + n % 2, 0:256].bitcast(BF16)[:, k * P:(k + 1) * P],
                                             whole[:, k * P:(k + 1) * P], g.ident16[:, :])
                mm.then_inc(turned, 1)
            for t in range(NT):
                pe.wait_ge(diag_done, t + 1)
                if t == 0:
                    pe.wait_ge(v_done, B * NKT)
                nc.tensor.matmul(g.ps[:, 4 + t // 4, t % 4 * P:(t % 4 + 1) * P], g.ones[:, :], diag[:, t % 2, :],
                                 start=True, stop=True).then_inc(row_made, 1)
            pe.wait_ge(turned_done, NJ)
            pe.wait_ge(k_done, KC * NCH)
            for j in range(2 * KC):
                c, b = divmod(j, B)
                if j >= 4:
                    pe.wait_ge(q_scaled, j - 3)
                for k in range(KC):
                    mm = nc.tensor.matmul(g.ps[:, j % 4, :], wqt[:, k, c * P:(c + 1) * P],
                                          xqt[:, k, b * S:(b + 1) * S], start=(k == 0), stop=(k == KC - 1))
                mm.then_inc(q_made, 1)


def output_cross0(nc, g, st, ot, wpt, wp_scale, bp):
    o_int = st.sbuf("o_int", [P, NT, D], BF16)
    oqt = st.sbuf("oqt", [P, NT, KC, P], BF16)
    rounded = st.sbuf("rounded", [P, NT, D])
    top, scale, inv = st.sbuf("top", [P, NT]), st.sbuf("scale", [P, NT]), st.sbuf("inv", [P, NT])
    diag = st.sbuf("diag", [P, KC, P])
    ws_row, bps = st.sbuf("ws_row", [P, D]), st.sbuf("bps", [P, D])
    y = st.sbuf("y", [P, 2, D])
    b_loaded, diag_done, row_made, row_done = st.sem("b_loaded"), st.sem("diag_done"), st.sem("row_made"), st.sem("row_done")
    rows, tops, scaled, inverted = st.sem("rows"), st.sem("tops"), st.sem("scaled"), st.sem("inverted")
    shifted, clipped, ints = st.sem("shifted"), st.sem("clipped"), st.sem("ints")
    turned, turned_done, made, y_done, added = (st.sem("turned"), st.sem("turned_done"), st.sem("made"),
                                                st.sem("y_done"), st.sem("added"))
    biased = st.sem("biased")
    with nc.Block() as block:
        @block.sync
        def _(sp):
            sp.dma_start(bps[:, :], bp.partition_broadcast(P)).then_inc(b_loaded, 16)

        @block.gpsimd
        def _(pool):
            pool.wait_ge(b_loaded, 16)
            for t in range(NT):
                nc.gpsimd.tensor_tensor(g.x[:, t, :], g.x[:, t, :], bps[:, :], ALU.add).then_inc(biased, 1)

        def project(pe, t):
            pe.wait_ge(turned_done, t + 1)
            if t >= 2:
                pe.wait_ge(y_done, t - 1)
            for k in range(KC):
                mm = nc.tensor.matmul(g.ps[:, 2 + t % 2, :], oqt[:, t, k, :], wpt[:, k, :], start=(k == 0),
                                      stop=(k == KC - 1))
            mm.then_inc(made, 1)

        @block.tensor
        def _(pe):
            for c in range(KC):
                pe.wait_ge(diag_done, c + 1)
                mm = nc.tensor.matmul(g.ps[:, 7, c * P:(c + 1) * P], g.ones[:, :], diag[:, c, :], start=True, stop=True)
            mm.then_inc(row_made, 1)
            pe.wait_ge(row_done, 1)
            for t in range(NT):
                b, s = divmod(t * P, S)
                for k in range(KC):
                    mm = nc.tensor.transpose(g.ps[:, t, k * P:(k + 1) * P], ot[:, b * KC + k, s:s + P], g.ident[:, :])
                mm.then_inc(rows, 1)
            for t in range(NT):
                pe.wait_ge(ints, t + 1)
                if t == 0:
                    pe.wait_ge(clipped, 4)
                if t >= 2:
                    pe.wait_ge(turned_done, t - 1)
                for k in range(KC):
                    mm = nc.tensor.transpose(g.ps[:, t % 2, 0:256].bitcast(BF16)[:, k * P:(k + 1) * P],
                                             o_int[:, t, k * P:(k + 1) * P], g.ident16[:, :])
                mm.then_inc(turned, 1)
                if t >= 1:
                    project(pe, t - 1)
            project(pe, NT - 1)

        @block.vector
        def _(dve):
            for c in range(KC):
                nc.vector.tensor_scalar(diag[:, c, :], g.ident[:, :], wp_scale[:, c:c + 1], None,
                                        ALU.mult).then_inc(diag_done, 1)
            for t in range(NT):
                dve.wait_ge(rows, t + 1)
                nc.vector.tensor_reduce(top[:, t:t + 1], g.ps[:, t, :], X_AXIS, ALU.max,
                                        apply_absolute_value=True).then_inc(tops, 1)
            dve.wait_ge(tops, NT)
            nc.vector.tensor_scalar(scale[:, :], top[:, :], 1.0 / 127.0, 1e-8, ALU.mult, ALU.max).then_inc(scaled, 1)
            dve.wait_ge(scaled, 1)
            nc.vector.reciprocal(inv[:, :], scale[:, :]).then_inc(inverted, 1)
            dve.wait_ge(inverted, 1)
            for t in range(NT):
                nc.vector.tensor_scalar(rounded[:, t, :], g.ps[:, t, :], inv[:, t:t + 1], ROUND, ALU.mult,
                                        ALU.add).then_inc(shifted, 1)
                dve.wait_ge(shifted, t + 1)
                nc.vector.tensor_scalar(rounded[:, t, :], rounded[:, t, :], ROUND - 127.0, ROUND + 127.0, ALU.max,
                                        ALU.min).then_inc(clipped, 1)
            for t in range(NT):
                dve.wait_ge(made, t + 1)
                if t == 0:
                    dve.wait_ge(row_done, 1)
                nc.vector.scalar_tensor_tensor(y[:, t % 2, :], g.ps[:, 2 + t % 2, :], scale[:, t:t + 1], ws_row[:, :],
                                               ALU.mult, ALU.mult).then_inc(y_done, 1)
                dve.wait_ge(y_done, t + 1)
                dve.wait_ge(biased, t + 1)
                nc.vector.tensor_tensor(g.x[:, t, :], g.x[:, t, :], y[:, t % 2, :], ALU.add).then_inc(added, 1)

        def put(act, t):
            act.wait_ge(turned, t + 1)
            nc.scalar.activation(oqt[:, t, :, :],
                                 g.ps[:, t % 2, 0:256].bitcast(BF16).rearrange("p (k c) -> p k c", k=KC),
                                 ACT.Copy).then_inc(turned_done, 1)

        @block.scalar
        def _(act):
            act.wait_ge(row_made, 1)
            nc.scalar.activation(ws_row[:, :], g.ps[:, 7, :], ACT.Copy).then_inc(row_done, 1)
            for t in range(NT):
                act.wait_ge(clipped, t + 1)
                nc.scalar.activation(o_int[:, t, :], rounded[:, t, :], ACT.Copy, bias=-ROUND).then_inc(ints, 1)
                if t >= 1:
                    put(act, t - 1)
            put(act, NT - 1)



def router(nc, g, st, wr, bias, experts, top_k, gates, iota_e, pick, best):
    w = st.sbuf("w", [P, KC, experts])
    bs = st.sbuf("bs", [P, experts])
    logit = st.sbuf("logit", [P, NT, experts])
    top = st.sbuf("top", [P, NT])
    total, inv = st.sbuf("total", [P, NT]), st.sbuf("inv", [P, NT])
    at, atf = st.sbuf("at", [P, NT, 8], U32), st.sbuf("atf", [P, NT, 8])
    ksum, kinv = st.sbuf("ksum", [P, NT]), st.sbuf("kinv", [P, NT])
    part = st.sbuf("part", [P, NT, experts])
    iota = st.sbuf("iota", [P, experts])
    loaded, made, exped, step = st.sem("loaded"), st.sem("made"), st.sem("exped"), st.sem("step")
    shape = [P, NT, experts]

    def over(a):
        return a.rearrange("p (t o) -> p t o", o=1).to_broadcast(shape)

    with nc.Block() as block:
        @block.sync
        def _(sp):
            sp.dma_start(w[:, :, :], wr.rearrange("(k p) e -> p k e", p=P)).then_inc(loaded, 16)
            sp.dma_start(iota[:, :], iota_e[0:experts].partition_broadcast(P)).then_inc(loaded, 16)
            if bias is not None:
                sp.dma_start(bs[:, :], bias.partition_broadcast(P)).then_inc(loaded, 16)

        @block.tensor
        def _(pe):
            pe.wait_ge(loaded, 32 if bias is None else 48)
            for t in range(NT):
                for k in range(KC):
                    mm = nc.tensor.matmul(g.ps[:, 0, t * experts:(t + 1) * experts], g.xt[:, k, t * P:(t + 1) * P],
                                          w[:, k, :], start=(k == 0), stop=(k == KC - 1))
            mm.then_inc(made, 1)

        @block.scalar
        def _(act):
            act.wait_ge(step, 3)
            nc.scalar.activation(logit[:, :, :], logit[:, :, :], ACT.Exp).then_inc(exped, 1)

        @block.vector
        def _(dve):
            done = [0]

            def then(ins):
                ins.then_inc(step, 1)
                done[0] += 1
                dve.wait_ge(step, done[0])

            raw = g.ps[:, 0, 0:NT * experts].rearrange("p (t e) -> p t e", t=NT)
            dve.wait_ge(made, 1)
            if bias is None:
                then(nc.vector.tensor_copy(logit[:, :, :], raw))
            else:
                dve.wait_ge(loaded, 48)
                then(nc.vector.tensor_tensor(logit[:, :, :], raw,
                                             bs[:, :].rearrange("p (o e) -> p o e", o=1).to_broadcast(shape), ALU.add))
            then(nc.vector.tensor_reduce(top[:, :], logit[:, :, :], X_AXIS, ALU.max))
            then(nc.vector.tensor_tensor(logit[:, :, :], logit[:, :, :], over(top[:, :]), ALU.subtract))
            dve.wait_ge(exped, 1)
            then(nc.vector.tensor_reduce(total[:, :], logit[:, :, :], X_AXIS, ALU.add))
            then(nc.vector.reciprocal(inv[:, :], total[:, :]))
            then(nc.vector.tensor_tensor(logit[:, :, :], logit[:, :, :], over(inv[:, :]), ALU.mult))
            for t in range(NT):
                then(nc.vector.max(best[:, t, :], logit[:, t, :]))
                then(nc.vector.max_index(at[:, t, :], best[:, t, :], logit[:, t, :]))
            then(nc.vector.tensor_copy(atf[:, :, :], at[:, :, :]))
            then(nc.vector.tensor_reduce(ksum[:, :], best[:, :, 0:top_k], X_AXIS, ALU.add))
            then(nc.vector.tensor_scalar(ksum[:, :], ksum[:, :], TOPK_EPS, None, ALU.add))
            then(nc.vector.reciprocal(kinv[:, :], ksum[:, :]))
            then(nc.vector.tensor_tensor(best[:, :, :], best[:, :, :],
                                         kinv[:, :].rearrange("p (t o) -> p t o", o=1).to_broadcast([P, NT, 8]), ALU.mult))
            for k in range(top_k):
                then(nc.vector.tensor_tensor(pick[:, k], iota[:, :].rearrange("p (o e) -> p o e", o=1).to_broadcast(shape),
                                             atf[:, :, k:k + 1].to_broadcast(shape), ALU.is_equal))
                then(nc.vector.tensor_tensor(gates if k == 0 else part[:, :, :], pick[:, k],
                                             best[:, :, k:k + 1].to_broadcast(shape), ALU.mult))
                if k:
                    then(nc.vector.tensor_tensor(gates, gates, part[:, :, :], ALU.add))


def shared_expert(nc, g, st, a, e, share, pool_work=None, top_k=0, add_picks=None, out=None):
    NF, HALF = len(FCH), NT // 2
    HU = 2 * NF
    w1, w2 = st.sbuf("w1", [P, KC, F]), st.sbuf("w2", [P, NF, D])
    b1, b2 = st.sbuf("b1", [P, NF]), st.sbuf("b2", [1, D])
    ht = st.sbuf("ht", [P, NF, T])
    w1_loaded, w2_loaded = st.sem("w1_loaded"), st.sem("w2_loaded")
    h_made = st.sem("h_made")
    h_done = st.sem("h_done")
    y_made = st.sem("y_made")
    y_added = st.sem("y_added")
    picks_added = st.sem("picks_added")
    stored = st.sem("stored")
    with nc.Block() as block:
        @block.sync
        def _(sp):
            sp.dma_start(w1[:, :, :], a["L1_ffn_sw1"][e].rearrange("(k p) f -> p k f", p=P)).then_inc(w1_loaded, 16)
            sp.dma_start(b1[:, :], a["sb1_cols"][e]).then_inc(w1_loaded, 16)
            sp.dma_start(w2[:, 0:2, :], a["L1_ffn_sw2"][e, 0:256, :].rearrange("(c p) n -> p c n", p=P)
                         ).then_inc(w2_loaded, 16)
            sp.dma_start(w2[0:FCH[2][1], 2, :], a["L1_ffn_sw2"][e, 256:F, :]).then_inc(w2_loaded, 16)
            sp.dma_start(b2[:, :], a["L1_ffn_sb2"][e:e + 1, :]).then_inc(w2_loaded, 16)
            if out is not None:
                for t in range(NT):
                    sp.wait_ge(y_added, t + 1)
                    sp.dma_start(out[t * P:(t + 1) * P, :], g.x[:, t, :]).then_inc(stored, 16)
                sp.wait_ge(stored, 16 * NT)

        if pool_work is not None:
            @block.gpsimd
            def _(pool):
                pool_work(pool, picks_added)

        @block.tensor
        def _(pe):
            pe.wait_ge(w1_loaded, 32)
            for u in range(HU):
                half, f = divmod(u, NF)
                f0, fn = FCH[f]
                if u >= 4:
                    pe.wait_ge(h_done, u - 3)
                for k in range(KC):
                    mm = nc.tensor.matmul(g.ps[0:fn, u % 4, :], w1[:, k, f0:f0 + fn],
                                          g.xt[:, k, half * 512:(half + 1) * 512], start=(k == 0), stop=(k == KC - 1))
                mm.then_inc(h_made, 1)
            pe.wait_ge(w2_loaded, 48)
            for t in range(NT):
                if t % HALF == 0:
                    pe.wait_ge(h_done, NF * (t // HALF + 1))
                if t >= 4:
                    pe.wait_ge(y_added, t - 3)
                nc.tensor.matmul(g.ps[:, 4 + t % 4, :], g.ones[0:1, :], b2[:, :], start=True, stop=False)
                for f, (f0, fn) in enumerate(FCH):
                    mm = nc.tensor.matmul(g.ps[:, 4 + t % 4, :], ht[0:fn, f, t * P:(t + 1) * P], w2[0:fn, f, :],
                                          start=False, stop=(f == NF - 1))
                mm.then_inc(y_made, 1)

        @block.scalar
        def _(act):
            act.wait_ge(w1_loaded, 32)
            for u in range(HU):
                half, f = divmod(u, NF)
                f0, fn = FCH[f]
                act.wait_ge(h_made, u + 1)
                nc.scalar.activation(ht[0:fn, f, half * 512:(half + 1) * 512], g.ps[0:fn, u % 4, :], ACT.Relu,
                                     bias=b1[0:fn, f:f + 1]).then_inc(h_done, 1)

        @block.vector
        def _(dve):
            def add(t):
                dve.wait_ge(y_made, t + 1)
                if add_picks is not None:
                    dve.wait_ge(picks_added, top_k * (t + 1))
                nc.vector.scalar_tensor_tensor(g.x[:, t, :], g.ps[:, 4 + t % 4, :], share[:, 0:1], g.x[:, t, :],
                                               ALU.mult, ALU.add).then_inc(y_added, 1)

            if add_picks is None:
                for t in range(NT):
                    add(t)
            else:
                for t in range(HALF):
                    add_picks(dve, t, picks_added)
                for t in range(HALF):
                    add(t)
                    add_picks(dve, HALF + t, picks_added)
                for t in range(HALF, NT):
                    add(t)


def blocks_bound(experts, top_k):
    most = (T * top_k + experts * (P - 1)) // P
    return -(-most // 4) * 4


def place_tokens(nc, g, st, a, experts, top_k, pick, places, block_row, blocks, zeros_stored, table):
    mine = st.sbuf("mine", [P, NT, experts])
    earlier = st.sbuf("earlier", [P, P])
    iota = st.sbuf("iota", [P, P])
    limits = st.sbuf("limits", [P, NT])
    above = st.sbuf("above", [P, experts, NT])
    counts = st.sbuf("counts", [P, experts])
    need = st.sbuf("need", [P, experts])
    ends = [st.sbuf(f"ends{n}", [P, experts]) for n in range(2)]
    begin = st.sbuf("begin", [P, experts])
    base = st.sbuf("base", [P, NT, experts])
    spread = st.sbuf("spread", [P, top_k, NT * experts])
    place = st.sbuf("place", [P, top_k * NT])
    past = st.sbuf("past", [1, blocks, experts])
    row = st.sbuf("row", [1, blocks])
    zeros = st.sbuf("zeros", [P, blocks])
    loaded, step, ranked, zeroed = st.sem("loaded"), st.sem("step"), st.sem("ranked"), st.sem("zeroed")
    with nc.Block() as block:
        @block.sync
        def _(sp):
            sp.dma_start(earlier[:, :], a["earlier"]).then_inc(loaded, 16)
            sp.dma_start(iota[:, :], a["iota"].partition_broadcast(P)).then_inc(loaded, 16)
            sp.wait_ge(zeroed, 1)
            sp.dma_start(table.rearrange("(p n) o -> p (n o)", p=P), zeros[:, :]).then_inc(zeros_stored, 16)

        @block.gpsimd
        def _(pool):
            nc.gpsimd.memset(zeros[:, :], 0.0).then_inc(zeroed, 1)

        @block.tensor
        def _(pe):
            pe.wait_ge(loaded, 32)
            pe.wait_ge(step, 1)
            for t in range(NT):
                for j in range(t + 1):
                    nc.tensor.matmul(g.ps[:, 1, t * experts:(t + 1) * experts],
                                     earlier[:, :] if j == t else g.ones[:, :], mine[:, j, :], start=(j == 0),
                                     stop=(j == t))
            for j in range(NT):
                mm = nc.tensor.matmul(g.ps[:, 2, 0:experts], g.ones[:, :], mine[:, j, :], start=(j == 0),
                                      stop=(j == NT - 1))
            mm.then_inc(ranked, 1)

        @block.vector
        def _(dve):
            done = [0]

            def then(ins):
                ins.then_inc(step, 1)
                done[0] += 1
                dve.wait_ge(step, done[0])

            then(nc.vector.tensor_reduce(mine[:, :, :], pick.rearrange("p k t e -> p t e k"), X_AXIS, ALU.add))
            dve.wait_ge(loaded, 32)
            then(nc.vector.tensor_scalar(limits[:, :], iota[:, 0:NT], float(P), None, ALU.mult))
            dve.wait_ge(ranked, 1)
            then(nc.vector.tensor_copy(counts[:, :], g.ps[:, 2, 0:experts]))
            then(nc.vector.tensor_tensor(above[:, :, :],
                                         counts[:, :].rearrange("p (e o) -> p e o", o=1).to_broadcast([P, experts, NT]),
                                         limits[:, :].rearrange("p (o n) -> p o n", o=1).to_broadcast([P, experts, NT]),
                                         ALU.is_gt))
            then(nc.vector.tensor_reduce(need[:, :], above[:, :, :], X_AXIS, ALU.add))
            then(nc.vector.tensor_copy(ends[0][:, :], need[:, :]))
            w, n = 1, 0
            while w < experts:
                then(nc.vector.tensor_copy(ends[1 - n][:, 0:w], ends[n][:, 0:w]))
                then(nc.vector.tensor_tensor(ends[1 - n][:, w:experts], ends[n][:, w:experts], ends[n][:, 0:experts - w],
                                             ALU.add))
                w, n = 2 * w, 1 - n
            end = ends[n]
            then(nc.vector.tensor_tensor(begin[:, :], end[:, :], need[:, :], ALU.subtract))
            then(nc.vector.tensor_scalar(begin[:, :], begin[:, :], float(P), None, ALU.mult))
            then(nc.vector.tensor_tensor(base[:, :, :],
                                         g.ps[:, 1, 0:NT * experts].rearrange("p (t e) -> p t e", t=NT),
                                         begin[:, :].rearrange("p (o e) -> p o e", o=1).to_broadcast([P, NT, experts]),
                                         ALU.add))
            then(nc.vector.tensor_tensor(spread[:, :, :], pick.rearrange("p k t e -> p k (t e)"),
                                         base[:, :, :].rearrange("p (o t) e -> p o (t e)", o=1).to_broadcast(
                                             [P, top_k, NT * experts]), ALU.mult))
            then(nc.vector.tensor_reduce(place[:, :], spread[:, :, :].rearrange("p k (t e) -> p (k t) e", t=NT), X_AXIS,
                                         ALU.add))
            then(nc.vector.tensor_copy(places[:, :], place[:, :]))
            then(nc.vector.tensor_tensor(past[:, :, :],
                                         iota[0:1, 0:blocks].rearrange("p (b o) -> p b o", o=1).to_broadcast(
                                             [1, blocks, experts]),
                                         end[0:1, :].rearrange("p (o e) -> p o e", o=1).to_broadcast(
                                             [1, blocks, experts]), ALU.is_ge))
            then(nc.vector.tensor_reduce(row[:, :], past[:, :, :], X_AXIS, ALU.add))
            then(nc.vector.tensor_scalar(row[:, :], row[:, :], float(experts - 1), None, ALU.min))
            then(nc.vector.tensor_copy(block_row[:, :], row[:, :]))


def place_tokens_back(nc, g, st, table, blocks, scattered, top_k, index):
    rows = st.sbuf("rows", [blocks, P])
    loaded, turned, done = st.sem("loaded"), st.sem("turned"), st.sem("done")
    with nc.Block() as block:
        @block.sync
        def _(sp):
            sp.wait_ge(scattered, 16 * top_k * NT)
            sp.dma_start(rows[:, :], table.rearrange("(n p) o -> n (p o)", p=P)).then_inc(loaded, 16)

        @block.tensor
        def _(pe):
            pe.wait_ge(loaded, 16)
            nc.tensor.transpose(g.ps[:, 0, 0:blocks], rows[:, :], g.ident[0:blocks, 0:blocks]).then_inc(turned, 1)

        @block.vector
        def _(dve):
            dve.wait_ge(turned, 1)
            nc.vector.tensor_copy(index[:, :], g.ps[:, 0, 0:blocks]).then_inc(done, 1)
            dve.wait_ge(done, 1)


def experts_by_block(nc, g, st, w1, w2, b1_cols, gated, blocks, block_row, index, rows_dram, y_dram):
    NF = len(FCH)
    W1 = 2 * F if gated else F
    R = 4
    NR = blocks // R
    w1s = [st.sbuf(f"w1_{n}", [P, KC, W1]) for n in range(R)]
    w2s = [st.sbuf(f"w2_{n}", [P, NF, D]) for n in range(R)]
    b1s = st.sbuf("b1s", [P, R, NF])
    idx = st.sbuf("idx", [P, R], U32)
    xg = st.sbuf("xg", [P, R, D])
    xgt = st.sbuf("xgt", [P, 2, KC, P])
    ht = st.sbuf("ht", [P, 2, NF, P])
    silu = st.sbuf("silu", [P, 2, NF, P]) if gated else None
    y = st.sbuf("y", [P, R, D])
    LOADS = 3 if gated else 4
    HD = 2 if gated else NF
    w_loaded = [st.sem(f"w_loaded{n}") for n in range(R)]
    xg_loaded = [st.sem(f"xg_loaded{n}") for n in range(R)]
    y_stored = [st.sem(f"y_stored{n}") for n in range(R)]
    idx_put = st.sem("idx_put")
    x_turned = st.sem("x_turned")
    xt_done = st.sem("xt_done")
    h_made = st.sem("h_made")
    silu_done = st.sem("silu_done")
    h_done = st.sem("h_done")
    y_made = st.sem("y_made")
    y_done = st.sem("y_done")
    FULL = [(P, 0, NF - 1), (FCH[-1][1], NF - 1, NF)]

    def rings(eng, step):
        for s in range(R):
            step(0, s, first=True)
        with eng.Fori(1, NR - 1) as i:
            for s in range(R):
                step(i, s)
        for s in range(R):
            step(NR - 1, s, last=(s == R - 1))

    with nc.Block() as block:
        @block.sync
        def _(sp):
            def step(i, s, first=False, last=False):
                j = R * i + s
                if not first:
                    sp.wait_ge(y_made, j - R + 1)
                e = sp.value_load(block_row[0:1, bass.ds(j, 1)], min_val=0, max_val=w1.shape[0] - 1)
                sp.dma_start(w1s[s][:, :, :], w1[e, :, :].rearrange("(k p) f -> p k f", p=P)).then_inc(w_loaded[s], 16)
                sp.dma_start(w2s[s][:, 0:2, :], w2[e, 0:256, :].rearrange("(c p) n -> p c n", p=P)).then_inc(w_loaded[s], 16)
                sp.dma_start(w2s[s][0:FCH[2][1], 2, :], w2[e, 256:F, :]).then_inc(w_loaded[s], 16)
                if not gated:
                    sp.dma_start(b1s[:, s, :], b1_cols[e, :, :]).then_inc(w_loaded[s], 16)

            rings(sp, step)

        @block.gpsimd
        def _(pool):
            def put(i, s):
                nc.gpsimd.tensor_copy(idx[:, s:s + 1], index[:, bass.ds(R * i + s, 1)]).then_inc(idx_put, 1)

            def step(i, s, first=False, last=False):
                j = R * i + s
                if not first or s == R - 1:
                    pool.wait_ge(x_turned, j - R + 2)
                pool.wait_ge(idx_put, j + 1)
                if s < R - 1:
                    put(i, s + 1)
                elif not last:
                    put(i + 1, 0)
                nc.gpsimd.indirect_dma_start(xg[:, s, :], None, rows_dram[:, :],
                                             bass.IndirectOffsetOnAxis(ap=idx[:, s:s + 1], axis=0)).then_inc(xg_loaded[s], 16)

            put(0, 0)
            rings(pool, step)

        @block.tensor
        def _(pe):
            def turn(i, s, free):
                j = R * i + s
                pe.wait_ge(xg_loaded[s], 16 * i + 16)
                if free:
                    pe.wait_ge(xt_done, j - 1)
                for k in range(KC):
                    mm = nc.tensor.transpose(g.ps[:, s % 2, k * P:(k + 1) * P], xg[:, s, k * P:(k + 1) * P], g.ident[:, :])
                mm.then_inc(x_turned, 1)

            def outputs(i, s, free):
                j = R * i + s
                pe.wait_ge(h_done, HD * j + HD)
                if free:
                    pe.wait_ge(y_done, j - 1)
                for f, (f0, fn) in enumerate(FCH):
                    mm = nc.tensor.matmul(g.ps[:, 6 + s % 2, :], ht[0:fn, s % 2, f, :], w2s[s][0:fn, f, :], start=(f == 0),
                                          stop=(f == NF - 1))
                mm.then_inc(y_made, 1)

            def step(i, s, first=False, last=False):
                j = R * i + s
                if not last:
                    if s < R - 1:
                        turn(i, s + 1, not (first and s < 1))
                    else:
                        turn(i + 1, 0, True)
                pe.wait_ge(xt_done, j + 1)
                pe.wait_ge(w_loaded[s], 16 * LOADS * i + 16 * LOADS)
                if not (first and s < 2):
                    pe.wait_ge(h_done, HD * j - HD)
                for half in range(2 if gated else 1):
                    for f, (f0, fn) in enumerate(FCH):
                        for k in range(KC):
                            mm = nc.tensor.matmul(g.ps[0:fn, 2 + s % 2 + 2 * half, f * P:(f + 1) * P],
                                                  w1s[s][:, k, half * F + f0:half * F + f0 + fn], xgt[:, s % 2, k, :],
                                                  start=(k == 0), stop=(k == KC - 1))
                mm.then_inc(h_made, 1)
                if s > 0:
                    outputs(i, s - 1, not (first and s - 1 < 2))
                elif not first:
                    outputs(i - 1, R - 1, True)

            turn(0, 0, False)
            rings(pe, step)
            outputs(NR - 1, R - 1, True)

        @block.scalar
        def _(act):
            def rows(i, s, free):
                j = R * i + s
                act.wait_ge(x_turned, j + 1)
                if free:
                    act.wait_ge(h_made, j - 1)
                nc.scalar.activation(xgt[:, s % 2, :, :], g.ps[:, s % 2, :].rearrange("p (k c) -> p k c", k=KC),
                                     ACT.Copy).then_inc(xt_done, 1)

            def store(i, s):
                j = R * i + s
                act.wait_ge(y_done, j + 1)
                act.dma_start(y_dram[bass.ds(j * P, P), :], y[:, s, :]).then_inc(y_stored[s], 16)

            def step(i, s, first=False, last=False):
                j = R * i + s
                if not last:
                    if s < R - 1:
                        rows(i, s + 1, not (first and s < 1))
                    else:
                        rows(i + 1, 0, True)
                act.wait_ge(h_made, j + 1)
                free = not (first and s < 2)
                if gated:
                    if free:
                        act.wait_ge(h_done, HD * j - HD)
                    for rws, lo, hi in FULL:
                        nc.scalar.activation(silu[0:rws, s % 2, lo:hi, :],
                                             g.ps[0:rws, 2 + s % 2, lo * P:hi * P].rearrange("p (f c) -> p f c", f=hi - lo),
                                             ACT.Silu).then_inc(silu_done, 1)
                else:
                    act.wait_ge(w_loaded[s], 16 * LOADS * i + 16 * LOADS)
                    if free:
                        act.wait_ge(y_made, j - 1)
                    for f, (f0, fn) in enumerate(FCH):
                        nc.scalar.activation(ht[0:fn, s % 2, f, :], g.ps[0:fn, 2 + s % 2, f * P:(f + 1) * P], ACT.Relu,
                                             bias=b1s[0:fn, s, f:f + 1]).then_inc(h_done, 1)
                if s >= 2:
                    store(i, s - 2)
                elif not first:
                    store(i - 1, s + R - 2)

            rows(0, 0, False)
            rings(act, step)
            store(NR - 1, R - 2)
            store(NR - 1, R - 1)
            for s in range(R):
                act.wait_ge(y_stored[s], 16 * NR)

        @block.vector
        def _(dve):
            def out(i, s, free):
                j = R * i + s
                dve.wait_ge(y_made, j + 1)
                if free:
                    dve.wait_ge(y_stored[s], 16 * i)
                nc.vector.tensor_copy(y[:, s, :], g.ps[:, 6 + s % 2, :]).then_inc(y_done, 1)

            def step(i, s, first=False, last=False):
                j = R * i + s
                if gated:
                    for n, (rws, lo, hi) in enumerate(FULL):
                        dve.wait_ge(silu_done, 2 * j + n + 1)
                        dve.wait_ge(h_made, j + 1)
                        if not (first and s < 2):
                            dve.wait_ge(y_made, j - 1)
                        nc.vector.tensor_tensor(ht[0:rws, s % 2, lo:hi, :],
                                                g.ps[0:rws, 4 + s % 2, lo * P:hi * P].rearrange("p (f c) -> p f c", f=hi - lo),
                                                silu[0:rws, s % 2, lo:hi, :], ALU.mult).then_inc(h_done, 1)
                if s > 0:
                    out(i, s - 1, not first)
                elif not first:
                    out(i - 1, R - 1, True) if not isinstance(i, int) or i > 1 else out(i - 1, R - 1, False)

            rings(dve, step)
            out(NR - 1, R - 1, True)


def combine(nc, g, st, top_k, places, best, y_dram, last=None):
    RING = 8
    rows = st.sbuf("rows", [P, RING, D])
    loaded = [st.sem(f"loaded{n}") for n in range(RING)]

    def gather(pool, added):
        for n in range(top_k * NT):
            t, k = divmod(n, top_k)
            if n >= RING:
                pool.wait_ge(added, n - RING + 1)
            nc.gpsimd.indirect_dma_start(rows[:, n % RING, :], None, y_dram[:, :],
                                         bass.IndirectOffsetOnAxis(ap=places[:, k * NT + t:k * NT + t + 1], axis=0)
                                         ).then_inc(loaded[n % RING], 16)

    def add_picks(dve, t, added):
        for k in range(top_k):
            n = t * top_k + k
            dve.wait_ge(loaded[n % RING], 16 * (n // RING + 1))
            if k:
                dve.wait_ge(added, n)
            nc.vector.scalar_tensor_tensor(g.x[:, t, :], rows[:, n % RING, :], best[:, t, k:k + 1], g.x[:, t, :],
                                           ALU.mult, ALU.add).then_inc(added, 1)

    if last is not None:
        last(gather, add_picks)
        return
    added = st.sem("added")
    with nc.Block() as block:
        @block.gpsimd
        def _(pool):
            gather(pool, added)

        @block.vector
        def _(dve):
            for t in range(NT):
                add_picks(dve, t, added)


def scatter_tokens(nc, pool, top_k, ids, places, table, zeros_stored, scattered):
    pool.wait_ge(zeros_stored, 16)
    for n in range(top_k * NT):
        nc.gpsimd.indirect_dma_start(table[:, :], bass.IndirectOffsetOnAxis(ap=places[:, n:n + 1], axis=0),
                                     ids[:, n % NT:n % NT + 1], None).then_inc(scattered, 16)


def moe(nc, g, name, a, experts, top_k, wr, br, w1, w2, b1_cols, b2_rows, gated, shared=False, out=None):
    blocks = blocks_bound(experts, top_k)
    table = nc.dram_tensor(name + "_table", (blocks * P, 1), F32, kind="Internal").ap()
    y_dram = nc.dram_tensor(name + "_y", (blocks * P, D), F32, kind="Internal").ap()
    rows_dram = nc.dram_tensor(name + "_rows", (T, D), F32, kind="Internal").ap()
    layer_norm(nc, g, name + "_ln", rows_dram=rows_dram)
    with Stage(nc, name) as st:
        gates = st.sbuf("gates", [P, NT, experts])
        best = st.sbuf("best", [P, NT, 8])
        places = st.sbuf("places", [P, top_k * NT], U32)
        block_row = st.sbuf("block_row", [1, blocks], U32)
        index = st.sbuf("index", [P, blocks], U32)
        ids = st.sbuf("ids", [P, NT])
        share = st.sbuf("share", [P, 1])
        zeros_stored, scattered, ids_loaded = st.sem("zeros_stored"), st.sem("scattered"), st.sem("ids_loaded")
        with Stage(nc, name + "_pick") as pi:
            pick = pi.sbuf("pick", [P, top_k, NT, experts])
            with Stage(nc, name + "_route") as ro:
                router(nc, g, ro, wr, br, experts, top_k, gates[:, :, :], a["iota"], pick, best)
            with Stage(nc, name + "_place") as pl:
                place_tokens(nc, g, pl, a, experts, top_k, pick[:, :, :, :], places, block_row, blocks, zeros_stored, table)
        with Stage(nc, name + "_ids") as il:
            set_ = il.sem("set")
            with nc.Block() as block:
                @block.sync
                def _(sp):
                    sp.dma_start(ids[:, :], a["ids"]).then_inc(ids_loaded, 16)
                    sp.wait_ge(ids_loaded, 16)

                @block.vector
                def _(dve):
                    nc.vector.memset(share[:, :], 1.0 / NSH).then_inc(set_, 1)
                    dve.wait_ge(set_, 1)

        def scatter(pool, _=None):
            scatter_tokens(nc, pool, top_k, ids, places, table, zeros_stored, scattered)

        if shared:
            with Stage(nc, name + "_shared0") as sh:
                shared_expert(nc, g, sh, a, 0, share, pool_work=scatter)
            with Stage(nc, name + "_bias") as bi:
                second_biases(nc, g, bi, experts, gates, b2_rows)
        else:
            with nc.Block() as block:
                @block.gpsimd
                def _(pool):
                    scatter(pool)
        with Stage(nc, name + "_back") as bk:
            place_tokens_back(nc, g, bk, table, blocks, scattered, top_k, index)
        with Stage(nc, name + "_blocks") as bl:
            experts_by_block(nc, g, bl, w1, w2, b1_cols, gated, blocks, block_row, index, rows_dram, y_dram)
        with Stage(nc, name + "_sum") as su:
            def beside_shared(gather, add_picks):
                shared_expert(nc, g, su, a, 1, share, gather, top_k, add_picks, out)

            combine(nc, g, su, top_k, places, best, y_dram, beside_shared if shared else None)


def second_biases(nc, g, st, experts, gates, b2_rows):
    b2 = st.sbuf("b2", [experts, D])
    gt = st.sbuf("gt", [experts, T])
    loaded, turned, done, made, added = (st.sem("loaded"), st.sem("turned"), st.sem("done"), st.sem("made"),
                                         st.sem("added"))
    with nc.Block() as block:
        @block.sync
        def _(sp):
            sp.dma_start(b2[:, :], b2_rows).then_inc(loaded, 16)

        @block.tensor
        def _(pe):
            for t in range(NT):
                mm = nc.tensor.transpose(g.ps[0:experts, t // 4, t % 4 * P:(t % 4 + 1) * P], gates[:, t, :], g.ident[:, :])
            mm.then_inc(turned, 1)
            pe.wait_ge(loaded, 16)
            pe.wait_ge(done, 1)
            for t in range(NT):
                if t >= 4:
                    pe.wait_ge(added, t - 3)
                nc.tensor.matmul(g.ps[:, 4 + t % 4, :], gt[:, t * P:(t + 1) * P], b2[:, :], start=True,
                                 stop=True).then_inc(made, 1)

        @block.scalar
        def _(act):
            act.wait_ge(turned, 1)
            nc.scalar.activation(gt[:, :], g.ps[0:experts, 0:2, :].rearrange("p a n -> p (a n)"),
                                 ACT.Copy).then_inc(done, 1)

        @block.vector
        def _(dve):
            for t in range(NT):
                dve.wait_ge(made, t + 1)
                nc.vector.tensor_tensor(g.x[:, t, :], g.x[:, t, :], g.ps[:, 4 + t % 4, :], ALU.add).then_inc(added, 1)


def cross_attention1(nc, g, name, a):
    NKT = CTX // P
    k_dram = nc.dram_tensor("k_raw", (B * H, P, CTX), F32, kind="Internal").ap()
    q_dram = nc.dram_tensor("q_raw", (B * H, P, S), F32, kind="Internal").ap()
    v_dram = nc.dram_tensor("v_rows", (B * H, NKT, P, DX), F32, kind="Internal").ap()
    with Stage(nc, name) as st:
        rk = st.sbuf("rk", [P, B * CTX])
        rq = st.sbuf("rq", [P, T])
        k_scale = st.sbuf("k_scale", [P, 2, B * H])
        with Stage(nc, name + "_made") as md:
            ctx_high = md.sbuf("ctx_high", [P, KC, B * CTX], F32R)
            ctx_low = md.sbuf("ctx_low", [P, KC, B * CTX], F32R)
            with Stage(nc, name + "_kq") as kq:
                project_kq1(nc, g, kq, a, ctx_high, ctx_low, k_dram, q_dram, rk, rq, k_scale)
            with Stage(nc, name + "_v") as vs:
                project_v1(nc, g, vs, a, ctx_high, ctx_low, v_dram)
        ot = st.sbuf("ot", [P, B * H, S])
        wo = st.sbuf("wo", [P, H, D])
        bo = st.sbuf("bo", [P, D])
        o_loaded = st.sem("o_loaded")
        with Stage(nc, name + "_core") as co:
            attention_core1(nc, g, co, a, k_dram, q_dram, v_dram, rk, rq, k_scale, ot, wo, bo, o_loaded)
        with Stage(nc, name + "_out") as ou:
            made, added, biased = ou.sem("made"), ou.sem("added"), ou.sem("biased")
            with nc.Block() as block:
                @block.gpsimd
                def _(pool):
                    pool.wait_ge(o_loaded, 32)
                    for t in range(NT):
                        nc.gpsimd.tensor_tensor(g.x[:, t, :], g.x[:, t, :], bo[:, :], ALU.add).then_inc(biased, 1)

                @block.tensor
                def _(pe):
                    pe.wait_ge(o_loaded, 32)
                    for t in range(NT):
                        b, s = divmod(t * P, S)
                        if t >= 4:
                            pe.wait_ge(added, t - 3)
                        for h in range(H):
                            mm = nc.tensor.matmul(g.ps[:, t % 4, :], ot[:, b * H + h, s:s + P], wo[:, h, :],
                                                  start=(h == 0), stop=(h == H - 1))
                        mm.then_inc(made, 1)

                @block.vector
                def _(dve):
                    for t in range(NT):
                        dve.wait_ge(made, t + 1)
                        dve.wait_ge(biased, t + 1)
                        nc.vector.tensor_tensor(g.x[:, t, :], g.x[:, t, :], g.ps[:, t % 4, :],
                                                ALU.add).then_inc(added, 1)


def split_matmul(nc, out, lhs_high, lhs_low, rhs_high, rhs_low, start, stop):
    nc.tensor.matmul(out, lhs_high, rhs_high, start=start, stop=False)
    nc.tensor.matmul(out, lhs_high, rhs_low, start=False, stop=False)
    return nc.tensor.matmul(out, lhs_low, rhs_high, start=False, stop=stop)


def project_kq1(nc, g, st, a, ctx_high, ctx_low, k_dram, q_dram, rk, rq, k_scale):
    UH = 6
    EVEN = NIMG // 2 * 2
    NEXT = 3
    NS = B * CTX + T
    ki_w, k_w, q_w = a["L1_xattn_ki_w"], a["L1_xattn_k_w"], a["L1_xattn_q_w"]
    w = st.sbuf("w", [P, 3, KC, DX])
    w_high = [st.sbuf(f"w_high{n}", [P, 3, KC, DX], F32R) for n in range(2)]
    w_low = [st.sbuf(f"w_low{n}", [P, 3, KC, DX], F32R) for n in range(2)]
    x_high, x_low = st.sbuf("x_high", [P, KC, T], F32R), st.sbuf("x_low", [P, KC, T], F32R)
    cols = st.sbuf("cols", [P, 3, H])
    bias = st.sbuf("bias", [P, 2, 3])
    bias_put = st.sem("bias_put")
    norm_cols = st.sbuf("norm_cols", [P, 3, H])
    raw = st.sbuf("raw", [P, UH, 512])
    sums = g.xt[:, 0:NS // T, :].rearrange("p k n -> p (k n)")
    sq = g.xt[:, NS // T, :].rearrange("p (a n) -> p a n", a=2)
    stage = [raw[:, 0:KC, :], rk[:, :].rearrange("p (k n) -> p k n", k=KC)]
    rms = st.sbuf("rms", [P, 2, 512])
    eps_q = st.sbuf("eps_q", [P, 1])
    w_loaded = st.sem("w_loaded")
    ctx_loaded = [st.sem(f"ctx_loaded{n}") for n in range(2)]
    w_highs, w_lows = st.sem("w_highs"), st.sem("w_lows")
    c_highs, c_lows = st.sem("c_highs"), st.sem("c_lows")
    x_highs, x_lows = st.sem("x_highs"), st.sem("x_lows")
    b_loaded, made, done = st.sem("b_loaded"), st.sem("made"), st.sem("done")
    squared, summed, zeroed = st.sem("squared"), st.sem("summed"), st.sem("zeroed")
    stored = [st.sem(f"stored{n}") for n in range(UH)]
    total, rooted, inverted, scaled = st.sem("total"), st.sem("rooted"), st.sem("inverted"), st.sem("scaled")

    def load_weights(sp, h):
        for n, src in enumerate((ki_w, k_w, q_w)):
            sp.dma_start(w[:, n, :, :],
                         src[:, bass.ds(h * DX, DX)].rearrange("(k p) n -> p k n", p=P)).then_inc(w_loaded, 16)

    def load_chunk(sp, c):
        sp.dma_start(stage[c % 2], a["ctxt"][:, c * 512:(c + 1) * 512].rearrange("(k p) n -> p k n", p=P)
                     ).then_inc(ctx_loaded[c % 2], 16)

    def load_first(sp):
        load_weights(sp, 0)
        load_chunk(sp, 0)
        load_chunk(sp, 1)

    layer_norm(nc, g, st.name + "_ln", prefetch=load_first)
    with nc.Block() as block:
        @block.sync
        def _(sp):
            def load(h):
                sp.wait_ge(w_lows, h)
                load_weights(sp, h)

            def store(h):
                for u in range(UH):
                    sp.wait_ge(done, UH * h + u + 1)
                    if u < 4:
                        b, half = divmod(u, 2)
                        dst = k_dram[h + b * H, :, half * 512:(half + 1) * 512]
                    else:
                        dst = q_dram[h + (u - 4) * H, :, :]
                    sp.dma_start(dst, raw[:, u, :]).then_inc(stored[u], 16)

            for c in range(B * 2):
                if c >= 2:
                    sp.wait_ge(c_lows, c - 1)
                    load_chunk(sp, c)
                if c == 0:
                    for n, b in enumerate(("ki_b", "k_b", "q_b")):
                        sp.dma_start(cols[:, n, :], a[b + "_cols"]).then_inc(b_loaded, 16)
                    for n, b in enumerate(("nq_s", "nki_s", "nkt_s")):
                        sp.dma_start(norm_cols[:, n, :], a[b + "_cols"]).then_inc(b_loaded, 16)
            load(1)
            store(0)
            load(2)
            store(1)
            load(3)
            with sp.Fori(1, H // 2 - 1) as i:
                store(2 * i)
                load(2 * i + 2)
                store(2 * i + 1)
                load(2 * i + 3)
            store(H - 2)
            store(H - 1)
            for u in range(UH):
                sp.wait_ge(stored[u], 16 * H)

        @block.tensor
        def _(pe):
            def head(i, slot, first=False):
                h = 2 * i + slot
                pe.wait_ge(w_lows, h + 1)
                for u in range(UH):
                    if first and slot == 0:
                        if u < 4:
                            pe.wait_ge(c_lows, u + 1)
                        else:
                            pe.wait_ge(x_lows, 1)
                    if not (first and slot == 0):
                        pe.wait_ge(done, UH * h + u - UH + 1)
                    if u >= 4:
                        parts = [(2, x_high, x_low, u, 0, (u - 4) * S, (u - 3) * S)]
                    elif u in (0, 2):
                        parts = [(0, ctx_high, ctx_low, 6 + u // 2, 0, u * 512, u * 512 + EVEN + 2),
                                 (1, ctx_high, ctx_low, u, EVEN, u * 512 + EVEN, (u + 1) * 512)]
                    else:
                        parts = [(1, ctx_high, ctx_low, u, 0, u * 512, (u + 1) * 512)]
                    for n, high, low, bank, at, lo, hi in parts:
                        for k in range(KC):
                            mm = split_matmul(nc, g.ps[:, bank, at:at + hi - lo], w_high[slot][:, n, k, :],
                                              w_low[slot][:, n, k, :], high[:, k, lo:hi],
                                              low[:, k, lo:hi], start=(k == 0), stop=(k == KC - 1))
                    mm.then_inc(made, 1)

            head(0, 0, first=True)
            head(0, 1, first=True)
            with pe.Fori(1, H // 2) as i:
                head(i, 0)
                head(i, 1)
            pe.wait_ge(summed, UH * H)
            for c in range(NS // 512):
                nc.tensor.matmul(g.ps[:, c, :], g.ones[:, :], sums[:, c * 512:(c + 1) * 512], start=True,
                                 stop=True).then_inc(total, 1)

        @block.scalar
        def _(act):
            def split_weights(h, slot):
                act.wait_ge(w_loaded, 48 * h + 48)
                nc.scalar.activation(w_high[slot][:, :, :, :], w[:, :, :, :], ACT.Copy).then_inc(w_highs, 1)

            def head(i, slot, first=False, last=False):
                h = 2 * i + slot
                nc.scalar.activation(bias[:, slot, :], cols[:, :, bass.ds(h, 1)].rearrange("p n o -> p (n o)"),
                                     ACT.Copy).then_inc(bias_put, 1)
                act.wait_ge(bias_put, h + 1)
                for u in range(UH):
                    act.wait_ge(made, UH * h + u + 1)
                    if not (first and slot == 0):
                        act.wait_ge(stored[u], 16 * h)
                        act.wait_ge(squared, UH * h + u - UH + 1)
                    parts = [(0, 0, NIMG), (1, NIMG, 512)] if u in (0, 2) else [(1 if u < 4 else 2, 0, 512)]
                    for n, lo, hi in parts:
                        bank = 6 + u // 2 if n == 0 else u
                        ins = nc.scalar.activation(raw[:, u, lo:hi], g.ps[:, bank, lo:hi], ACT.Identity,
                                                   bias=bias[:, slot, n:n + 1])
                    ins.then_inc(done, 1)
                    if u == NEXT and not last:
                        split_weights(h + 1, 1 - slot)

            split_weights(0, 0)
            for c in range(B * 2):
                act.wait_ge(ctx_loaded[c % 2], 16 * (c // 2 + 1))
                nc.scalar.activation(ctx_high[:, :, c * 512:(c + 1) * 512], stage[c % 2], ACT.Copy).then_inc(c_highs, 1)
                if c == 1:
                    nc.scalar.activation(x_high[:, :, :], g.xt[:, :, :], ACT.Copy).then_inc(x_highs, 1)
            act.wait_ge(c_lows, B * 2)
            act.wait_ge(b_loaded, 96)
            head(0, 0, first=True)
            head(0, 1, first=True)
            with act.Fori(1, H // 2 - 1) as i:
                head(i, 0)
                head(i, 1)
            head(H // 2 - 1, 0)
            head(H // 2 - 1, 1, last=True)
            act.wait_ge(zeroed, 2)
            for c in range(NS // 512):
                act.wait_ge(total, c + 1)
                if c >= 2:
                    act.wait_ge(inverted, c - 1)
                keys = c < B * 2
                nc.scalar.activation(rms[:, c % 2, :], g.ps[:, c, :], ACT.Sqrt,
                                     scale=1.0 / INNER if keys else float(DX) / INNER,
                                     bias=g.rms_eps[:, 0:1] if keys else eps_q[:, 0:1]).then_inc(rooted, 1)

        @block.vector
        def _(dve):
            def split_weights(h, slot):
                dve.wait_ge(w_highs, h + 1)
                nc.vector.tensor_tensor(w_low[slot][:, :, :, :], w[:, :, :, :], w_high[slot][:, :, :, :],
                                        ALU.subtract).then_inc(w_lows, 1)

            def head(i, slot, first=False, last=False):
                h = 2 * i + slot
                for u in range(UH):
                    dve.wait_ge(done, UH * h + u + 1)
                    if not (first and slot == 0 and u < 2):
                        dve.wait_ge(summed, UH * h + u - 1)
                    nc.vector.tensor_tensor(sq[:, u % 2, :], raw[:, u, :], raw[:, u, :], ALU.mult).then_inc(squared, 1)
                    if u == NEXT and not last:
                        split_weights(h + 1, 1 - slot)

            split_weights(0, 0)
            for c in range(B * 2):
                dve.wait_ge(c_highs, c + 1)
                chunk = slice(c * 512, (c + 1) * 512)
                nc.vector.tensor_tensor(ctx_low[:, :, chunk], stage[c % 2], ctx_high[:, :, chunk],
                                        ALU.subtract).then_inc(c_lows, 1)
                if c == 1:
                    dve.wait_ge(x_highs, 1)
                    nc.vector.tensor_tensor(x_low[:, :, :], g.xt[:, :, :], x_high[:, :, :],
                                            ALU.subtract).then_inc(x_lows, 1)
            nc.vector.memset(eps_q[:, :], RMS_EPS * DX).then_inc(zeroed, 1)
            dve.wait_ge(b_loaded, 96)
            for n in range(2):
                for b in range(B):
                    nc.vector.tensor_tensor(k_scale[:, n, b * H:(b + 1) * H], norm_cols[:, 0, :], norm_cols[:, 1 + n, :],
                                            ALU.mult).then_inc(scaled, 1)
            head(0, 0, first=True)
            head(0, 1, first=True)
            with dve.Fori(1, H // 2 - 1) as i:
                head(i, 0)
                head(i, 1)
            head(H // 2 - 1, 0)
            head(H // 2 - 1, 1, last=True)
            for c in range(NS // 512):
                dve.wait_ge(rooted, c + 1)
                dst = rk[:, c * 512:(c + 1) * 512] if c < B * 2 else rq[:, (c - B * 2) * 512:(c - B * 2 + 1) * 512]
                nc.vector.reciprocal(dst, rms[:, c % 2, :]).then_inc(inverted, 1)

        @block.gpsimd
        def _(pool):
            def head(i, slot, first=False):
                h = 2 * i + slot
                for u in range(UH):
                    pool.wait_ge(squared, UH * h + u + 1)
                    if not (first and slot == 0):
                        pool.wait_ge(summed, UH * h + u - UH + 1)
                    nc.gpsimd.tensor_tensor(sums[:, u * 512:(u + 1) * 512], sums[:, u * 512:(u + 1) * 512],
                                            sq[:, u % 2, :], ALU.add).then_inc(summed, 1)

            pool.wait_ge(x_lows, 1)
            nc.gpsimd.memset(sums[:, :], 0.0).then_inc(zeroed, 1)
            pool.wait_ge(zeroed, 2)
            head(0, 0, first=True)
            head(0, 1, first=True)
            with pool.Fori(1, H // 2) as i:
                head(i, 0)
                head(i, 1)


def project_v1(nc, g, st, a, ctx_high, ctx_low, v_dram):
    NKT = CTX // P
    HG = 512 // DX
    NG = H // HG
    EDGE, REST = divmod(NIMG, P)
    assert REST == 1
    RING = 4
    w = st.sbuf("w", [P, 2, KC, 512])
    w_high = [st.sbuf(f"w_high{n}", [P, 2, KC, 512], F32R) for n in range(2)]
    w_low = [st.sbuf(f"w_low{n}", [P, 2, KC, 512], F32R) for n in range(2)]
    rows = g.xt[:, 0:2, :].rearrange("p k (a n) -> p (k a) n", n=512)
    bias = g.xt[:, 2:4, :].rearrange("p k (a n) -> p k a n", n=512)
    loaded = [st.sem(f"loaded{m}") for m in range(2)]
    w_highs, w_lows = st.sem("w_highs"), st.sem("w_lows")
    made, done, edged = st.sem("made"), st.sem("done"), st.sem("edged")
    stored = [st.sem(f"stored{n}") for n in range(RING)]
    UT = B * NKT
    with nc.Block() as block:
        @block.sync
        def _(sp):
            def load(n, slot, first=False):
                if not first:
                    sp.wait_ge(w_lows, 2 * n)
                for m, src in enumerate((a["L1_xattn_vi_w"], a["L1_xattn_v_w"])):
                    sp.dma_start(w[:, m, :, :],
                                 src[:, bass.ds(n * 512, 512)].rearrange("(k p) n -> p k n", p=P)).then_inc(loaded[m], 16)
                for m, src in enumerate((a["L1_xattn_vi_b"], a["L1_xattn_v_b"])):
                    sp.dma_start(bias[:, slot, m, :],
                                 src[bass.ds(n * 512, 512)].partition_broadcast(P)).then_inc(loaded[m], 16)

            def store(n):
                for t in range(UT):
                    b, kb = divmod(t, NKT)
                    sp.wait_ge(done, UT * n + t + 1)
                    sp.dma_start(v_dram[bass.ds(n * HG + b * H, HG), kb, :, :].rearrange("h p d -> p h d"),
                                 rows[:, t % RING, :].rearrange("p (h d) -> p h d", h=HG)).then_inc(stored[t % RING], 16)

            load(0, 0, first=True)
            load(1, 1)
            with sp.Fori(0, NG // 2 - 1) as i:
                store(2 * i)
                load(2 * i + 2, 0)
                store(2 * i + 1)
                load(2 * i + 3, 1)
            store(NG - 2)
            store(NG - 1)
            for r in range(RING):
                sp.wait_ge(stored[r], 16 * NG * UT // RING)

        @block.tensor
        def _(pe):
            def group(i, slot, first=False):
                n = 2 * i + slot
                pe.wait_ge(w_lows, 2 * n + 1)
                for t in range(UT):
                    b, kb = divmod(t, NKT)
                    if t == EDGE:
                        pe.wait_ge(w_lows, 2 * n + 2)
                    if not (first and slot == 0 and t < 4):
                        pe.wait_ge(done, UT * n + t - 3)
                    kind = 0 if kb < EDGE else 1
                    for kind, bank in [(kind, t % 4)] + ([(0, 4 + b)] if kb == EDGE else []):
                        for k in range(KC):
                            mm = split_matmul(nc, g.ps[:, bank, :], ctx_high[:, k, t * P:(t + 1) * P],
                                              ctx_low[:, k, t * P:(t + 1) * P], w_high[slot][:, kind, k, :],
                                              w_low[slot][:, kind, k, :], start=(k == 0), stop=(k == KC - 1))
                    mm.then_inc(made, 1)

            group(0, 0, first=True)
            group(0, 1, first=True)
            with pe.Fori(1, NG // 2) as i:
                group(i, 0)
                group(i, 1)

        @block.scalar
        def _(act):
            for n in range(NG):
                if n >= 2:
                    act.wait_ge(made, UT * (n - 1))
                for m in range(2):
                    act.wait_ge(loaded[m], 32 * (n + 1))
                    nc.scalar.activation(w_high[n % 2][:, m, :, :], w[:, m, :, :], ACT.Copy).then_inc(w_highs, 1)

        def split_low(eng, engine, n, m):
            eng.wait_ge(w_highs, 2 * n + m + 1)
            engine.tensor_tensor(w_low[n % 2][:, m, :, :], w[:, m, :, :], w_high[n % 2][:, m, :, :],
                                 ALU.subtract).then_inc(w_lows, 1)

        @block.gpsimd
        def _(pool):
            pool.wait_ge(w_lows, 2)
            for n in range(1, NG):
                for m in range(2):
                    split_low(pool, nc.gpsimd, n, m)

        @block.vector
        def _(dve):
            def group(i, slot, first=False):
                n = 2 * i + slot
                for t in range(UT):
                    b, kb = divmod(t, NKT)
                    dve.wait_ge(made, UT * n + t + 1)
                    r = t % RING
                    if not (first and slot == 0 and t < RING):
                        dve.wait_ge(stored[r], (UT // RING * n + t // RING) * 16)
                    kind = 0 if kb < EDGE else 1
                    ins = nc.vector.tensor_tensor(rows[:, r, :], g.ps[:, t % 4, :], bias[:, slot, kind, :],
                                                  ALU.add)
                    if kb == EDGE:
                        ins.then_inc(edged, 1)
                        dve.wait_ge(edged, B * n + b + 1)
                        ins = nc.vector.tensor_tensor(rows[0:1, r, :], g.ps[0:1, 4 + b, :],
                                                      bias[0:1, slot, 0, :], ALU.add)
                    ins.then_inc(done, 1)

            for m in range(2):
                split_low(dve, nc.vector, 0, m)
            group(0, 0, first=True)
            group(0, 1, first=True)
            with dve.Fori(1, NG // 2) as i:
                group(i, 0)
                group(i, 1)


def attention_core1(nc, g, st, a, k_dram, q_dram, v_dram, rk, rq, k_scale, ot, wo, bo, o_loaded):
    NKT, QB = CTX // P, S // P
    HP, U = 2, 2 * QB
    NI = B * H // HP
    NB = NI // B
    SB, SKEW, PR = 2, 3, 4
    LAG = 0
    SPANS = [(0, NIMG), (NIMG, CTX)]
    k = st.sbuf("k", [P, HP, CTX])
    q = st.sbuf("q", [P, HP, S])
    v = st.sbuf("v", [P, HP, NKT, DX])
    prob = g.xt
    pt = st.sbuf("pt", [P, HP, NKT, S])
    nmax, rsum, rinv = st.sbuf("nmax", [P, PR, 2]), st.sbuf("rsum", [P, PR, 2]), st.sbuf("rinv", [P, PR, 2])
    kq_loaded = [st.sem(f"kq_loaded{n}") for n in range(HP)]
    v_loaded = [st.sem(f"v_loaded{n}") for n in range(HP)]
    k_done, q_done = st.sem("k_done"), st.sem("q_done")
    scores = st.sem("scores")
    max_done = st.sem("max_done")
    exp_done = st.sem("exp_done")
    rinv_done = st.sem("rinv_done")
    prob_done = st.sem("prob_done")
    turned = [st.sem(f"turned{n}") for n in range(2)]
    pt_done = [st.sem(f"pt_done{n}") for n in range(2)]
    pv_done = st.sem("pv_done")
    ot_done = st.sem("ot_done")

    def s_ps(n):
        return g.ps[:, 2 * (n % SB):2 * (n % SB) + 2, :].rearrange("p a n -> p (a n)")

    def over_pairs(eng, step):
        for n in range(U):
            step(0, n, 0, 0, first=True)
        with eng.Fori(1, NB - 1) as i:
            for n in range(U):
                step(i, n, 0, 0)
        for n in range(U):
            step(NB - 1, n, 0, 1)
        with eng.Fori(NB, NI - 1) as i:
            for n in range(U):
                step(i, n, 1, 1)
        for n in range(U):
            step(NI - 1, n, 1, None)

    with nc.Block() as block:
        @block.sync
        def _(sp):
            def load(i, s, first=False):
                j = HP * i + s
                if not first:
                    sp.wait_ge(scores, QB * (j - 1))
                sp.dma_start(k[:, s, :], k_dram[j, :, :]).then_inc(kq_loaded[s], 16)
                sp.dma_start(q[:, s, :], q_dram[j, :, :]).then_inc(kq_loaded[s], 16)
                if not first:
                    sp.wait_ge(pv_done, j - 1)
                sp.dma_start(v[:, s, :, :], v_dram[j, :, :, :].rearrange("t p d -> p t d")).then_inc(v_loaded[s], 16)

            load(0, 0, first=True)
            load(0, 1, first=True)
            sp.dma_start(wo[:, :, :], a["L1_xattn_o_w"].rearrange("(h p) n -> p h n", p=P)).then_inc(o_loaded, 16)
            sp.dma_start(bo[:, :], a["L1_xattn_o_b"].partition_broadcast(P)).then_inc(o_loaded, 16)
            with sp.Fori(1, NI) as i:
                load(i, 0)
                load(i, 1)
            sp.wait_ge(o_loaded, 32)

        @block.tensor
        def _(pe):
            def step(i, n, b=0, nb=0, first=False, tail=False):
                u = U * i + n
                s, qb = divmod(n % U, QB)
                if not tail:
                    if qb == 0:
                        pe.wait_ge(k_done, HP * i + s + 1)
                        pe.wait_ge(q_done, HP * i + s + 1)
                    if not (first and n < SB):
                        pe.wait_ge(exp_done, u - SB + 1)
                    for c in range(0, CTX, 512):
                        mm = nc.tensor.matmul(s_ps(n)[:, c:c + 512], q[:, s, qb * P:(qb + 1) * P], k[:, s, c:c + 512],
                                              start=True, stop=True)
                    mm.then_inc(scores, 1)
                nn = n - SKEW
                if first and nn < 0:
                    return
                w = u - SKEW
                if nn < U:
                    pe.wait_ge(prob_done, w + 1)
                    for half in range(2):
                        if not (first and nn < 1):
                            pe.wait_ge(pt_done[half], w)
                        for m in range(4):
                            c = (4 * half + m) * P
                            mm = nc.tensor.transpose(g.ps[:, 4 + half, m * P:(m + 1) * P], prob[:, nn % PR, c:c + P],
                                                     g.ident[:, :])
                        mm.then_inc(turned[half], 1)
                if nn % QB == LAG and not (first and nn < QB):
                    hs = (nn // QB - 1) % HP
                    heads = HP * i + nn // QB
                    for half in range(2):
                        pe.wait_ge(pt_done[half], w - LAG)
                    pe.wait_ge(v_loaded[hs], 16 * (i + (nn // QB + 1) // HP))
                    if not (first and nn // QB - 1 < HP):
                        pe.wait_ge(ot_done, heads - HP)
                    for m in range(NKT):
                        mm = nc.tensor.matmul(g.ps[:, 6 + hs, :], v[:, hs, m, :], pt[:, hs, m, :], start=(m == 0),
                                              stop=(m == NKT - 1))
                    mm.then_inc(pv_done, 1)

            over_pairs(pe, step)
            for n in range(U, U + SKEW + LAG + 1):
                step(NI - 1, n, tail=True)

        @block.vector
        def _(dve):
            def put_k(j, s, b, loads):
                dve.wait_ge(kq_loaded[s], 32 * loads)
                for m, (lo, hi) in enumerate(SPANS):
                    ins = nc.vector.scalar_tensor_tensor(k[:, s, lo:hi], k[:, s, lo:hi], k_scale[:, m, bass.ds(j, 1)],
                                                         rk[:, b * CTX + lo:b * CTX + hi], ALU.mult, ALU.mult)
                ins.then_inc(k_done, 1)

            def step(i, n, b=0, nb=0, first=False, tail=False):
                u = U * i + n
                s, qb = divmod(n % U, QB)
                if not tail:
                    dve.wait_ge(scores, u + 1)
                    for m, (lo, hi) in enumerate(SPANS):
                        ins = nc.vector.tensor_reduce(nmax[:, n % PR, m:m + 1], s_ps(n)[:, lo:hi], X_AXIS, ALU.max,
                                                      negate=True)
                    ins.then_inc(max_done, 1)
                if not (first and n < 1) and n <= U:
                    dve.wait_ge(exp_done, u)
                    nc.vector.reciprocal(rinv[:, (n - 1) % PR, :], rsum[:, (n - 1) % PR, :]).then_inc(rinv_done, 1)
                nn = n - SKEW
                if not (first and nn < 0) and nn < U:
                    w = u - SKEW
                    hs, wq = divmod(nn % U, QB)
                    dve.wait_ge(turned[0], w + 1)
                    if wq == 0 and not (first and nn // QB < HP):
                        dve.wait_ge(pv_done, HP * i + nn // QB - 1)
                    nc.vector.tensor_copy(pt[:, hs, 0:4, wq * P:(wq + 1) * P],
                                          g.ps[:, 4, :].rearrange("p (m q) -> p m q", m=4)).then_inc(pt_done[0], 1)
                if not tail and qb == 2:
                    if s == 0 and not first:
                        put_k(HP * i + 1, 1, b, i + 1)
                    if s == 1 and nb is not None:
                        put_k(HP * i + 2, 0, nb, i + 2)

            put_k(0, 0, 0, 1)
            put_k(1, 1, 0, 1)
            over_pairs(dve, step)
            for n in range(U, U + SKEW):
                step(NI - 1, n, tail=True)

        @block.scalar
        def _(act):
            def store(j, s):
                act.wait_ge(pv_done, j + 1)
                nc.scalar.activation(ot[:, j, :], g.ps[:, 6 + s, :], ACT.Copy).then_inc(ot_done, 1)

            def step(i, n, b=0, nb=0, first=False, tail=False):
                u = U * i + n
                if not tail:
                    act.wait_ge(max_done, u + 1)
                    if not (first and n < PR):
                        for half in range(2):
                            act.wait_ge(turned[half], u - PR + 1)
                    for m, (lo, hi) in enumerate(SPANS):
                        ins = nc.scalar.activation(prob[:, n % PR, lo:hi], s_ps(n)[:, lo:hi], ACT.Exp,
                                                   bias=nmax[:, n % PR, m:m + 1], accum_out=rsum[:, n % PR, m:m + 1])
                    ins.then_inc(exp_done, 1)
                nn = n - SKEW
                if not (first and nn < 0) and nn < U:
                    w = u - SKEW
                    hs, wq = divmod(nn % U, QB)
                    act.wait_ge(turned[1], w + 1)
                    if wq == 0 and not (first and nn // QB < HP):
                        act.wait_ge(pv_done, HP * i + nn // QB - 1)
                    nc.scalar.activation(pt[:, hs, 4:8, wq * P:(wq + 1) * P],
                                         g.ps[:, 5, :].rearrange("p (m q) -> p m q", m=4), ACT.Copy).then_inc(pt_done[1], 1)
                heads, rest = divmod(n - SKEW - LAG - 1, QB)
                if not tail and rest == 0 and not (first and heads < 1):
                    store(HP * i + heads - 1, (heads - 1) % HP)

            over_pairs(act, step)
            for n in range(U, U + SKEW):
                step(NI - 1, n, tail=True)
            for j in range(B * H - HP + (U - 1 - SKEW - LAG - 1) // QB, B * H):
                store(j, j % HP)

        @block.gpsimd
        def _(pool):
            def put_q(j, s, b, loads):
                pool.wait_ge(kq_loaded[s], 32 * loads)
                nc.gpsimd.tensor_tensor(q[:, s, :], q[:, s, :], rq[:, b * S:(b + 1) * S], ALU.mult).then_inc(q_done, 1)

            def step(i, n, b=0, nb=0, first=False):
                u = U * i + n
                s, qb = divmod(n, QB)
                pool.wait_ge(rinv_done, u + 1)
                for m, (lo, hi) in enumerate(SPANS):
                    ins = nc.gpsimd.tensor_tensor(prob[:, n % PR, lo:hi], prob[:, n % PR, lo:hi],
                                                  rinv[:, n % PR, m:m + 1].to_broadcast([P, hi - lo]), ALU.mult)
                ins.then_inc(prob_done, 1)
                if qb == 2:
                    if s == 0 and not first:
                        put_q(HP * i + 1, 1, b, i + 1)
                    if s == 1 and nb is not None:
                        put_q(HP * i + 2, 0, nb, i + 2)

            put_q(0, 0, 0, 1)
            put_q(1, 1, 0, 1)
            over_pairs(pool, step)


def store_residual(nc, g, out):
    with Stage(nc, "store") as st:
        stored = st.sem("stored")
        with nc.Block() as block:
            @block.sync
            def _(sp):
                sp.dma_start(out.rearrange("(t p) d -> p t d", p=P), g.x[:, :, :]).then_inc(stored, 16)
                sp.wait_ge(stored, 16)


def decoder_kernel(nc, a, out, stages=6):
    with ExitStack() as stack:
        g = Shared()

        def sb(name, shape, dt=F32):
            return stack.enter_context(nc.sbuf_tensor(name, shape, dt))

        g.x = sb("residual", [P, NT, D])
        g.xt = sb("normed", [P, KC, T])
        g.ident, g.ident16, g.ones = sb("identity", [P, P]), sb("identity16", [P, P], BF16), sb("all_ones", [P, P])
        g.ln_eps, g.rms_eps = sb("ln_eps", [P, 1]), sb("rms_eps", [P, 1])
        g.ps = stack.enter_context(nc.psum_tensor("ps", [P, 8, 512], F32))
        load_constants(nc, g, a["x"], a["ident"], a["ones"])
        if 1 in stages:
            self_attention(nc, g, "sa0", a["wqkv0"], a["wo0"], (a["cos"], a["sin"], a["swap"]), a["mask"])
        if 2 in stages:
            cross_attention0(nc, g, "xa0", a["ctxt"], a["L0_xattn_wq"], a["bq0_cols"], a["wkvt0"],
                             a["bk0_cols"], a["L0_xattn_bkv"],
                             a["L0_xattn_wp"], a["L0_xattn_bp"])
        if 3 in stages:
            moe(nc, g, "moe0", a, NE0, TOP0, a["wgt0"], None, a["L0_ffn_w1"], a["L0_ffn_w2"], None, None, True)
        if 4 in stages:
            self_attention(nc, g, "sa1", a["wqkv1"], a["wo1"], None, a["mask"])
        if 5 in stages:
            cross_attention1(nc, g, "xa1", a)
        if 6 in stages:
            moe(nc, g, "moe1", a, NE1, TOP1, a["L1_ffn_router_w"], a["L1_ffn_router_b"], a["L1_ffn_rw1"],
                a["L1_ffn_rw2"], a["rb1_cols"], a["L1_ffn_rb2"], False,
                shared=True, out=out)
        if 6 not in stages:
            store_residual(nc, g, out)


def lay_out(inputs):
    a = {}
    for name in ("L0_xattn_wq", "L0_xattn_bkv", "L0_xattn_wp", "L0_xattn_bp", "L0_ffn_w1", "L0_ffn_w2",
                 "L1_xattn_q_w", "L1_xattn_k_w", "L1_xattn_v_w", "L1_xattn_v_b",
                 "L1_xattn_ki_w", "L1_xattn_vi_w", "L1_xattn_vi_b", "L1_xattn_o_w", "L1_xattn_o_b",
                 "L1_ffn_sw1", "L1_ffn_sw2",
                 "L1_ffn_sb2", "L1_ffn_rw1", "L1_ffn_rw2", "L1_ffn_rb2", "L1_ffn_router_w",
                 "L1_ffn_router_b"):
        a[name] = np.asarray(inputs[name])
    a["x"] = np.asarray(inputs["x"]).reshape(T, D)
    a["ctxt"] = np.asarray(inputs["ctx_2048"]).reshape(B * CTX, D).T
    a["wqkv0"] = np.concatenate([np.asarray(inputs[f"L0_attn_W{c}"]).T for c in "qkv"], axis=1)
    a["wo0"] = np.asarray(inputs["L0_attn_Wo"]).T
    a["wkvt0"] = np.asarray(inputs["L0_xattn_wkv"]).T
    a["wgt0"] = np.asarray(inputs["L0_ffn_wg"]).T
    a["wqkv1"] = np.asarray(inputs["L1_attn_w_project"]).T
    a["wo1"] = np.asarray(inputs["L1_attn_w_out"]).T
    def columns(v):
        return v.reshape(-1, P).T

    a["bq0_cols"] = columns(np.asarray(inputs["L0_xattn_bq"]))
    a["bk0_cols"] = columns(np.asarray(inputs["L0_xattn_bkv"])[0:D])
    for name in ("q_b", "k_b", "ki_b", "nq_s", "nkt_s", "nki_s"):
        a[name + "_cols"] = columns(np.asarray(inputs["L1_xattn_" + name]))
    rb1 = np.asarray(inputs["L1_ffn_rb1"])
    a["rb1_cols"] = np.concatenate([rb1, np.zeros((NE1, len(FCH) * P - F), rb1.dtype)], axis=1
                                   ).reshape(NE1, len(FCH), P).transpose(0, 2, 1)
    sb1 = np.asarray(inputs["L1_ffn_sb1"])
    a["sb1_cols"] = np.concatenate([sb1, np.zeros((NSH, len(FCH) * P - F), sb1.dtype)], axis=1
                                   ).reshape(NSH, len(FCH), P).transpose(0, 2, 1)
    freq = np.float32(10000.0) ** (-np.arange(0, DH, 2, dtype=np.float32) / np.float32(DH))
    angles = np.arange(S, dtype=np.float32)[:, None] * freq[None, :]
    a["cos"] = np.tile(np.repeat(np.cos(angles).T, 2, axis=0), (HPC, 1)).astype(np.float32)
    a["sin"] = np.tile(np.repeat(np.sin(angles).T, 2, axis=0), (HPC, 1)).astype(np.float32)
    even = np.arange(0, P, 2)
    swap = np.zeros((P, P), np.float32)
    swap[even + 1, even] = -1.0
    swap[even, even + 1] = 1.0
    a["swap"] = swap
    a["mask"] = np.triu(np.full((P, P), MASKED, np.float32), 1)
    a["ident"] = np.eye(P, dtype=np.float32)
    a["ones"] = np.ones((P, P), np.float32)
    a["earlier"] = np.triu(np.ones((P, P), np.float32), 1)
    a["ids"] = np.arange(T, dtype=np.float32).reshape(NT, P).T
    a["iota"] = np.arange(P, dtype=np.float32)
    return {name: np.ascontiguousarray(v) for name, v in a.items()}


def kernel(**inputs):
    import concourse.bacc as bacc
    from concourse.bass_utils import run_bass_kernel_spmd

    nc = bacc.Bacc("TRN2", target_bir_lowering=False, num_devices=1)
    arrays = lay_out(inputs)
    aps = {name: nc.dram_tensor(name, v.shape, mybir.dt.from_np(v.dtype), kind="ExternalInput").ap()
           for name, v in arrays.items()}
    out = nc.dram_tensor("out", (T, D), F32, kind="ExternalOutput").ap()
    decoder_kernel(nc, aps, out, stages=(1, 2, 3, 4, 5, 6))
    result = run_bass_kernel_spmd(nc, [arrays], core_ids=[0])
    return result.results[0]["out"].reshape(B, S, D)
```
